# Optimizing a Trainium2 kernel written in Bass

```python
import numpy as np
import jax
import jax.numpy as jnp

def _softmax(x, axis=-1):
    return jax.nn.softmax(x, axis=axis)

def _gelu(x):
    return jax.nn.gelu(x, approximate=True)

def _silu(x):
    return jax.nn.silu(x)

def _sigmoid(x):
    return jax.nn.sigmoid(x)

def _layernorm(x, axis=-1, eps=1e-05):
    m = jnp.mean(x, axis=axis, keepdims=True)
    v = jnp.var(x, axis=axis, keepdims=True)
    return (x - m) / jnp.sqrt(v + eps)

def _scatter_add(tgt, idx, src, axis=0):
    return tgt.at[idx].add(src)

def _segment_sum(src, seg, n):
    return jax.ops.segment_sum(src, seg, n)
kernel_name = 'mk_xattn_ffn_d2_seqx_r8_289006'

def setup_inputs(seed: int=0):
    np.random.seed(seed)
    _w = jnp.asarray

    def _rec_inputs():
        import jax
        import jax.numpy as jnp
        _rk = jax.random.key(seed)
        x = -0.0002928 + 1 * jax.random.normal(jax.random.fold_in(_rk, 1), (16, 64, 128), jnp.float32)
        _lenS = 64 - jax.random.randint(jax.random.fold_in(_rk, 7), (16,), 0, max(1, 64 // 4) + 1, jnp.int32)
        _lenS2 = 64 - jax.random.randint(jax.random.fold_in(_rk, 8), (16,), 0, max(1, 64 // 4) + 1, jnp.int32)
        _ctx_1024P = jax.random.normal(jax.random.fold_in(_rk, 11), (16, 16, 128), jnp.float32)
        _ctx_1024c = jax.random.dirichlet(jax.random.fold_in(_rk, 511), 0.3 * jnp.ones((16,), jnp.float32), (16, 64))
        _ctx_1024t = jnp.einsum('bsk,bkd->bsd', _ctx_1024c, _ctx_1024P)
        _ctx_1024t = _ctx_1024t * jax.lax.rsqrt(jnp.mean(jnp.square(_ctx_1024t)) + 1e-12) * 0.953939
        ctx_1024 = -1.39393e-06 + 0.999914 * (_ctx_1024t + 0.3 * jax.random.normal(jax.random.fold_in(_rk, 611), (16, 64, 128), jnp.float32))
        return (x, ctx_1024)
    x, ctx_1024 = _rec_inputs()

    def _L0_xattn_setup():
        import jax, jax.numpy as jnp
        import numpy as np
        import math
        EPS = 1e-08
        LN_EPS = 1e-05
        B, S, E, NH = (2, 256, 128, 4)
        DH = E // NH

        def _mlstm_cell(q, k, v, igate_w, igate_b, fgate_w, fgate_b, out_w):
            Bq, Sq, Eq = q.shape
            if_in = jnp.concatenate([q, k, v], axis=-1)
            ig = jnp.einsum('bsf,hf->bsh', if_in, igate_w) + igate_b
            fg = jnp.einsum('bsf,hf->bsh', if_in, fgate_w) + fgate_b
            ig = jnp.transpose(ig, (0, 2, 1))[..., None]
            fg = jnp.transpose(fg, (0, 2, 1))[..., None]
            qh = q.reshape(Bq, Sq, NH, DH).transpose(0, 2, 1, 3)
            kh = k.reshape(Bq, Sq, NH, DH).transpose(0, 2, 1, 3)
            vh = v.reshape(Bq, Sq, NH, DH).transpose(0, 2, 1, 3)
            log_fg = jax.nn.log_sigmoid(fg)
            cs = jnp.cumsum(log_fg, axis=2)
            cs_shift = jnp.concatenate([jnp.zeros_like(cs[:, :, :1]), cs[:, :, :-1]], axis=2)
            logfg_mat = cs - jnp.swapaxes(cs_shift, -2, -1)
            ltr = jnp.tril(jnp.ones((Sq, Sq), dtype=bool))
            logfg_mat = jnp.where(ltr, logfg_mat, -jnp.inf)
            log_D = logfg_mat + jnp.swapaxes(ig, -2, -1)
            max_log_D = jnp.max(log_D, axis=-1, keepdims=True)
            D = jnp.exp(log_D - max_log_D)
            qk = jnp.einsum('bhsd,bhtd->bhst', qh, kh / math.sqrt(DH))
            C = qk * D
            sum_C_abs = jnp.abs(jnp.sum(C, axis=-1, keepdims=True))
            normaliser = jnp.maximum(sum_C_abs, jnp.exp(-max_log_D))
            C_norm = C / (normaliser + EPS)
            h = jnp.einsum('bhst,bhtd->bhsd', C_norm, vh)
            mean = jnp.mean(h, axis=-1, keepdims=True)
            var = jnp.mean((h - mean) ** 2, axis=-1, keepdims=True)
            h_norm = (h - mean) / jnp.sqrt(var + LN_EPS)
            scale = (1.0 + out_w).reshape(1, NH, 1, DH)
            h_norm = h_norm * scale
            return h_norm.transpose(0, 2, 1, 3).reshape(Bq, Sq, Eq)
        key = jax.random.key(seed)
        ks = jax.random.split(key, 7)
        std_g = math.sqrt(2.0 / (5.0 * 3 * E))
        return {'q': jax.random.normal(ks[0], (B, S, E), dtype=jnp.float32), 'k': jax.random.normal(ks[1], (B, S, E), dtype=jnp.float32), 'v': jax.random.normal(ks[2], (B, S, E), dtype=jnp.float32), 'igate_w': jax.random.normal(ks[3], (NH, 3 * E), dtype=jnp.float32) * std_g, 'igate_b': jax.random.normal(ks[4], (NH,), dtype=jnp.float32) * 0.1, 'fgate_w': jax.random.normal(ks[5], (NH, 3 * E), dtype=jnp.float32) * std_g, 'fgate_b': jnp.linspace(3.4, 6.0, NH, dtype=jnp.float32), 'out_w': jnp.zeros((E,), dtype=jnp.float32)}
    _L0_xattn_all = _L0_xattn_setup()
    _L0_xattn_in = {k: v for k, v in _L0_xattn_all.items() if k in ('igate_w', 'igate_b', 'fgate_w', 'fgate_b', 'out_w')}
    del _L0_xattn_all

    def _L0_ffn_setup():
        import jax, jax.numpy as jnp
        import numpy as np
        from jax import lax
        DIM = 128
        INTER = 64
        N_EXPERTS = 16
        TOPK = 4
        ROUTE_SCALE = 2.5
        VOCAB = 4000

        def _silu_and_mul(gu):
            gate, up = jnp.split(gu, 2, axis=-1)
            return jax.nn.silu(gate) * up
        key = jax.random.key(seed)
        ks = jax.random.split(key, 8)
        x = jax.random.normal(ks[0], (2, 64, DIM), dtype=jnp.float32)
        input_ids = jax.random.randint(ks[1], (2, 64), 0, VOCAB)
        s = 0.02
        gate_w = jax.random.normal(ks[2], (N_EXPERTS, DIM), dtype=jnp.float32) * s
        gate_b = jax.random.normal(ks[3], (N_EXPERTS,), dtype=jnp.float32) * s
        w13 = jax.random.normal(ks[4], (N_EXPERTS, 2 * INTER, DIM), dtype=jnp.float32) * s
        w2 = jax.random.normal(ks[5], (N_EXPERTS, DIM, INTER), dtype=jnp.float32) * s
        w13_s = jax.random.normal(ks[6], (2 * INTER, DIM), dtype=jnp.float32) * s
        w2_s = jax.random.normal(ks[7], (DIM, INTER), dtype=jnp.float32) * s
        return {'x': x, 'input_ids': input_ids, 'gate_w': gate_w, 'gate_b': gate_b, 'w13': w13, 'w2': w2, 'w13_s': w13_s, 'w2_s': w2_s}
    _L0_ffn_all = _L0_ffn_setup()
    _L0_ffn_in = {k: v for k, v in _L0_ffn_all.items() if k in ('input_ids', 'gate_w', 'gate_b', 'w13', 'w2', 'w13_s', 'w2_s')}
    del _L0_ffn_all

    def _L1_xattn_setup():
        import jax, jax.numpy as jnp
        import numpy as np
        D_MODEL = 128
        NUM_HEADS = 16
        D_K = D_MODEL // NUM_HEADS
        SCALE = float(np.sqrt(D_K))
        key = jax.random.key(seed)
        ks = jax.random.split(key, 11)
        B, S = (2, 256)
        bound = float(np.sqrt(6.0 / (D_MODEL + D_MODEL)))

        def xavier(k):
            return jax.random.uniform(k, (D_MODEL, D_MODEL), jnp.float32, -bound, bound)
        return {'query': jax.random.normal(ks[0], (B, S, D_MODEL), jnp.float32), 'key': jax.random.normal(ks[1], (B, S, D_MODEL), jnp.float32), 'value': jax.random.normal(ks[2], (B, S, D_MODEL), jnp.float32), 'W_q': xavier(ks[3]), 'b_q': jnp.zeros((D_MODEL,), jnp.float32), 'W_k': xavier(ks[4]), 'b_k': jnp.zeros((D_MODEL,), jnp.float32), 'W_v': xavier(ks[5]), 'b_v': jnp.zeros((D_MODEL,), jnp.float32), 'W_o': xavier(ks[6]), 'b_o': jnp.zeros((D_MODEL,), jnp.float32)}
    _L1_xattn_all = _L1_xattn_setup()
    _L1_xattn_in = {k: v for k, v in _L1_xattn_all.items() if k in ('W_q', 'b_q', 'W_k', 'b_k', 'W_v', 'b_v', 'W_o', 'b_o')}
    del _L1_xattn_all

    def _L1_ffn_setup():
        import jax, jax.numpy as jnp
        import numpy as np
        B, T, D = (4, 256, 128)
        FF = 512
        E = 8
        TOP_K = 2
        key = jax.random.key(seed)
        k1, k2, k3, k4 = jax.random.split(key, 4)
        x = jax.random.normal(k1, (B, T, D), dtype=jnp.float32)
        router_w = jax.random.normal(k2, (E, D), dtype=jnp.float32) * 0.02
        w1 = jax.random.normal(k3, (E, FF, D), dtype=jnp.float32) * 0.02
        w2 = jax.random.normal(k4, (E, D, FF), dtype=jnp.float32) * 0.02
        return {'x': x, 'router_w': router_w, 'w1': w1, 'w2': w2}
    _L1_ffn_all = _L1_ffn_setup()
    _L1_ffn_in = {k: v for k, v in _L1_ffn_all.items() if k in ('router_w', 'w1', 'w2')}
    del _L1_ffn_all
    return {'x': x, 'ctx_1024': ctx_1024, 'L0_xattn_igate_w': _L0_xattn_in['igate_w'], 'L0_xattn_igate_b': _L0_xattn_in['igate_b'], 'L0_xattn_fgate_w': _L0_xattn_in['fgate_w'], 'L0_xattn_fgate_b': _L0_xattn_in['fgate_b'], 'L0_xattn_out_w': _L0_xattn_in['out_w'], 'L0_ffn_input_ids': _L0_ffn_in['input_ids'], 'L0_ffn_gate_w': _L0_ffn_in['gate_w'], 'L0_ffn_gate_b': _L0_ffn_in['gate_b'], 'L0_ffn_w13': _L0_ffn_in['w13'], 'L0_ffn_w2': _L0_ffn_in['w2'], 'L0_ffn_w13_s': _L0_ffn_in['w13_s'], 'L0_ffn_w2_s': _L0_ffn_in['w2_s'], 'L1_xattn_W_q': _L1_xattn_in['W_q'], 'L1_xattn_b_q': _L1_xattn_in['b_q'], 'L1_xattn_W_k': _L1_xattn_in['W_k'], 'L1_xattn_b_k': _L1_xattn_in['b_k'], 'L1_xattn_W_v': _L1_xattn_in['W_v'], 'L1_xattn_b_v': _L1_xattn_in['b_v'], 'L1_xattn_W_o': _L1_xattn_in['W_o'], 'L1_xattn_b_o': _L1_xattn_in['b_o'], 'L1_ffn_router_w': _L1_ffn_in['router_w'], 'L1_ffn_w1': _L1_ffn_in['w1'], 'L1_ffn_w2': _L1_ffn_in['w2']}

def reference(x, ctx_1024, L0_xattn_igate_w, L0_xattn_igate_b, L0_xattn_fgate_w, L0_xattn_fgate_b, L0_xattn_out_w, L0_ffn_input_ids, L0_ffn_gate_w, L0_ffn_gate_b, L0_ffn_w13, L0_ffn_w2, L0_ffn_w13_s, L0_ffn_w2_s, L1_xattn_W_q, L1_xattn_b_q, L1_xattn_W_k, L1_xattn_b_k, L1_xattn_W_v, L1_xattn_b_v, L1_xattn_W_o, L1_xattn_b_o, L1_ffn_router_w, L1_ffn_w1, L1_ffn_w2):
    import jax
    import jax.numpy as jnp

    def _L0_xattn_ref(q, k, v, igate_w, igate_b, fgate_w, fgate_b, out_w):
        import jax, jax.numpy as jnp
        import numpy as np
        import math
        EPS = 1e-08
        LN_EPS = 1e-05
        B, S, E, NH = (2, 256, 128, 4)
        DH = E // NH

        def _mlstm_cell(q, k, v, igate_w, igate_b, fgate_w, fgate_b, out_w):
            Bq, Sq, Eq = q.shape
            if_in = jnp.concatenate([q, k, v], axis=-1)
            ig = jnp.einsum('bsf,hf->bsh', if_in, igate_w) + igate_b
            fg = jnp.einsum('bsf,hf->bsh', if_in, fgate_w) + fgate_b
            ig = jnp.transpose(ig, (0, 2, 1))[..., None]
            fg = jnp.transpose(fg, (0, 2, 1))[..., None]
            qh = q.reshape(Bq, Sq, NH, DH).transpose(0, 2, 1, 3)
            kh = k.reshape(Bq, Sq, NH, DH).transpose(0, 2, 1, 3)
            vh = v.reshape(Bq, Sq, NH, DH).transpose(0, 2, 1, 3)
            log_fg = jax.nn.log_sigmoid(fg)
            cs = jnp.cumsum(log_fg, axis=2)
            cs_shift = jnp.concatenate([jnp.zeros_like(cs[:, :, :1]), cs[:, :, :-1]], axis=2)
            logfg_mat = cs - jnp.swapaxes(cs_shift, -2, -1)
            ltr = jnp.tril(jnp.ones((Sq, Sq), dtype=bool))
            logfg_mat = jnp.where(ltr, logfg_mat, -jnp.inf)
            log_D = logfg_mat + jnp.swapaxes(ig, -2, -1)
            max_log_D = jnp.max(log_D, axis=-1, keepdims=True)
            D = jnp.exp(log_D - max_log_D)
            qk = jnp.einsum('bhsd,bhtd->bhst', qh, kh / math.sqrt(DH))
            C = qk * D
            sum_C_abs = jnp.abs(jnp.sum(C, axis=-1, keepdims=True))
            normaliser = jnp.maximum(sum_C_abs, jnp.exp(-max_log_D))
            C_norm = C / (normaliser + EPS)
            h = jnp.einsum('bhst,bhtd->bhsd', C_norm, vh)
            mean = jnp.mean(h, axis=-1, keepdims=True)
            var = jnp.mean((h - mean) ** 2, axis=-1, keepdims=True)
            h_norm = (h - mean) / jnp.sqrt(var + LN_EPS)
            scale = (1.0 + out_w).reshape(1, NH, 1, DH)
            h_norm = h_norm * scale
            return h_norm.transpose(0, 2, 1, 3).reshape(Bq, Sq, Eq)
        return _mlstm_cell(q, k, v, igate_w, igate_b, fgate_w, fgate_b, out_w)

    def _L0_ffn_ref(x, input_ids, gate_w, gate_b, w13, w2, w13_s, w2_s):
        import jax, jax.numpy as jnp
        import numpy as np
        from jax import lax
        DIM = 128
        INTER = 64
        N_EXPERTS = 16
        TOPK = 4
        ROUTE_SCALE = 2.5
        VOCAB = 4000

        def _silu_and_mul(gu):
            gate, up = jnp.split(gu, 2, axis=-1)
            return jax.nn.silu(gate) * up
        B, S, D = x.shape
        xt = x.reshape(-1, D)
        T = xt.shape[0]
        scores = jax.nn.sigmoid(xt.astype(jnp.float32) @ gate_w.T)
        biased = scores + gate_b
        _, idx = lax.top_k(biased, TOPK)
        w = jnp.take_along_axis(scores, idx, axis=-1)
        w = w / jnp.sum(w, axis=-1, keepdims=True)
        w = w * ROUTE_SCALE
        comb = jnp.zeros((T, N_EXPERTS), jnp.float32)
        comb = comb.at[jnp.arange(T)[:, None], idx].add(w)
        comb = comb.astype(x.dtype)

        def expert_body(y, args):
            w13_e, w2_e, c_e = args
            h = _silu_and_mul(xt @ w13_e.T)
            return (y + c_e[:, None] * (h @ w2_e.T), None)
        y, _ = lax.scan(expert_body, jnp.zeros_like(xt), (w13, w2, comb.T))
        y = y + _silu_and_mul(xt @ w13_s.T) @ w2_s.T
        return y.astype(x.dtype).reshape(B, S, D)

    def _L1_xattn_ref(query, key, value, W_q, b_q, W_k, b_k, W_v, b_v, W_o, b_o):
        import jax, jax.numpy as jnp
        import numpy as np
        D_MODEL = 128
        NUM_HEADS = 16
        D_K = D_MODEL // NUM_HEADS
        SCALE = float(np.sqrt(D_K))
        B, Sq, _ = query.shape
        Sk = key.shape[1]
        Q = query @ W_q.T + b_q
        K = key @ W_k.T + b_k
        V = value @ W_v.T + b_v
        Q = Q.reshape(B, Sq, NUM_HEADS, D_K).transpose(0, 2, 1, 3)
        K = K.reshape(B, Sk, NUM_HEADS, D_K).transpose(0, 2, 1, 3)
        V = V.reshape(B, Sk, NUM_HEADS, D_K).transpose(0, 2, 1, 3)
        scores = jnp.einsum('bhqd,bhkd->bhqk', Q, K) / SCALE
        attn = jax.nn.softmax(scores, axis=-1)
        attn = jnp.nan_to_num(attn, nan=0.0)
        context = jnp.einsum('bhqk,bhkd->bhqd', attn, V)
        context = context.transpose(0, 2, 1, 3).reshape(B, Sq, D_MODEL)
        output = context @ W_o.T + b_o
        return output

    def _L1_ffn_ref(x, router_w, w1, w2):
        import jax, jax.numpy as jnp
        import numpy as np
        B, T, D = (4, 256, 128)
        FF = 512
        E = 8
        TOP_K = 2
        Bx, Tx, Dx = x.shape
        N = Bx * Tx
        xf = x.reshape(N, Dx)
        logits = xf @ router_w.T
        top_vals, top_idx = jax.lax.top_k(logits, TOP_K)
        gate = jax.nn.softmax(top_vals.astype(jnp.float32), axis=-1).astype(x.dtype)
        comb = jnp.zeros((N, E), dtype=x.dtype).at[jnp.arange(N)[:, None], top_idx].add(gate)
        out = jnp.zeros((N, Dx), dtype=x.dtype)
        for e in range(E):
            h = jax.nn.gelu(xf @ w1[e].T, approximate=False)
            out = out + comb[:, e:e + 1] * (h @ w2[e].T)
        return out.reshape(Bx, Tx, Dx)
    x = x + _L0_xattn_ref(_layernorm(x, axis=-1), ctx_1024, ctx_1024, L0_xattn_igate_w, L0_xattn_igate_b, L0_xattn_fgate_w, L0_xattn_fgate_b, L0_xattn_out_w)
    x = x + _L0_ffn_ref(_layernorm(x, axis=-1), L0_ffn_input_ids, L0_ffn_gate_w, L0_ffn_gate_b, L0_ffn_w13, L0_ffn_w2, L0_ffn_w13_s, L0_ffn_w2_s)
    x = x + _L1_xattn_ref(_layernorm(x, axis=-1), ctx_1024, ctx_1024, L1_xattn_W_q, L1_xattn_b_q, L1_xattn_W_k, L1_xattn_b_k, L1_xattn_W_v, L1_xattn_b_v, L1_xattn_W_o, L1_xattn_b_o)
    x = x + _L1_ffn_ref(_layernorm(x, axis=-1), L1_ffn_router_w, L1_ffn_w1, L1_ffn_w2)
    return x

_drawn_inputs = setup_inputs


def setup_inputs(seed=0):
    import zlib

    import numpy as np

    out = dict(_drawn_inputs(seed))
    spreads = {'L0_xattn_out_w': (0.0, 0.1),
     'L1_xattn_b_q': (0.0, 1.71),
     'L1_xattn_b_k': (0.0, 2.0),
     'L1_xattn_b_v': (0.0, 0.355),
     'L1_xattn_b_o': (0.0, 0.372)}
    factors = {'L0_xattn_igate_b': 64.0,
     'L0_xattn_fgate_w': 3.265,
     'L0_ffn_gate_w': 8.0,
     'L0_ffn_gate_b': 8.0,
     'L0_ffn_w13': 8.0,
     'L0_ffn_w2': 8.0,
     'L0_ffn_w13_s': 8.0,
     'L0_ffn_w2_s': 8.0,
     'L1_ffn_router_w': 2.993,
     'L1_ffn_w1': 2.681}
    for name, (base, spread) in spreads.items():
        noise = np.random.default_rng([zlib.crc32(name.encode()), seed]).standard_normal(out[name].shape)
        drawn = base * np.exp(spread * noise) if base else spread * noise
        out[name] = jnp.asarray(drawn.astype(out[name].dtype))
    for name, factor in factors.items():
        out[name] = (out[name] * factor).astype(out[name].dtype)
    return out
```

```python
from contextlib import ExitStack

import concourse.bass as bass
from concourse import mybir

ALU = mybir.AluOpType
ACT = mybir.ActivationFunctionType
F32 = mybir.dt.float32
F16 = mybir.dt.float16
BF16 = mybir.dt.bfloat16
AX_X = mybir.AxisListType.X

P = 128
E = 128
S = 64
NB = 16
NT = NB * S // P
G = 2
TG = NT // G
N = TG * P
NBG = NB // G
H0, D0 = 4, 32
H1, D1 = 16, 8
X0, TOP0 = 16, 4
PAIRS = X0 // 2 + 1
X1 = 8
FC = 4
XS = 256.0
HS = 16.0
LN_EPS = 1e-5
NORM_EPS = 1e-8
ROUTE_SCALE = 2.5
LOWEST = -1e30
PACK = {}
_at = 0
for _name, _w in (("ident", 128), ("wg", 108), ("gb", 1), ("headmask", 16), ("bq", 1), ("bk", 1),
                  ("out_w", 128), ("bv", 128), ("bo", 128), ("gate_b", 16), ("gate_w", 16), ("router_w", 8)):
    PACK[_name] = (_at, _at + _w)
    _at += _w
PACK_W = _at


def build_program(nc, x, ctx_t, ctx_v, pack, rows, w_first, w_second, qkvo, causal, ident_h, ident_b, sel_first, sel_second, out):
    with ExitStack() as stack:
        def sb(name, shape, dt=F32):
            return stack.enter_context(nc.sbuf_tensor(name, shape, dt))

        def sem(name):
            return stack.enter_context(nc.semaphore(name))

        ps = stack.enter_context(nc.psum_tensor("ps", [P, 8, 512], F32))

        def bank(n):
            return ps[:, n, :]

        xr = sb("xr", [P, NT, E])
        ctxT = sb("ctxT", [P, NB * S])
        pk = sb("pk", [P, PACK_W])
        rw = sb("rw", [4, 2 * N + 4 * S])
        wq = sb("wq", [P, 4, E])
        cz = sb("cz", [P, S], BF16)
        idh = sb("idh", [P, P], F16)
        idb = sb("idb", [P, P], BF16)
        sel0 = sb("sel0", [P, PAIRS, P], F16)
        sel1 = sb("sel1", [P, X1, P], F16)

        def pc(name, rows_=P):
            a, b = PACK[name]
            return pk[0:rows_, a:b]

        ident = pc("ident")
        reset_mul, reset_add = rw[:, 0:N], rw[:, N:2 * N]
        head_sel = rw[:, 2 * N:].rearrange("a (h s) -> a h s", h=4)
        wgv = pc("wg").rearrange("p (c m) -> p c m", c=3)

        def shared(name, width):
            arena = sb(name, [P, width])
            at = [0, 0]

            def take(life, shape, dt=F32):
                cols = 1
                for n in shape[1:]:
                    cols *= n
                cols = cols * (2 if dt == F16 else 4) // 4
                a = arena[0:shape[0], at[life]:at[life] + cols]
                at[life] += cols
                assert at[life] <= width, (name, at)
                if dt == F16:
                    a = a.bitcast(F16)
                if len(shape) > 2:
                    dims = " ".join(f"d{i}" for i in range(len(shape) - 1))
                    a = a.rearrange(f"p ({dims}) -> p {dims}", **{f"d{i}": n for i, n in enumerate(shape[1:])})
                return a
            return take

        kept = shared("keys_or_scores", 8 * NB * S)
        work = shared("attention_or_experts", 11328)

        stats = sb("stats", [P, NT, 6])
        mv = sb("mv", [P, NT, 2])
        ve = sb("ve", [P, NT])
        rstd = sb("rstd", [P, NT])
        minus_half = sb("minus_half", [P, 16])
        xn = sb("xn", [P, NT, E])
        xT = sb("xT", [P, NB * S])
        wgc = sb("wgc", [P, 36])
        ctxM = kept(0, [P, NB, H0, S])
        v0 = work(0, [P, NB, 2, 66])
        zrow = work(0, [4, G, N])
        lrow = work(0, [4, G, N])
        lf = zrow
        csum = work(0, [4, G, N])
        urow = work(0, [4, G, N])
        crow = urow
        nmrow = csum
        strow = work(0, [64, G, N])
        sttok = sb("sttok", [P, G, TG, 64])
        decay = kept(0, [P, G, TG * H0 * S])
        cmat = kept(0, [P, G, TG * H0 * S])
        cT = work(0, [P, G, TG * 2 * P])
        den = sb("den", [P, G, TG * H0])
        rden = sb("rden", [P, G, TG * H0])
        hh = work(0, [P, G, TG * H0, D0])
        hsq = work(0, [P, G, TG * H0, D0])
        hsum = sb("hsum", [P, G, TG * H0])
        hve = sb("hve", [P, G, TG * H0])
        hrs = sb("hrs", [P, G, TG * H0])
        owp = sb("owp", [P, E])
        kT = sb("kT", [P, NB * S])
        kMa = sb("kMa", [P, 8, NB * S])
        kMb = kept(1, [P, 8, NB * S])
        kM = (kMa, kMb)
        v1 = sb("v1", [P, NB, 8, 18])
        bqs = sb("bqs", [P, 1])
        qT = sb("qT", [P, NB * S])
        rmax = sb("rmax", [P, 2, H1])
        prob = work(1, [P, 2, H1 * S])
        pT = work(1, [P, 8, P])
        rs1 = sb("rs1", [P, H1])
        rs1b = sb("rs1b", [P, H1])
        o1 = sb("o1", [P, H1, D1])
        o1n = sb("o1n", [P, H1, D1])
        o1c = sb("o1c", [P, E])
        oT = sb("oT", [P, P])
        xhi = sb("xhi", [P, NB * S], F16)
        xlo = sb("xlo", [P, NB * S], F16)
        rt = sb("rt", [P, G, 6, TG, X0])
        top = sb("top", [P, G, TG, 8])
        rsum = sb("rsum", [P, G, TG])
        rrec = sb("rrec", [P, G, TG])
        combt = sb("combt", [P, G, TG, P], F16)
        combT = sb("combT", [P, G, N], F16)
        raw = sb("raw", [P, 2, 2 * N])
        raws = sb("raws", [P, 2 * N])
        wsp = sb("wsp", [P, 2, 2, 2 * N], F16)
        act = work(1, [P, 2, N])
        cb = work(1, [P, 2, N])
        gu = work(1, [P, 2, N])
        h32 = work(1, [P, 2, N])
        hhi = work(1, [P, 2, N], F16)
        hlo = work(1, [P, 2, N], F16)
        yT = work(1, [P, G, N])
        ytmp = work(1, [P, 2, N])

        names = """in_pack in_ctx in_rows in_v in_cz in_qkvo in_idh in_sel out_done
            ones_set var_ready rstd_ready xn_ready xnT_ready xT_ready
            wgc_ready ctxm_zero ctxm_ready kproj kT_ready kM_ready vproj v1_zero v1_bias bqs_ready
            rdiff gates z_ready az_ready ez_ready ln_ready c_ready cm_ready en_ready st_zero
            cbc stT sttok_ready dpre dexp s0 cmat_ready cTp cT_ready o0 h_var h_rstd
            fill_chain stat_chain row_chain head_chain route_chain
            logits lexp comb_zero comb_ready combTp combT_ready xhi_ready xlo_ready
            raws_ready wsp_hi wsp_ready
            mm1 silu cbx tmul hmul hhi_r hlo_r mm2 yT_ready yTp
            qproj qT_ready s1 smax ssub sexp pTp pT_ready av o1_chain o1_ready oTp oT_ready oproj x_att
            raws1_ready wsp1_hi wsp1_ready mm1b gelu cbx1 hhi1 hlo1 mm2b ymul yacc acc_zero
            yTp1 x_out""".split()
        s = {n: sem(n) for n in names}

        def reached(count):
            return max(count, 0) if type(count) is int else count

        def chain(eng, own):
            count = [0]

            def link(ins):
                count[0] += 1
                ins.then_inc(own, 1)
                eng.wait_ge(own, count[0])
            return link

        in_x = [sem(f"in_x{g}") for g in range(G)]
        raw_ready = [sem(f"raw_ready{p}") for p in range(2)]
        raw1_ready = [sem(f"raw1_ready{p}") for p in range(2)]

        block = stack.enter_context(nc.Block())
        x_v = x.rearrange("(t p) e -> p t e", p=P)
        out_v = out.rearrange("(t p) e -> p t e", p=P)

        def tok(g):
            return slice(g * N, (g + 1) * N)

        def gt(g):
            return slice(g * TG, (g + 1) * TG)

        @block.sync
        def _(sp):
            sp.dma_start(xr[:, gt(0), :], x_v[:, gt(0), :]).then_inc(in_x[0], 16)
            sp.dma_start(pk[:], pack).then_inc(s["in_pack"], 16)
            sp.dma_start(ctxT[:], ctx_t).then_inc(s["in_ctx"], 16)
            sp.dma_start(wq[:], qkvo).then_inc(s["in_qkvo"], 16)
            sp.dma_start(v0[:], ctx_v).then_inc(s["in_v"], 16)
            sp.dma_start(sel0[:], sel_first).then_inc(s["in_sel"], 16)
            sp.dma_start(sel1[:], sel_second).then_inc(s["in_sel"], 16)
            for j in range(2):
                sp.dma_start(raw[:, j, 0:3 * P], w_first[j, :, :]).then_inc(raw_ready[j], 16)
            with sp.Fori(1, PAIRS // 2) as i:
                for p in range(2):
                    sp.wait_ge(s["wsp_ready"], i * 4 + 2 * (p - 1))
                    sp.dma_start(raw[:, p, 0:3 * P], w_first[bass.ds(i * 2 + p, 1), :, :]).then_inc(raw_ready[p], 16)
            sp.wait_ge(s["wsp_ready"], 2 * (PAIRS - 2))
            sp.dma_start(raw[:, 0, 0:3 * P], w_first[PAIRS - 1, :, :]).then_inc(raw_ready[0], 16)
            sp.wait_ge(s["wsp_ready"], 2 * PAIRS)
            for e in range(2):
                sp.dma_start(raw[:, e, :], w_second[e, :, :]).then_inc(raw1_ready[e], 16)
            with sp.Fori(1, X1 // 2) as i:
                for p in range(2):
                    sp.wait_ge(s["wsp1_ready"], reached(i * 2 + (p - 1)))
                    sp.dma_start(raw[:, p, :], w_second[bass.ds(i * 2 + p, 1), :, :]).then_inc(raw1_ready[p], 16)
            for g in range(G):
                sp.wait_ge(s["x_out"], g + 1)
                sp.dma_start(out_v[:, gt(g), :], xr[:, gt(g), :]).then_inc(s["out_done"], 16)
            sp.wait_ge(s["out_done"], 16 * G)

        @block.gpsimd
        def _(pool):
            fill = chain(pool, s["fill_chain"])
            pool.memset(minus_half[:], -0.5)
            pool.memset(strow[:], 0.0).then_inc(s["st_zero"], 1)
            fill(pool.memset(combt[:], 0.0))
            pool.memset(combt[:, :, :, X0:X0 + 1], XS).then_inc(s["comb_zero"], 1)
            pool.memset(ctxM[:], 0.0).then_inc(s["ctxm_zero"], 1)
            fill(pool.memset(v1[:], 0.0))
            pool.memset(v1[0:S, :, :, 8:9], 1.0)
            pool.memset(v1[S:P, :, :, 17:18], 1.0).then_inc(s["v1_zero"], 1)
            pool.wait_ge(s["v1_zero"], 1)

            def rsqrt(l, g):
                pool.wait_ge(s["var_ready"], l * G + g + 1)
                pool.tensor_tensor(rstd[:, gt(g)], ve[:, gt(g)], minus_half[:, 0:TG], ALU.pow).then_inc(s["rstd_ready"], 1)

            def key_mask(h):
                pool.tensor_scalar(kM[h // 8][:, h % 8, :], kT[:], pc("headmask")[:, h:h + 1], 1.0, ALU.mult, ALU.mult)\
                    .then_inc(s["kM_ready"], 1)

            for g in range(G):
                rsqrt(0, g)
            pool.wait_ge(s["rstd_ready"], G)
            pool.wait_ge(s["in_ctx"], 16)
            pool.wait_ge(s["ctxm_zero"], 1)
            for h in range(H0):
                q = slice(h * D0, (h + 1) * D0)
                pool.tensor_scalar(ctxM[q, :, h, :], ctxT[q, :].rearrange("p (b s) -> p b s", s=S), D0 ** -0.5, 1.0,
                                   ALU.mult, ALU.mult).then_inc(s["ctxm_ready"], 1)
                pool.wait_ge(s["ctxm_ready"], h + 1)
            pool.wait_ge(s["kT_ready"], G)
            for h in range(4):
                key_mask(h)
            for g in range(G):
                pool.wait_ge(s["h_var"], g + 1)
                pool.tensor_tensor(hrs[:, g, :], hve[:, g, :], minus_half[:, 0:TG * H0], ALU.pow).then_inc(s["h_rstd"], 1)
                key_mask(4 + g)
            for g in range(G):
                rsqrt(1, g)

            def split_pair(j, p, arrivals):
                for q in range(2):
                    c = slice(0, 2 * P) if q == 0 else slice(2 * P, 3 * P)
                    n = 2 * j + q
                    pool.wait_ge(raw_ready[p], arrivals)
                    pool.wait_ge(s["wsp_ready"], n)
                    pool.tensor_scalar(raws[:, c], raw[:, p, c], XS, 1.0, ALU.mult, ALU.mult).then_inc(s["raws_ready"], 1)
                    pool.wait_ge((s["mm1"], s["mm2"])[q], reached(2 * j - 2))
                    pool.tensor_scalar(wsp[:, p, 0, c], raw[:, p, c], XS, 1.0, ALU.mult, ALU.mult).then_inc(s["wsp_hi"], 1)
                    pool.wait_ge(s["raws_ready"], n + 1)
                    pool.wait_ge(s["wsp_hi"], n + 1)
                    pool.tensor_tensor(wsp[:, p, 1, c], raws[:, c], wsp[:, p, 0, c], ALU.subtract).then_inc(s["wsp_ready"], 1)

            split_pair(0, 0, 16)
            split_pair(1, 1, 16)
            key_mask(6)
            key_mask(7)
            pool.wait_ge(s["cTp"], G)
            for h in range(8, H1):
                key_mask(h)
            for j in range(2, PAIRS):
                split_pair(j, j % 2, 16 * (j // 2 + 1))
            for g in range(G):
                rsqrt(2, g)

            def split_expert(e, p, arrivals):
                pool.wait_ge(raw1_ready[p], arrivals)
                pool.wait_ge(s["wsp1_ready"], e)
                pool.tensor_scalar(raws[:], raw[:, p, :], XS, 1.0, ALU.mult, ALU.mult).then_inc(s["raws1_ready"], 1)
                pool.wait_ge(s["mm2b"], reached(8 * e - 8))
                pool.tensor_scalar(wsp[:, p, 0, :], raw[:, p, :], XS, 1.0, ALU.mult, ALU.mult).then_inc(s["wsp1_hi"], 1)
                pool.wait_ge(s["raws1_ready"], e + 1)
                pool.wait_ge(s["wsp1_hi"], e + 1)
                pool.tensor_tensor(wsp[:, p, 1, :], raws[:], wsp[:, p, 0, :], ALU.subtract).then_inc(s["wsp1_ready"], 1)

            pool.wait_ge(s["mm2"], 2 * PAIRS)
            split_expert(0, 0, 16)
            split_expert(1, 1, 16)
            for g in range(G):
                rsqrt(3, g)

            def accumulate(n, g):
                pool.wait_ge(s["ymul"], n + 1)
                pool.wait_ge(s["yacc"], reached(n - 1))
                pool.tensor_tensor(yT[:, g, :], yT[:, g, :], ytmp[:, g, :], ALU.add).then_inc(s["yacc"], 1)

            pool.wait_ge(s["yTp"], G)
            pool.memset(yT[:], 0.0).then_inc(s["acc_zero"], 1)
            pool.wait_ge(s["acc_zero"], 1)
            for g in range(G):
                accumulate(g, g)
            for e in range(2, X1):
                split_expert(e, e % 2, 16 * (e // 2 + 1))
                for g in range(G):
                    accumulate(2 * (e - 1) + g, g)
            for g in range(G):
                accumulate(2 * (X1 - 1) + g, g)

        @block.scalar
        def _(a):
            a.dma_start(xr[:, gt(1), :], x_v[:, gt(1), :]).then_inc(in_x[1], 16)
            a.dma_start(rw[:], rows).then_inc(s["in_rows"], 16)
            a.dma_start(cz[:], causal).then_inc(s["in_cz"], 16)
            a.dma_start(idh[:], ident_h).then_inc(s["in_idh"], 16)
            a.dma_start(idb[:], ident_b).then_inc(s["in_idh"], 16)
            for g in range(G):
                a.wait_ge(s["kproj"], g + 1)
                a.activation(kT[:, tok(g)], bank(4 + g), ACT.Identity, bias=pc("bk")).then_inc(s["kT_ready"], 1)

            def copy_xT(l, g, b):
                a.wait_ge(s["xnT_ready"], l * G + g + 1)
                a.activation(xT[:, tok(g)], bank(b), ACT.Copy).then_inc(s["xT_ready"], 1)

            for g in range(G):
                copy_xT(0, g, 4 * g)
            for g in range(G):
                a.wait_ge(s["z_ready"], g + 1)
                a.activation(lrow[:, g, :], zrow[:, g, :], ACT.Abs).then_inc(s["az_ready"], 1)
                a.wait_ge(s["az_ready"], g + 1)
                a.activation(lrow[:, g, :], lrow[:, g, :], ACT.Exp, scale=-1.0).then_inc(s["ez_ready"], 1)
                a.wait_ge(s["ez_ready"], g + 1)
                a.activation(lrow[:, g, :], lrow[:, g, :], ACT.Ln, bias=1.0).then_inc(s["ln_ready"], 1)
            for g in range(G):
                a.wait_ge(s["cm_ready"], g + 1)
                a.activation(strow[32:36, g, :], nmrow[:, g, :], ACT.Exp, scale=-1.0).then_inc(s["en_ready"], 1)
            for g in range(G):
                a.wait_ge(s["dpre"], g + 1)
                a.activation(decay[:, g, :], decay[:, g, :], ACT.Exp).then_inc(s["dexp"], 1)
            for g in range(G):
                a.wait_ge(s["cTp"], g + 1)
                a.activation(cT[:, g, :], ps[:, 4 * g + 2:4 * g + 4, :], ACT.Copy).then_inc(s["cT_ready"], 1)

            def split_x(l, k, g, b):
                copy_xT(l, g, b)
                a.activation(xhi[:, tok(g)], bank(b), ACT.Copy, scale=XS).then_inc(s["xhi_ready"], 1)

            for g in range(G):
                split_x(1, 0, g, 4 * g)
            for g in range(G):
                a.wait_ge(s["logits"], g + 1)
                a.activation(rt[:, g, 0, :, :], bank(4 * g + 1)[:, 0:TG * X0].rearrange("p (t x) -> p t x", x=X0),
                             ACT.Exp, scale=-1.0).then_inc(s["lexp"], 1)
            for g in range(G):
                a.wait_ge(s["combTp"], g + 1)
                a.activation(combT[:, g, :], bank(4 * g + 2)[:, 0:N // 2].bitcast(F16), ACT.Copy).then_inc(s["combT_ready"], 1)

            def silu_step(n, k):
                a.wait_ge(s["mm1"], n + 1)
                a.wait_ge(s["tmul"], reached(n - 1))
                a.activation(act[:, k, :], bank(k), ACT.Silu, scale=1 / (XS * XS)).then_inc(s["silu"], 1)
                a.wait_ge(s["hmul"], reached(n - 1))
                a.activation(cb[:, k, :], bank(4 + k), ACT.Copy, scale=HS / (XS * XS * XS)).then_inc(s["cbx"], 1)

            def high_step(n, k):
                a.wait_ge(s["hmul"], n + 1)
                a.wait_ge(s["mm2"], reached(n - 1))
                a.activation(hhi[:, k, :], h32[:, k, :], ACT.Copy).then_inc(s["hhi_r"], 1)

            def ffn0_step(n, k, last=False):
                if not last:
                    silu_step(n + 1, (k + 1) % 2)
                high_step(n, k)

            silu_step(0, 0)
            for n in range(4):
                ffn0_step(n, n % 2)
            with a.Fori(4, 4 * (PAIRS // 2), 4) as n:
                for k in range(4):
                    ffn0_step(n + k, k % 2)
            n0 = 2 * (PAIRS - 1)
            ffn0_step(n0, 0)
            ffn0_step(n0 + 1, 1, last=True)
            for g in range(G):
                a.wait_ge(s["mm2"], reached(2 * PAIRS - 1 + g))
                a.activation(yT[:, g, :], bank(6 + g), ACT.Copy, scale=1 / (XS * HS)).then_inc(s["yT_ready"], 1)

            for g in range(G):
                copy_xT(2, g, 7 - g)
            for g in range(G):
                a.wait_ge(s["qproj"], g + 1)
                a.wait_ge(s["bqs_ready"], 1)
                a.activation(qT[:, tok(g)], bank(5 - g), ACT.Identity, bias=bqs[:], scale=D1 ** -0.5)\
                    .then_inc(s["qT_ready"], 1)

            def copy_oT(t):
                a.wait_ge(s["oTp"], t + 1)
                a.wait_ge(s["oproj"], reached(t))
                a.activation(oT[:], bank(7)[:, 0:P], ACT.Copy).then_inc(s["oT_ready"], 1)

            for t in range(NT):
                a.wait_ge(s["ssub"], t + 1)
                a.activation(prob[:, t % 2, :], prob[:, t % 2, :], ACT.Exp).then_inc(s["sexp"], 1)
                if t:
                    copy_oT(t - 1)
                for k in range(2):
                    a.wait_ge(s["pTp"], 2 * t + k + 1)
                    a.wait_ge(s["av"], reached(t))
                    a.activation(pT[:, 4 * k:4 * k + 4, :], bank(4 + k).rearrange("p (c m) -> p c m", m=P), ACT.Copy)\
                        .then_inc(s["pT_ready"], 1)
            copy_oT(NT - 1)

            for g in range(G):
                split_x(3, 1, g, 4 * g)
            for g in range(G):
                a.wait_ge(s["rdiff"], g + 1)
                a.activation(rt[:, g, 1, :, 0:X1], rt[:, g, 0, :, 0:X1], ACT.Exp).then_inc(s["lexp"], 1)
            for g in range(G):
                a.wait_ge(s["combTp"], G + g + 1)
                a.activation(combT[:, g, :], bank(4 * g + 2)[:, 0:N // 2].bitcast(F16), ACT.Copy).then_inc(s["combT_ready"], 1)

            def gelu_step(n, q, k):
                a.wait_ge(s["mm1b"], n + 1)
                a.wait_ge(s["hlo1"], reached(n - 1))
                a.activation(h32[:, k % 2, :], bank(k % 4), ACT.Gelu, scale=1 / (XS * XS)).then_inc(s["gelu"], 1)
                if k % FC == 0:
                    g = k // FC % 2
                    a.wait_ge(s["ymul"], reached(q - 1))
                    a.activation(cb[:, g, :], bank(6 + g), ACT.Copy, scale=1 / (XS * XS * HS)).then_inc(s["cbx1"], 1)

            def high1_step(n, k):
                a.wait_ge(s["gelu"], n + 1)
                a.wait_ge(s["mm2b"], reached(n - 1))
                a.activation(hhi[:, k % 2, :], h32[:, k % 2, :], ACT.Copy, scale=HS).then_inc(s["hhi1"], 1)

            def expert_pair(base, q0, last=False):
                for k in range(16):
                    if not (last and k == 15):
                        gelu_step(base + (k + 1), q0 + (k + 1) // FC, k + 1)
                    high1_step(base + k, k)

            gelu_step(0, 0, 0)
            expert_pair(0, 0)
            with a.Fori(1, 3) as i:
                expert_pair(i * 16, i * 4)
            expert_pair(48, 12, last=True)

        @block.vector
        def _(v):
            stat = chain(v, s["stat_chain"])
            row = chain(v, s["row_chain"])
            head = chain(v, s["head_chain"])
            route = chain(v, s["route_chain"])

            def ln_stats(l, g):
                for t in range(g * TG, (g + 1) * TG):
                    last = v.bn_stats(stats[:, t, :], xr[:, t, :])
                stat(last)
                for t in range(g * TG, (g + 1) * TG):
                    last = v.bn_aggr(mv[:, t, :], stats[:, t, :])
                stat(last)
                if l:
                    v.wait_ge(s["rstd_ready"], l * G)
                v.tensor_scalar(ve[:, gt(g)], mv[:, gt(g), 1], LN_EPS, None, ALU.add).then_inc(s["var_ready"], 1)

            def ln_apply(l, g):
                v.wait_ge(s["rstd_ready"], l * G + g + 1)
                if l:
                    v.wait_ge(s["xnT_ready"], l * G)
                for t in range(g * TG, (g + 1) * TG):
                    last = v.tensor_scalar(xn[:, t, :], xr[:, t, :], mv[:, t, 0:1], rstd[:, t:t + 1],
                                           ALU.subtract, ALU.mult)
                last.then_inc(s["xn_ready"], 1)

            for g in range(G):
                v.wait_ge(in_x[g], 16)
                ln_stats(0, g)
            v.wait_ge(s["in_pack"], 16)
            v.tensor_tensor(wgc[:], wgv[:, 1, :], wgv[:, 2, :], ALU.add).then_inc(s["wgc_ready"], 1)
            v.tensor_scalar(bqs[:], pc("bq"), D1 ** -0.5, None, ALU.mult).then_inc(s["bqs_ready"], 1)
            v.tensor_scalar(owp[:], pc("out_w"), 1.0, None, ALU.add)
            for g in range(G):
                ln_apply(0, g)
            v.wait_ge(s["v1_zero"], 1)
            for c in range(4):
                v.wait_ge(s["vproj"], c + 1)
                src = bank((6, 7, 4, 5)[c]).rearrange("p (b c d) -> p b c d", b=4, d=16)
                bias = pc("bv").rearrange("p (c d) -> p c d", d=16).unsqueeze(1).to_broadcast([P, 4, 8, 16])
                for hf in range(2):
                    q = slice(hf * S, (hf + 1) * S)
                    last = v.tensor_tensor(v1[q, 4 * c:4 * c + 4, :, 9 * hf:9 * hf + 8], src[q, :, :, 8 * hf:8 * hf + 8],
                                           bias[q, :, :, 8 * hf:8 * hf + 8], ALU.add)
                last.then_inc(s["v1_bias"], 1)
            fg_bias = pk[32:36, PACK["gb"][0]:PACK["gb"][1]]
            ig_bias = pk[0:4, PACK["gb"][0]:PACK["gb"][1]]
            for g in range(G):
                v.wait_ge(s["gates"], g + 1)
                v.tensor_scalar(zrow[:, g, :], bank(4 * g + 1)[32:36, :], fg_bias, None, ALU.add).then_inc(s["z_ready"], 1)
            v.wait_ge(s["in_rows"], 16)
            v.wait_ge(s["st_zero"], 1)
            for g in range(G):
                v.wait_ge(s["ln_ready"], g + 1)
                row(v.scalar_tensor_tensor(lf[:, g, :], zrow[:, g, :], 0.0, lrow[:, g, :], ALU.min, ALU.subtract))
                row(v.tensor_tensor_scan(csum[:, g, :], reset_mul, lf[:, g, :], 0.0, ALU.mult, ALU.add))
                row(v.scalar_tensor_tensor(urow[:, g, :], bank(4 * g + 1)[0:4, :], ig_bias, lf[:, g, :],
                                                ALU.add, ALU.add))
                v.tensor_tensor(crow[:, g, :], urow[:, g, :], csum[:, g, :], ALU.subtract).then_inc(s["c_ready"], 1)
                v.wait_ge(s["c_ready"], g + 1)
                row(v.tensor_tensor_scan(strow[0:4, g, :], reset_add, crow[:, g, :], 0.0, ALU.add, ALU.max))
                v.tensor_tensor(nmrow[:, g, :], csum[:, g, :], strow[0:4, g, :], ALU.add).then_inc(s["cm_ready"], 1)
            for g in range(G):
                v.wait_ge(s["stT"], g + 1)
                v.tensor_copy(sttok[:, g, :, :], bank(4 * g)[:, 0:TG * S].rearrange("p (t c) -> p t c", c=S))\
                    .then_inc(s["sttok_ready"], 1)
            for g in range(G):
                v.wait_ge(s["cbc"], g + 1)
                v.wait_ge(s["sttok_ready"], g + 1)
                dv = decay[:, g, :].rearrange("p (t h k) -> p h t k", t=TG, h=H0)
                cv = ps[:, 4 * g + 2:4 * g + 4, :].rearrange("p b (h t k) -> p (b h) t k", t=TG, k=S)
                for h in range(H0):
                    mxv = sttok[:, g, :, h:h + 1].to_broadcast([P, TG, S])
                    last = v.tensor_tensor(dv[:, h, :, :], cv[:, h, :, :], mxv, ALU.subtract)
                last.then_inc(s["dpre"], 1)
            for g in range(G):
                v.wait_ge(s["s0"], g + 1)
                v.wait_ge(s["dexp"], g + 1)
                v.tensor_tensor(cmat[:, g, :], ps[:, 4 * g:4 * g + 2, :].rearrange("p b c -> p (b c)"), decay[:, g, :],
                                ALU.mult).then_inc(s["cmat_ready"], 1)
            for g in range(G):
                v.wait_ge(s["o0"], g + 1)
                ov = ps[:, 4 * g:4 * g + 2, 0:2 * 132].rearrange("p b (th c) -> p b th c", c=33)
                d2 = den[:, g, :].rearrange("p (b th) -> p b th", b=2)
                head(v.tensor_copy(d2.unsqueeze(3), ov[:, :, :, 32:33]))
                head(v.scalar_tensor_tensor(den[:, g, :], den[:, g, :], -1.0, den[:, g, :], ALU.mult, ALU.max))
                head(v.tensor_tensor(den[:, g, :].rearrange("p (t h) -> p t h", h=H0),
                                          den[:, g, :].rearrange("p (t h) -> p t h", h=H0),
                                          sttok[:, g, :, 32:36], ALU.max))
                head(v.tensor_scalar(den[:, g, :], den[:, g, :], NORM_EPS, None, ALU.add))
                head(v.reciprocal(rden[:, g, :], den[:, g, :]))
                head(v.tensor_tensor(hh[:, g, :, :].rearrange("p (b th) d -> p b th d", b=2), ov[:, :, :, 0:32],
                                          rden[:, g, :].rearrange("p (b th) -> p b th", b=2).unsqueeze(3)
                                          .to_broadcast([P, 2, 8, D0]), ALU.mult))
                head(v.tensor_reduce(hsum[:, g, :], hh[:, g, :, :], AX_X, ALU.add))
                head(v.tensor_scalar(hsum[:, g, :], hsum[:, g, :], 1 / D0, None, ALU.mult))
                head(v.tensor_tensor(hh[:, g, :, :], hh[:, g, :, :],
                                          hsum[:, g, :].unsqueeze(2).to_broadcast([P, TG * H0, D0]), ALU.subtract))
                head(v.tensor_tensor(hsq[:, g, :, :], hh[:, g, :, :], hh[:, g, :, :], ALU.mult))
                head(v.tensor_reduce(hsum[:, g, :], hsq[:, g, :, :], AX_X, ALU.add))
                v.tensor_scalar(hve[:, g, :], hsum[:, g, :], 1 / D0, LN_EPS, ALU.mult, ALU.add).then_inc(s["h_var"], 1)
            for g in range(G):
                v.wait_ge(s["h_rstd"], g + 1)
                head(v.tensor_tensor(hh[:, g, :, :], hh[:, g, :, :],
                                          hrs[:, g, :].unsqueeze(2).to_broadcast([P, TG * H0, D0]), ALU.mult))
                h4 = hh[:, g, :, :].rearrange("p (t h) d -> p t (h d)", h=H0)
                q4 = hsq[:, g, :, :].rearrange("p (t h) d -> p t (h d)", h=H0)
                head(v.tensor_tensor(q4, h4, owp[:].unsqueeze(1).to_broadcast([P, TG, E]), ALU.mult))
                head(v.tensor_tensor(xr[:, gt(g), :], xr[:, gt(g), :], q4, ALU.add))
                ln_stats(1, g)

            def low_x(l, k, g, b):
                v.wait_ge(s["xhi_ready"], k * G + g + 1)
                v.scalar_tensor_tensor(xlo[:, tok(g)], bank(b), XS, xhi[:, tok(g)], ALU.mult, ALU.subtract)\
                    .then_inc(s["xlo_ready"], 1)

            for g in range(G):
                ln_apply(1, g)
            for g in range(G):
                low_x(1, 0, g, 4 * g)
            v.wait_ge(s["comb_zero"], 1)
            for g in range(G):
                v.wait_ge(s["lexp"], g + 1)
                r = rt[:, g, :, :, :]
                gbias = pc("gate_b").unsqueeze(1).to_broadcast([P, TG, X0])
                route(v.tensor_scalar(r[:, 0], r[:, 0], 1.0, None, ALU.add))
                route(v.reciprocal(r[:, 1], r[:, 0]))
                route(v.tensor_tensor(r[:, 2], r[:, 1], gbias, ALU.add))
                for t in range(TG):
                    last = v.max(top[:, g, t, :], r[:, 2, t, :])
                route(last)
                route(v.memset(top[:, g, :, TOP0:], 3 * LOWEST))
                for t in range(TG):
                    last = v.match_replace(r[:, 3, t, :], top[:, g, t, :], r[:, 2, t, :], LOWEST)
                route(last)
                route(v.tensor_scalar(r[:, 4], r[:, 3], LOWEST / 2, None, ALU.is_lt))
                route(v.tensor_tensor(r[:, 4], r[:, 4], r[:, 1], ALU.mult))
                route(v.tensor_reduce(rsum[:, g, :], r[:, 4], AX_X, ALU.add))
                route(v.reciprocal(rrec[:, g, :], rsum[:, g, :]))
                route(v.tensor_scalar(rrec[:, g, :], rrec[:, g, :], ROUTE_SCALE * XS, None, ALU.mult))
                route(v.tensor_tensor(r[:, 5], r[:, 4], rrec[:, g, :].unsqueeze(2).to_broadcast([P, TG, X0]), ALU.mult))
                route(v.tensor_copy(combt[:, g, :, 0:X0], r[:, 5]))
                v.tensor_tensor(combt[:, g, :, 32:32 + X0], r[:, 5], combt[:, g, :, 0:X0], ALU.subtract)\
                    .then_inc(s["comb_ready"], 1)

            def mul_step(n, k):
                v.wait_ge(s["silu"], n + 1)
                v.tensor_tensor(gu[:, k, :], act[:, k, :], bank(2 + k), ALU.mult).then_inc(s["tmul"], 1)
                v.wait_ge(s["cbx"], n + 1)
                v.wait_ge(s["tmul"], n + 1)
                v.wait_ge(s["hhi_r"], reached(n - 1))
                v.tensor_tensor(h32[:, k, :], gu[:, k, :], cb[:, k, :], ALU.mult).then_inc(s["hmul"], 1)

            def low_step(n, k):
                v.wait_ge(s["hhi_r"], n + 1)
                v.wait_ge(s["mm2"], reached(n - 1))
                v.tensor_tensor(hlo[:, k, :], h32[:, k, :], hhi[:, k, :], ALU.subtract).then_inc(s["hlo_r"], 1)

            def ffn0_step(n, k, last=False):
                if not last:
                    mul_step(n + 1, (k + 1) % 2)
                low_step(n, k)

            mul_step(0, 0)
            for n in range(4):
                ffn0_step(n, n % 2)
            with v.Fori(4, 4 * (PAIRS // 2), 4) as n:
                for k in range(4):
                    ffn0_step(n + k, k % 2)
            n0 = 2 * (PAIRS - 1)
            ffn0_step(n0, 0)
            ffn0_step(n0 + 1, 1, last=True)

            def add_y(g, b):
                v.wait_ge(s["yTp"], g + 1)
                stat(v.tensor_tensor(xr[:, gt(g), :], xr[:, gt(g), :], bank(b).rearrange("p (t e) -> p t e", e=E), ALU.add))

            for g in range(G):
                add_y(g, g)
                ln_stats(2, g)
            for g in range(G):
                ln_apply(2, g)
                v.wait_ge(s["xn_ready"], 2 * G + g + 1)
                last = v.tensor_tensor(xr[:, gt(g), :], xr[:, gt(g), :], pc("bo").unsqueeze(1).to_broadcast([P, TG, E]), ALU.add)
                stat(last)

            def scores(t):
                k = t % 2
                v.wait_ge(s["s1"], t + 1)
                sv = ps[:, 2 * k:2 * k + 2, :].rearrange("p b (h k) -> p (b h) k", k=S)
                v.tensor_reduce(rmax[:, k, :], sv, AX_X, ALU.max).then_inc(s["smax"], 1)
                v.wait_ge(s["smax"], t + 1)
                v.wait_ge(s["pTp"], reached(2 * t - 2))
                v.tensor_tensor(prob[:, k, :].rearrange("p (h k) -> p h k", k=S), sv,
                                rmax[:, k, :].unsqueeze(2).to_broadcast([P, H1, S]), ALU.subtract).then_inc(s["ssub"], 1)

            o1ch = chain(v, s["o1_chain"])

            def normalise(t):
                v.wait_ge(s["av"], t + 1)
                ov = bank(6)[:, 0:8 * 18].rearrange("p (h c) -> p h c", c=9)
                o1ch(v.tensor_scalar(rs1[:].unsqueeze(2), ov[:, :, 8:9], 0.5, None, ALU.max))
                o1ch(v.reciprocal(rs1b[:], rs1[:]))
                o1ch(v.tensor_tensor(o1[:], ov[:, :, 0:8], rs1b[:].unsqueeze(2).to_broadcast([P, H1, D1]), ALU.mult))
                o1ch(v.tensor_scalar(o1n[:], o1[:], 0.0, None, ALU.min))
                v.wait_ge(s["oTp"], reached(t))
                v.scalar_tensor_tensor(o1c[:], o1[:].rearrange("p h d -> p (h d)"), 0.0,
                                       o1n[:].rearrange("p h d -> p (h d)"), ALU.max, ALU.add).then_inc(s["o1_ready"], 1)

            def add_attention(t):
                v.wait_ge(s["oproj"], t + 1)
                v.tensor_tensor(xr[:, t, :], xr[:, t, :], bank(7)[:, P:2 * P], ALU.add).then_inc(s["x_att"], 1)

            scores(0)
            for t in range(NT):
                if t + 1 < NT:
                    scores(t + 1)
                if t:
                    add_attention(t - 1)
                normalise(t)
            add_attention(NT - 1)
            v.wait_ge(s["x_att"], NT)

            for g in range(G):
                ln_stats(3, g)
            for g in range(G):
                ln_apply(3, g)
            for g in range(G):
                low_x(3, 1, g, 4 * g)
            for g in range(G):
                v.wait_ge(s["logits"], G + g + 1)
                v.wait_ge(s["combTp"], G)
                r = rt[:, g, :, :, 0:X1]
                lv = bank(4 * g + 1)[:, 0:TG * X0].rearrange("p (t x) -> p t x", x=X0)[:, :, 0:X1]
                route(v.tensor_copy(r[:, 2], lv))
                for t in range(TG):
                    last = v.max(top[:, g, t, :], r[:, 2, t, :])
                route(last)
                v.tensor_tensor(r[:, 0], r[:, 2], top[:, g, :, 0:1].to_broadcast([P, TG, X1]), ALU.subtract)\
                    .then_inc(s["rdiff"], 1)
                route(v.memset(top[:, g, :, 2:], 3 * LOWEST))
                for t in range(TG):
                    last = v.match_replace(r[:, 3, t, :], top[:, g, t, :], r[:, 2, t, :], LOWEST)
                route(last)
                route(v.tensor_scalar(r[:, 4], r[:, 3], LOWEST / 2, None, ALU.is_lt))
                v.wait_ge(s["lexp"], G + g + 1)
                route(v.tensor_tensor(r[:, 4], r[:, 4], r[:, 1], ALU.mult))
                route(v.tensor_reduce(rsum[:, g, :], r[:, 4], AX_X, ALU.add))
                route(v.reciprocal(rrec[:, g, :], rsum[:, g, :]))
                route(v.tensor_scalar(rrec[:, g, :], rrec[:, g, :], XS, None, ALU.mult))
                route(v.tensor_tensor(r[:, 5], r[:, 4], rrec[:, g, :].unsqueeze(2).to_broadcast([P, TG, X1]), ALU.mult))
                route(v.tensor_copy(combt[:, g, :, 0:X1], r[:, 5]))
                v.tensor_tensor(combt[:, g, :, 32:32 + X1], r[:, 5], combt[:, g, :, 0:X1], ALU.subtract)\
                    .then_inc(s["comb_ready"], 1)

            def low1_step(n, k):
                v.wait_ge(s["hhi1"], n + 1)
                v.wait_ge(s["mm2b"], reached(n - 1))
                v.scalar_tensor_tensor(hlo[:, k % 2, :], h32[:, k % 2, :], HS, hhi[:, k % 2, :], ALU.mult, ALU.subtract)\
                    .then_inc(s["hlo1"], 1)

            def gated(n, q, g):
                v.wait_ge(s["mm2b"], n + 1)
                v.wait_ge(s["cbx1"], q + 1)
                v.wait_ge(s["yacc"], reached(q - 1))
                v.tensor_tensor(ytmp[:, g, :], bank(4 + g), cb[:, g, :], ALU.mult).then_inc(s["ymul"], 1)

            def ffn1_expert_pair(base, q0, first=False):
                for k in range(16):
                    low1_step(base + k, k)
                    if k % FC == 1 and not (first and k == 1):
                        q = k // FC - 1
                        gated(base + (FC * q + 3), q0 + q, q % 2)

            ffn1_expert_pair(0, 0, first=True)
            with v.Fori(1, 3) as i:
                ffn1_expert_pair(i * 16, i * 4)
            ffn1_expert_pair(48, 12)
            gated(63, 15, 1)
            for g in range(G):
                v.wait_ge(s["yTp1"], g + 1)
                v.tensor_tensor(xr[:, gt(g), :], xr[:, gt(g), :], bank(g).rearrange("p (t e) -> p t e", e=E), ALU.add)\
                    .then_inc(s["x_out"], 1)

        @block.tensor
        def _(pe):
            mm = pe.matmul

            pe.wait_ge(s["in_ctx"], 16)
            pe.wait_ge(s["in_qkvo"], 16)
            for g in range(G):
                mm(bank(4 + g), wq[:, 1, :], ctxT[:, tok(g)], start=True, stop=True).then_inc(s["kproj"], 1)

            def v_products(c):
                for b in range(4 * c, 4 * c + 4):
                    for hf in range(2):
                        last = mm(ps[hf * S:(hf + 1) * S, (6, 7, 4, 5)[c], (b % 4) * E:(b % 4 + 1) * E],
                                  ctxT[:, b * S:(b + 1) * S], wq[:, 2, :], start=True, stop=True)
                last.then_inc(s["vproj"], 1)

            v_products(0)
            v_products(1)
            pe.wait_ge(s["in_pack"], 16)

            def transpose_norm(l, g, b):
                pe.wait_ge(s["xn_ready"], l * G + g + 1)
                for t in range(TG):
                    last = pe.transpose(bank(b)[:, t * P:(t + 1) * P], xn[:, g * TG + t, :], ident)
                last.then_inc(s["xnT_ready"], 1)

            def gates(g):
                pe.wait_ge(s["wgc_ready"], 1)
                mm(bank(4 * g + 1)[0:36, :], wgc[:], ctxT[:, tok(g)], start=True, stop=False)
                pe.wait_ge(s["xT_ready"], g + 1)
                mm(bank(4 * g + 1)[0:36, :], wgv[:, 0, :], xT[:, tok(g)], start=False, stop=True).then_inc(s["gates"], 1)

            transpose_norm(0, 0, 0)
            gates(0)
            pe.wait_ge(s["kT_ready"], G)
            v_products(2)
            v_products(3)
            pe.wait_ge(s["v1_bias"], 4)
            transpose_norm(0, 1, 4)
            gates(1)
            pe.wait_ge(s["in_rows"], 16)
            pe.wait_ge(s["in_cz"], 16)
            pe.wait_ge(s["in_idh"], 32)
            for g in range(G):
                pe.wait_ge(s["c_ready"], g + 1)
                cv = crow[:, g, :].rearrange("a (t b k) -> a t b k", b=2, k=S)
                for pair in range(2):
                    for hf in range(2):
                        for h in range(2 * pair, 2 * pair + 2):
                            mm(ps[hf * S:(hf + 1) * S, 4 * g + 2 + pair, (h % 2) * TG * S:(h % 2 + 1) * TG * S],
                               head_sel[:, h, :], cv[:, :, hf, :], start=(h % 2 == 0), stop=False, skip_group_check=True)
                    last = mm(bank(4 * g + 2 + pair), idb[:], cz[:].unsqueeze(1).to_broadcast([P, 8, S]),
                              start=False, stop=True, skip_group_check=True)
                last.then_inc(s["cbc"], 1)
            for g in range(G):
                pe.wait_ge(s["en_ready"], g + 1)
                pe.wait_ge(s["xT_ready"], g + 1)
                for t in range(TG):
                    last = pe.transpose(bank(4 * g)[:, t * S:(t + 1) * S], strow[:, g, t * P:(t + 1) * P], ident[0:S, 0:S])
                last.then_inc(s["stT"], 1)
            pe.wait_ge(s["ctxm_ready"], H0)
            for g in range(G):
                pe.wait_ge(s["sttok_ready"], g + 1)
                for t in range(TG):
                    for hf in range(2):
                        b = 2 * (g * TG + t) + hf
                        last = mm(ps[hf * S:(hf + 1) * S, 4 * g + t // 2, (t % 2) * H0 * S:(t % 2 + 1) * H0 * S],
                                  xT[:, b * S:(b + 1) * S], ctxM[:, b, :, :].rearrange("p h k -> p (h k)"),
                                  start=True, stop=True)
                last.then_inc(s["s0"], 1)
            for g in range(G):
                pe.wait_ge(s["cmat_ready"], g + 1)
                for c in range(2 * TG):
                    last = pe.transpose(bank(4 * g + 2 + c // 4)[:, (c % 4) * P:(c % 4 + 1) * P],
                                        cmat[:, g, c * P:(c + 1) * P], ident)
                last.then_inc(s["cTp"], 1)
            pe.wait_ge(s["in_v"], 16)
            for g in range(G):
                pe.wait_ge(s["cT_ready"], g + 1)
                for t in range(TG):
                    for pair in range(2):
                        for hf in range(2):
                            b = 2 * (g * TG + t) + hf
                            c = (2 * t + pair) * P + hf * S
                            o = (t % 2) * 132 + pair * 66
                            last = mm(ps[hf * S:(hf + 1) * S, 4 * g + t // 2, o:o + 66], cT[:, g, c:c + S],
                                      v0[:, b, pair, :], start=True, stop=True)
                last.then_inc(s["o0"], 1)

            def router(l, k, g, width, name):
                pe.wait_ge(s["xT_ready"], l * G + g + 1)
                for t in range(TG):
                    c = g * N + t * P
                    last = mm(bank(4 * g + 1)[:, t * X0:t * X0 + width], xT[:, c:c + P], pc(name), start=True, stop=True)
                last.then_inc(s["logits"], 1)

            def transpose_gates(k, g):
                pe.wait_ge(s["comb_ready"], k * G + g + 1)
                for t in range(TG):
                    last = pe.transpose(bank(4 * g + 2)[:, t * S:(t + 1) * S].bitcast(F16), combt[:, g, t, :], idh[:])
                last.then_inc(s["combTp"], 1)

            for g in range(G):
                transpose_norm(1, g, 4 * g)
            for g in range(G):
                router(1, 0, g, X0, "gate_w")
            for g in range(G):
                transpose_gates(0, g)

            def up0(n, j, k, p):
                g = k
                pe.wait_ge(s["wsp_ready"], j * 2 + 1)
                pe.wait_ge(s["silu"], reached(n - 1))
                pe.wait_ge(s["tmul"], reached(n - 1))
                pe.wait_ge(s["cbx"], reached(n - 1))
                for i in range(2):
                    c = slice(i * P, (i + 1) * P)
                    mm(bank(2 * i + k), wsp[:, p, 0, c], xhi[:, tok(g)], start=True, stop=False)
                    mm(bank(2 * i + k), wsp[:, p, 0, c], xlo[:, tok(g)], start=False, stop=False)
                    mm(bank(2 * i + k), wsp[:, p, 1, c], xhi[:, tok(g)], start=False, stop=True)
                pick = sel0[:, j, :] if type(j) is int else sel0[:, bass.ds(j, 1), :].rearrange("p a m -> p (a m)")
                mm(bank(4 + k), pick, combT[:, g, :], start=True, stop=True).then_inc(s["mm1"], 1)

            def down0(n, j, k, p, first, last):
                c = slice(2 * P, 3 * P)
                pe.wait_ge(s["wsp_ready"], j * 2 + 2)
                pe.wait_ge(s["hlo_r"], n + 1)
                mm(bank(6 + k), wsp[:, p, 0, c], hhi[:, k, :], start=first, stop=False)
                mm(bank(6 + k), wsp[:, p, 0, c], hlo[:, k, :], start=False, stop=False)
                mm(bank(6 + k), wsp[:, p, 1, c], hhi[:, k, :], start=False, stop=last).then_inc(s["mm2"], 1)

            pe.wait_ge(s["combT_ready"], G)
            pe.wait_ge(s["xlo_ready"], G)
            pe.wait_ge(s["xhi_ready"], G)
            pe.wait_ge(s["in_sel"], 32)
            up0(0, 0, 0, 0)
            up0(1, 0, 1, 0)

            def two_pairs(j, first=False):
                for k in range(4):
                    up0(2 * j + (k + 2), j + (k // 2 + 1), k % 2, (k // 2 + 1) % 2)
                    down0(2 * j + k, j + k // 2, k % 2, k // 2, first and k < 2, False)

            two_pairs(0, first=True)
            with pe.Fori(1, PAIRS // 2) as i:
                two_pairs(i * 2)
            n0 = 2 * (PAIRS - 1)
            for g in range(G):
                down0(n0 + g, PAIRS - 1, g, 0, False, True)

            def transpose_y(g, b, done):
                for t in range(TG):
                    last = pe.transpose(bank(b)[:, t * P:(t + 1) * P], yT[:, g, t * P:(t + 1) * P], ident)
                last.then_inc(done, 1)

            for g in range(G):
                pe.wait_ge(s["yT_ready"], g + 1)
                transpose_y(g, g, s["yTp"])

            for g in range(G):
                pe.wait_ge(s["yT_ready"], G)
                transpose_norm(2, g, 7 - g)
            for g in range(G):
                pe.wait_ge(s["xT_ready"], 2 * G + g + 1)
                mm(bank(5 - g), wq[:, 0, :], xT[:, tok(g)], start=True, stop=True).then_inc(s["qproj"], 1)

            pe.wait_ge(s["kM_ready"], H1)
            km = [m[:].rearrange("p h (b k) -> p b h k", k=S) for m in kM]

            def scores1(t):
                pe.wait_ge(s["qT_ready"], G if t else 1)
                pe.wait_ge(s["ssub"], reached(t - 1))
                for half in range(2):
                    for hf in range(2):
                        b = 2 * t + hf
                        last = mm(ps[hf * S:(hf + 1) * S, 2 * (t % 2) + half, :], qT[:, b * S:(b + 1) * S],
                                  km[half][:, b, :, :], start=True, stop=True)
                last.then_inc(s["s1"], 1)

            def transpose_probs(t):
                pe.wait_ge(s["sexp"], t + 1)
                pe.wait_ge(s["qT_ready"], G)
                for k in range(2):
                    pe.wait_ge(s["pT_ready"], reached(2 * t - 1 + k))
                    for c in range(4):
                        last = pe.transpose(bank(4 + k)[:, c * P:(c + 1) * P],
                                            prob[:, t % 2, (4 * k + c) * P:(4 * k + c + 1) * P], ident)
                    last.then_inc(s["pTp"], 1)

            def weighted_values(t):
                pe.wait_ge(s["pT_ready"], 2 * t + 2)
                pe.wait_ge(s["o1_ready"], reached(t))
                for c in range(8):
                    for hf in range(2):
                        last = mm(ps[hf * S:(hf + 1) * S, 6, c * 18:(c + 1) * 18], pT[:, c, hf * S:(hf + 1) * S],
                                  v1[:, 2 * t + hf, c, :], start=True, stop=True)
                last.then_inc(s["av"], 1)

            def output_product(t):
                pe.wait_ge(s["o1_ready"], t + 1)
                pe.wait_ge(s["x_att"], reached(t))
                pe.transpose(bank(7)[:, 0:P], o1c[:], ident).then_inc(s["oTp"], 1)
                pe.wait_ge(s["oT_ready"], t + 1)
                mm(bank(7)[:, P:2 * P], oT[:], wq[:, 3, :], start=True, stop=True).then_inc(s["oproj"], 1)

            scores1(0)
            for t in range(NT):
                if t + 1 < NT:
                    scores1(t + 1)
                if t:
                    output_product(t - 1)
                transpose_probs(t)
                weighted_values(t)
            output_product(NT - 1)

            pe.wait_ge(s["x_att"], NT)
            for g in range(G):
                transpose_norm(3, g, 4 * g)
            for g in range(G):
                router(3, 1, g, X1, "router_w")
            for g in range(G):
                transpose_gates(1, g)
            pe.wait_ge(s["combT_ready"], 2 * G)
            pe.wait_ge(s["xlo_ready"], 2 * G)
            pe.wait_ge(s["xhi_ready"], 2 * G)

            def up1(n, e, q, k):
                p, g, c = k // 8 % 2, k // 4 % 2, k % FC
                pe.wait_ge(s["wsp1_ready"], e + 1)
                pe.wait_ge(s["gelu"], reached(n - 3))
                cs = slice(c * P, (c + 1) * P)
                if c == 0:
                    pe.wait_ge(s["cbx1"], reached(q - 1))
                    pick = sel1[:, e, :] if type(e) is int else sel1[:, bass.ds(e, 1), :].rearrange("p a m -> p (a m)")
                    mm(bank(6 + g), pick, combT[:, g, :], start=True, stop=True)
                mm(bank(k % 4), wsp[:, p, 0, cs], xhi[:, tok(g)], start=True, stop=False)
                mm(bank(k % 4), wsp[:, p, 0, cs], xlo[:, tok(g)], start=False, stop=False)
                mm(bank(k % 4), wsp[:, p, 1, cs], xhi[:, tok(g)], start=False, stop=True).then_inc(s["mm1b"], 1)

            def down1(n, q, k):
                p, g, c = k // 8 % 2, k // 4 % 2, k % FC
                cs = slice(N + c * P, N + (c + 1) * P)
                pe.wait_ge(s["hlo1"], n + 1)
                if c == 0:
                    pe.wait_ge(s["ymul"], reached(q - 1))
                mm(bank(4 + g), wsp[:, p, 0, cs], hhi[:, k % 2, :], start=(c == 0), stop=False)
                mm(bank(4 + g), wsp[:, p, 0, cs], hlo[:, k % 2, :], start=False, stop=False)
                mm(bank(4 + g), wsp[:, p, 1, cs], hhi[:, k % 2, :], start=False, stop=(c == FC - 1)).then_inc(s["mm2b"], 1)

            def expert_pair(e, last=False):
                for k in range(16):
                    ahead = k + 2
                    if not (last and ahead >= 16):
                        up1(8 * e + ahead, e + ahead // 8, 2 * e + ahead // 4, ahead)
                    down1(8 * e + k, 2 * e + k // 4, k)

            up1(0, 0, 0, 0)
            up1(1, 0, 0, 1)
            expert_pair(0)
            with pe.Fori(1, X1 // 2 - 1) as i:
                expert_pair(i * 2)
            expert_pair(X1 - 2, last=True)
            pe.wait_ge(s["yacc"], 2 * X1)
            for g in range(G):
                transpose_y(g, g, s["yTp1"])


def kernel(**inputs):
    import numpy as np
    import ml_dtypes
    import concourse.bacc as bacc
    from concourse.bass_utils import run_bass_kernel_spmd

    f = {k: np.asarray(v) for k, v in inputs.items()}
    f32 = np.float32
    x = f["x"].reshape(NB * S, E)
    ctx = f["ctx_1024"]
    pack = np.zeros((P, PACK_W), f32)

    def put(name, value):
        a, b = PACK[name]
        pack[:value.shape[0], a:b] = value.reshape(value.shape[0], b - a)

    wg = np.zeros((P, 3, 36), f32)
    gb = np.zeros((36, 1), f32)
    for c in range(3):
        wg[:, c, 0:H0] = f["L0_xattn_igate_w"][:, c * E:(c + 1) * E].T
        wg[:, c, 32:32 + H0] = f["L0_xattn_fgate_w"][:, c * E:(c + 1) * E].T
    gb[0:H0, 0] = f["L0_xattn_igate_b"]
    gb[32:32 + H0, 0] = f["L0_xattn_fgate_b"]
    put("ident", np.eye(P, dtype=f32))
    put("wg", wg)
    put("gb", gb)
    put("headmask", (np.arange(E)[:, None] // D1 == np.arange(H1)[None, :]).astype(f32))
    put("bq", f["L1_xattn_b_q"][:, None])
    put("bk", f["L1_xattn_b_k"][:, None])
    put("out_w", np.broadcast_to(f["L0_xattn_out_w"], (P, E)))
    put("bv", np.broadcast_to(f["L1_xattn_b_v"], (P, E)))
    put("bo", np.broadcast_to(f["L1_xattn_b_o"], (P, E)))
    put("gate_b", np.broadcast_to(f["L0_ffn_gate_b"], (P, X0)))
    put("gate_w", f["L0_ffn_gate_w"].T)
    put("router_w", f["L1_ffn_router_w"].T)

    rows = np.zeros((4, 2 * N + 4 * S), f32)
    starts = (np.arange(N) % S) == 0
    rows[:, 0:N] = ~starts
    rows[:, N:2 * N] = np.where(starts, LOWEST, 0.0)
    for h in range(H0):
        rows[h, 2 * N + h * S:2 * N + (h + 1) * S] = 1.0

    ctx_v = np.zeros((P, NB, 2, 66), f32)
    for hf in range(2):
        for pair in range(2):
            h = 2 * pair + hf
            ctx_v[hf * S:(hf + 1) * S, :, pair, hf * 33:hf * 33 + D0] = ctx[:, :, h * D0:(h + 1) * D0].transpose(1, 0, 2)
            ctx_v[hf * S:(hf + 1) * S, :, pair, hf * 33 + D0] = 1.0

    w_first = np.zeros((PAIRS, P, 3 * P), f32)
    w13, w2 = f["L0_ffn_w13"], f["L0_ffn_w2"]
    half = w13.shape[1] // 2
    experts = [(w13[e], w2[e]) for e in range(X0)] + [(f["L0_ffn_w13_s"], f["L0_ffn_w2_s"])]
    for e, (up, down) in enumerate(experts):
        j, c = e // 2, (e % 2) * half
        w_first[j, :, c:c + half] = up[0:half].T
        w_first[j, :, P + c:P + c + half] = up[half:].T
        w_first[j, c:c + half, 2 * P:] = down.T
    w_second = np.concatenate([f["L1_ffn_w1"].transpose(0, 2, 1),
                               f["L1_ffn_w2"].transpose(0, 2, 1).reshape(X1, FC, P, E).transpose(0, 2, 1, 3).reshape(X1, P, FC * E)], axis=2)
    qkvo = np.stack([f["L1_xattn_W_q"].T, f["L1_xattn_W_k"].T, f["L1_xattn_W_v"].T, f["L1_xattn_W_o"].T], axis=1)
    causal = np.where(np.arange(S)[None, :] > (np.arange(P) % S)[:, None], LOWEST, 0.0).astype(ml_dtypes.bfloat16)
    sel_first = np.zeros((P, PAIRS, P), np.float16)
    for e in range(X0 + 1):
        for r in (e, 32 + e):
            sel_first[r, e // 2, (e % 2) * half:(e % 2 + 1) * half] = 1.0
    sel_second = np.zeros((P, X1, P), np.float16)
    for e in range(X1):
        sel_second[[e, 32 + e], e, :] = 1.0

    arrays = {
        "x": x, "ctx_t": ctx.reshape(NB * S, E).T, "ctx_v": ctx_v, "pack": pack, "rows": rows, "w_first": w_first,
        "w_second": w_second, "qkvo": qkvo, "causal": causal, "ident_h": np.eye(P, dtype=np.float16),
        "ident_b": np.eye(P, dtype=ml_dtypes.bfloat16),
        "sel_first": sel_first, "sel_second": sel_second,
    }
    arrays = {k: np.ascontiguousarray(v) for k, v in arrays.items()}
    nc = bacc.Bacc("TRN2", target_bir_lowering=False, num_devices=1)
    args = {k: nc.dram_tensor(k, v.shape, mybir.dt.from_np(v.dtype), kind="ExternalInput").ap() for k, v in arrays.items()}
    out = nc.dram_tensor("out", (NB * S, E), F32, kind="ExternalOutput").ap()
    build_program(nc, out=out, **args)
    r = run_bass_kernel_spmd(nc, [arrays], core_ids=[0])
    return r.results[0]["out"].reshape(NB, S, E)
```

```python
import math
from contextlib import ExitStack

import concourse.bass as bass
from concourse import mybir

ALU = mybir.AluOpType
ACT = mybir.ActivationFunctionType
F32 = mybir.dt.float32
F16 = mybir.dt.float16
BF16 = mybir.dt.bfloat16
AX_X = mybir.AxisListType.X

P = 128
E = 128
S = 64
NB = 16
NT = NB * S // P
G = 2
TG = NT // G
N = TG * P
NBG = NB // G
H0, D0 = 4, 32
H1, D1 = 16, 8
X0, TOP0 = 16, 4
PAIRS = X0 // 2 + 1
X1 = 8
FC = 4
XS = 256.0
HS = 16.0
AS = 64.0
VS = 64.0
PS = 1024.0
Q4 = NB * S // 4
LN_EPS = 1e-5
NORM_EPS = 1e-8
ROUTE_SCALE = 2.5
LOWEST = -1e30
PACK = {}
_at = 0
for _name, _w in (("ident", 128), ("wg", 108), ("gb", 1), ("headmask", 4), ("bq", 4), ("bk", 1),
                  ("out_w", 128), ("bv", 128), ("bo", 128), ("gate_b", 16), ("gate_w", 16), ("router_w", 8)):
    PACK[_name] = (_at, _at + _w)
    _at += _w
PACK_W = _at


def build_program(nc, x, ctx_t, ctx_v, pack, rows, w_first, w_second, qkvo, causal, ident_h, ident_b, sel_first, sel_second, out):
    with ExitStack() as stack:
        def sb(name, shape, dt=F32):
            return stack.enter_context(nc.sbuf_tensor(name, shape, dt))

        def sem(name):
            return stack.enter_context(nc.semaphore(name))

        ps = stack.enter_context(nc.psum_tensor("ps", [P, 8, 512], F32))

        def bank(n):
            return ps[:, n, :]

        xr = sb("xr", [P, NT, E])
        ctxT = sb("ctxT", [P, NB * S])
        pk = sb("pk", [P, PACK_W])
        rw = sb("rw", [4, 2 * N + 4 * S])
        wq = sb("wq", [P, 4, E])
        cz = sb("cz", [P, S], BF16)
        idh = sb("idh", [P, P], F16)
        idb = sb("idb", [P, P], BF16)
        sel0 = sb("sel0", [P, PAIRS, P], F16)
        sel1 = sb("sel1", [P, X1, P], F16)

        def pc(name, rows_=P):
            a, b = PACK[name]
            return pk[0:rows_, a:b]

        ident = pc("ident")
        reset_mul, reset_add = rw[:, 0:N], rw[:, N:2 * N]
        head_sel = rw[:, 2 * N:].rearrange("a (h s) -> a h s", h=4)
        wgv = pc("wg").rearrange("p (c m) -> p c m", c=3)

        def shared(name, width):
            arena = sb(name, [P, width])
            at = [0, 0, 0]

            def take(life, shape, dt=F32):
                cols = 1
                for n in shape[1:]:
                    cols *= n
                cols = cols * (2 if dt == F16 else 4) // 4
                a = arena[0:shape[0], at[life]:at[life] + cols]
                at[life] += cols
                assert at[life] <= width, (name, at)
                if dt == F16:
                    a = a.bitcast(F16)
                if len(shape) > 2:
                    dims = " ".join(f"d{i}" for i in range(len(shape) - 1))
                    a = a.rearrange(f"p ({dims}) -> p {dims}", **{f"d{i}": n for i, n in enumerate(shape[1:])})
                return a
            return take

        kept = shared("keys_or_scores", 8 * NB * S)
        work = shared("attention_or_experts", 11328)

        stats = sb("stats", [P, NT, 6])
        mv = sb("mv", [P, NT, 2])
        ve = sb("ve", [P, NT])
        rstd = sb("rstd", [P, NT])
        minus_half = sb("minus_half", [P, 16])
        xn = sb("xn", [P, NT, E])
        xT = sb("xT", [P, NB * S])
        wgc = sb("wgc", [P, 36])
        ctxM = kept(0, [P, NB, H0, S])
        v0 = work(0, [P, NB, 2, 66])
        zrow = work(0, [4, G, N])
        lrow = work(0, [4, G, N])
        lf = zrow
        csum = work(0, [4, G, N])
        urow = work(0, [4, G, N])
        crow = urow
        nmrow = csum
        strow = work(0, [64, G, N])
        sttok = sb("sttok", [P, G, TG, 64])
        decay = kept(0, [P, G, TG * H0 * S])
        cmat = kept(0, [P, G, TG * H0 * S])
        cT = work(0, [P, G, TG * 2 * P])
        den = sb("den", [P, G, TG * H0])
        rden = sb("rden", [P, G, TG * H0])
        vmean = sb("vmean", [P, NB * 2 * 2])
        ones_row = sb("ones_row", [1, S])
        hh = work(0, [P, G, TG * H0, D0])
        hy = sb("hy", [P, G, TG * H0])
        hq = sb("hq", [P, G, TG * H0])
        hsq = work(0, [P, G, TG * H0, D0])
        hsum = sb("hsum", [P, G, TG * H0])
        hve = sb("hve", [P, G, TG * H0])
        hrs = sb("hrs", [P, G, TG * H0])
        owp = sb("owp", [P, E])
        kT = sb("kT", [P, NB * S])
        khi = xhi = sb("xhi", [P, NB * S], F16)
        klo = xlo = sb("xlo", [P, NB * S], F16)
        kS = sb("kS", [P, 4, NB * S], F16)
        kM = sb("kM", [P, H1, NB * S], F16)
        wqr = sb("wqr", [P, 4, P])
        bks = sb("bks", [P, 1])
        v1 = sb("v1", [P, NB, 8, 18])
        bqs = sb("bqs", [P, 4])
        qS = kept(1, [P, 4, NB * S], F16)
        rmax = sb("rmax", [P, 2, H1])
        prob = work(2, [P, 2, H1 * S])
        phi = work(2, [P, 2, H1 * S], F16)
        plo = work(2, [P, 2, H1 * S], F16)
        pT = work(2, [P, 2, 2, H1 * S], F16)
        v1hi = sb("v1hi", [P, NB, 8, 18], F16)
        v1lo = sb("v1lo", [P, NB, 8, 18], F16)
        log_ps = sb("log_ps", [P, 1])
        rs1 = sb("rs1", [P, H1])
        rs1b = sb("rs1b", [P, H1])
        o1 = sb("o1", [P, H1, D1])
        o1n = sb("o1n", [P, H1, D1])
        o1c = sb("o1c", [P, 2, E])
        oT = sb("oT", [P, P])
        rt = sb("rt", [P, G, 6, TG, X0])
        top = sb("top", [P, G, TG, 8])
        rsum = sb("rsum", [P, G, TG])
        rrec = sb("rrec", [P, G, TG])
        combt = sb("combt", [P, G, TG, P], F16)
        combT = sb("combT", [P, G, N], F16)
        raw = sb("raw", [P, 2, 2 * N])
        raws = kT
        wsp = sb("wsp", [P, 2, 2, 2 * N], F16)
        act = work(1, [P, 2, N])
        cb = work(1, [P, 2, N])
        h32 = work(1, [P, 4, N])
        gu = h32[:, 2:4, :]
        hhi = work(1, [P, 4, N], F16)
        hlo = work(1, [P, 4, N], F16)
        yT = work(1, [P, G, N])
        ytmp = work(1, [P, 2, N])

        names = """in_pack in_ctx in_rows in_v in_cz in_qkvo in_idh in_sel out_done
            ones_set var_ready rstd_ready xn_ready xnT_ready xT_ready
            wgc_ready ctxm_zero ctxm_ready kproj kT_ready khi_ready klo_ready kS_ready kM_ready wqr_ready vproj v1_zero v1hi_ready v1lo_ready bqs_ready
            rdiff gates z_ready az_ready ez_ready ln_ready c_ready cm_ready en_ready st_zero
            cbc stT sttok_ready dpre dexp s0 cmat_ready cTp cT_ready o0 hsq_ready h_var h_ln h_rstd vmean_ready v0_ready ones_ready v1_copied
            fill_chain stat_chain row_chain head_chain route_chain
            logits lexp comb_zero comb_ready combTp combT_ready xhi_ready xlo_ready
            raws_ready wsp_hi wsp_ready
            mm1 silu cbx tmul hmul hhi_r hlo_r mm2 yT_ready yTp
            qproj qhi_ready qS_ready s1 smax ssub phi_ready sexp plo_ready pTp pT_ready av o1_chain o1_ready oTp oT_ready oproj x_att
            raws1_ready wsp1_hi wsp1_ready mm1b gelu cbx1 hhi1 hlo1 mm2b ymul yacc acc_zero
            yTp1 x_out""".split()
        s = {n: sem(n) for n in names}

        def reached(count):
            return max(count, 0) if type(count) is int else count

        def chain(eng, own):
            count = [0]

            def link(ins):
                count[0] += 1
                ins.then_inc(own, 1)
                eng.wait_ge(own, count[0])
            return link

        in_x = [sem(f"in_x{g}") for g in range(G)]
        raw_ready = [sem(f"raw_ready{p}") for p in range(2)]
        raw1_ready = [sem(f"raw1_ready{p}") for p in range(2)]

        block = stack.enter_context(nc.Block())
        x_v = x.rearrange("(t p) e -> p t e", p=P)
        out_v = out.rearrange("(t p) e -> p t e", p=P)

        def qbank(c, jj):
            return (4, 5, 2, 3)[2 * c + jj] if c < 2 else 7

        def head_outputs(g):
            return ps[:, 4 * g:4 * g + 2, 0:2 * 132].rearrange("p b (th c) -> p b th c", c=33)

        def logit_bank(k, g):
            return 7 if k and g else 4 * g + 1

        def gate_bank(k, g):
            return 4 * g + 2 if (k, g) == (1, 0) else 6 + g

        def place(k, first):
            if first and k < 16:
                return k // 4 % 2, k // 8 % 2, k % FC
            return k // 8 % 2, k // 4 % 2, k % FC

        def before(q, first):
            if first and q < 4:
                return q if q % 2 else 0
            return reached(q - 1)

        def tok(g):
            return slice(g * N, (g + 1) * N)

        def gt(g):
            return slice(g * TG, (g + 1) * TG)

        @block.sync
        def _(sp):
            sp.dma_start(xr[:, gt(0), :], x_v[:, gt(0), :]).then_inc(in_x[0], 16)
            sp.dma_start(pk[:], pack).then_inc(s["in_pack"], 16)
            sp.dma_start(ctxT[:], ctx_t).then_inc(s["in_ctx"], 16)
            sp.dma_start(wq[:], qkvo).then_inc(s["in_qkvo"], 16)
            sp.dma_start(v0[:], ctx_v).then_inc(s["in_v"], 16)
            sp.dma_start(sel0[:], sel_first).then_inc(s["in_sel"], 16)
            sp.dma_start(sel1[:], sel_second).then_inc(s["in_sel"], 16)
            for j in range(2):
                sp.dma_start(raw[:, j, 0:3 * P], w_first[j, :, :]).then_inc(raw_ready[j], 16)
            sp.wait_ge(s["khi_ready"], 1)
            sp.wait_ge(s["klo_ready"], 1)
            for quad in range(4):
                for j in range(4):
                    sp.dma_start(kS[quad * 32:(quad + 1) * 32, j, :], (khi, klo)[quad % 2][j * 32:(j + 1) * 32, :])\
                        .then_inc(s["kS_ready"], 16)
            with sp.Fori(1, PAIRS // 2) as i:
                for p in range(2):
                    sp.wait_ge(s["wsp_ready"], i * 4 + 2 * (p - 1))
                    sp.dma_start(raw[:, p, 0:3 * P], w_first[bass.ds(i * 2 + p, 1), :, :]).then_inc(raw_ready[p], 16)
            sp.wait_ge(s["wsp_ready"], 2 * (PAIRS - 2))
            sp.dma_start(raw[:, 0, 0:3 * P], w_first[PAIRS - 1, :, :]).then_inc(raw_ready[0], 16)
            sp.wait_ge(s["wsp_ready"], 2 * PAIRS)
            for e in range(2):
                sp.dma_start(raw[:, e, :], w_second[e, :, :]).then_inc(raw1_ready[e], 16)
            with sp.Fori(1, X1 // 2) as i:
                for p in range(2):
                    sp.wait_ge(s["wsp1_ready"], i * 4 + 2 * (p - 1))
                    sp.dma_start(raw[:, p, :], w_second[bass.ds(i * 2 + p, 1), :, :]).then_inc(raw1_ready[p], 16)
            for g in range(G):
                sp.wait_ge(s["x_out"], g + 1)
                sp.dma_start(out_v[:, gt(g), :], xr[:, gt(g), :]).then_inc(s["out_done"], 16)
            sp.wait_ge(s["out_done"], 16 * G)

        @block.gpsimd
        def _(pool):
            fill = chain(pool, s["fill_chain"])
            def rsqrt(l, g):
                pool.wait_ge(s["var_ready"], l * G + g + 1)
                pool.tensor_tensor(rstd[:, gt(g)], ve[:, gt(g)], minus_half[:, 0:TG], ALU.pow).then_inc(s["rstd_ready"], 1)

            def key_mask(h):
                pool.tensor_scalar(kM[:, h, :], kS[:, h // 4, :], pc("headmask")[:, h % 4:h % 4 + 1], 1.0, ALU.mult, ALU.mult)\
                    .then_inc(s["kM_ready"], 1)

            fill(pool.memset(minus_half[:], -0.5))
            for g in range(G):
                rsqrt(0, g)
            pool.wait_ge(s["rstd_ready"], G)
            pool.memset(log_ps[:], math.log(PS))
            pool.memset(ones_row[:], 1.0).then_inc(s["ones_ready"], 1)
            pool.memset(strow[:], 0.0).then_inc(s["st_zero"], 1)
            fill(pool.memset(combt[:], 0.0))
            pool.memset(combt[:, :, :, X0:X0 + 1], XS).then_inc(s["comb_zero"], 1)
            pool.memset(ctxM[:], 0.0).then_inc(s["ctxm_zero"], 1)
            fill(pool.memset(v1[:], 0.0))
            pool.memset(v1[0:S, :, :, 8:9], VS)
            pool.memset(v1[S:P, :, :, 17:18], VS).then_inc(s["v1_zero"], 1)
            pool.wait_ge(s["v1_zero"], 1)

            pool.wait_ge(s["in_ctx"], 16)
            pool.wait_ge(s["ctxm_zero"], 1)
            for h in range(H0):
                q = slice(h * D0, (h + 1) * D0)
                pool.tensor_scalar(ctxM[q, :, h, :], ctxT[q, :].rearrange("p (b s) -> p b s", s=S), D0 ** -0.5, 1.0,
                                   ALU.mult, ALU.mult).then_inc(s["ctxm_ready"], 1)
                pool.wait_ge(s["ctxm_ready"], h + 1)
            pool.wait_ge(s["kT_ready"], G)
            pool.tensor_scalar(khi[:], kT[:], 1.0, 1.0, ALU.mult, ALU.mult).then_inc(s["khi_ready"], 1)
            pool.wait_ge(s["khi_ready"], 1)
            pool.tensor_tensor(klo[:], kT[:], khi[:], ALU.subtract).then_inc(s["klo_ready"], 1)
            pool.wait_ge(s["in_qkvo"], 16)
            pool.tensor_scalar(wqr[:].rearrange("p j (r f) -> p j r f", f=32),
                               wq[:, 0, :].rearrange("p (j f) -> p j f", f=32).unsqueeze(2).to_broadcast([P, 4, 4, 32]),
                               AS, 1.0, ALU.mult, ALU.mult).then_inc(s["wqr_ready"], 1)
            pool.wait_ge(s["vmean_ready"], 1)
            v0g = v0[:].rearrange("p b c (h d) -> p (b c h) d", h=2)[:, :, 0:D0]
            pool.tensor_tensor(v0g, v0g, vmean[:].unsqueeze(2).to_broadcast([P, NB * 4, D0]), ALU.subtract).then_inc(s["v0_ready"], 1)
            pool.wait_ge(s["kS_ready"], 16 * 16)
            for h in range(H1):
                key_mask(h)
            for g in range(G):
                rsqrt(1, g)

            def split_pair(j, p, arrivals):
                for q in range(2):
                    c = slice(0, 2 * P) if q == 0 else slice(2 * P, 3 * P)
                    n = 2 * j + q
                    pool.wait_ge(raw_ready[p], arrivals)
                    pool.wait_ge(s["wsp_ready"], n)
                    pool.tensor_scalar(raws[:, c], raw[:, p, c], XS, 1.0, ALU.mult, ALU.mult).then_inc(s["raws_ready"], 1)
                    pool.wait_ge((s["mm1"], s["mm2"])[q], reached(2 * j - 2))
                    pool.tensor_scalar(wsp[:, p, 0, c], raw[:, p, c], XS, 1.0, ALU.mult, ALU.mult).then_inc(s["wsp_hi"], 1)
                    pool.wait_ge(s["raws_ready"], n + 1)
                    pool.wait_ge(s["wsp_hi"], n + 1)
                    pool.tensor_tensor(wsp[:, p, 1, c], raws[:, c], wsp[:, p, 0, c], ALU.subtract).then_inc(s["wsp_ready"], 1)

            split_pair(0, 0, 16)
            split_pair(1, 1, 16)
            for j in range(2, PAIRS):
                split_pair(j, j % 2, 16 * (j // 2 + 1))
                if j == 2:
                    pool.wait_ge(s["v1_copied"], 4)
                    pool.tensor_scalar(v1hi[:], v1[:], 1.0, 1.0, ALU.mult, ALU.mult).then_inc(s["v1hi_ready"], 1)
                if j in (3, 4):
                    pool.wait_ge(s["v1hi_ready"], 1)
                    b = slice((j - 3) * NBG, (j - 2) * NBG)
                    pool.tensor_tensor(v1lo[:, b], v1[:, b], v1hi[:, b], ALU.subtract).then_inc(s["v1lo_ready"], 1)
            for g in range(G):
                rsqrt(2, g)

            def split_expert(e, p, arrivals):
                pool.wait_ge(raw1_ready[p], arrivals)
                for q in range(2):
                    c = slice(q * N, (q + 1) * N)
                    n = 2 * e + q
                    pool.wait_ge(s["wsp1_ready"], n)
                    pool.tensor_scalar(raws[:, c], raw[:, p, c], XS, 1.0, ALU.mult, ALU.mult).then_inc(s["raws1_ready"], 1)
                    pool.wait_ge((s["mm1b"], s["mm2b"])[q], 12 if e == 2 else reached(8 * e - 8))
                    pool.tensor_scalar(wsp[:, p, 0, c], raw[:, p, c], XS, 1.0, ALU.mult, ALU.mult).then_inc(s["wsp1_hi"], 1)
                    pool.wait_ge(s["raws1_ready"], n + 1)
                    pool.wait_ge(s["wsp1_hi"], n + 1)
                    pool.tensor_tensor(wsp[:, p, 1, c], raws[:, c], wsp[:, p, 0, c], ALU.subtract).then_inc(s["wsp1_ready"], 1)

            pool.wait_ge(s["mm2"], 2 * PAIRS)
            split_expert(0, 0, 16)
            split_expert(1, 1, 16)
            for t in range(NT):
                pool.wait_ge(s["sexp"], t + 1)
                pool.wait_ge(s["pTp"], reached(2 * t - 2))
                pool.tensor_tensor(plo[:, t % 2, :], prob[:, t % 2, :], phi[:, t % 2, :], ALU.subtract).then_inc(s["plo_ready"], 1)
                if t == NT - 2:
                    rsqrt(3, 0)
            rsqrt(3, 1)

            def accumulate(n, g):
                pool.wait_ge(s["ymul"], n + 1)
                pool.wait_ge(s["yacc"], n)
                pool.tensor_tensor(yT[:, g, :], yT[:, g, :], ytmp[:, g, :], ALU.add).then_inc(s["yacc"], 1)

            pool.wait_ge(s["yTp"], G)
            pool.memset(yT[:], 0.0).then_inc(s["acc_zero"], 1)
            pool.wait_ge(s["acc_zero"], 1)
            accumulate(0, 0)
            for e in range(2, X1):
                split_expert(e, e % 2, 16 * (e // 2 + 1))
                for n in (2 * e - 3, 2 * e - 2):
                    accumulate(n, n // 2 % 2 if n < 4 else n % 2)
            for n in range(2 * X1 - 3, 2 * X1):
                accumulate(n, n % 2)

        @block.scalar
        def _(a):
            a.dma_start(xr[:, gt(1), :], x_v[:, gt(1), :]).then_inc(in_x[1], 16)
            a.dma_start(rw[:], rows).then_inc(s["in_rows"], 16)
            a.dma_start(cz[:], causal).then_inc(s["in_cz"], 16)
            a.dma_start(idh[:], ident_h).then_inc(s["in_idh"], 16)
            a.dma_start(idb[:], ident_b).then_inc(s["in_idh"], 16)
            a.preload_act_table_set("natural_log_exp_and_others")

            def copy_xT(l, g, b):
                a.wait_ge(s["xnT_ready"], l * G + g + 1)
                a.activation(xT[:, tok(g)], bank(b), ACT.Copy).then_inc(s["xT_ready"], 1)

            for g in range(G):
                copy_xT(0, g, 4 * g)
            for g in range(G):
                a.wait_ge(s["kproj"], g + 1)
                a.wait_ge(s["bqs_ready"], 1)
                a.activation(kT[:, tok(g)], bank(6 + g), ACT.Identity, bias=bks[:], scale=AS).then_inc(s["kT_ready"], 1)
            for g in range(G):
                a.wait_ge(s["z_ready"], g + 1)
                a.activation(lrow[:, g, :], zrow[:, g, :], ACT.Abs).then_inc(s["az_ready"], 1)
                a.wait_ge(s["az_ready"], g + 1)
                a.activation(lrow[:, g, :], lrow[:, g, :], ACT.Exp, scale=-1.0).then_inc(s["ez_ready"], 1)
                a.wait_ge(s["ez_ready"], g + 1)
                a.activation(lrow[:, g, :], lrow[:, g, :], ACT.Ln, bias=1.0).then_inc(s["ln_ready"], 1)
            for g in range(G):
                a.wait_ge(s["cm_ready"], g + 1)
                a.activation(strow[32:36, g, :], nmrow[:, g, :], ACT.Exp, scale=-1.0).then_inc(s["en_ready"], 1)
            for g in range(G):
                a.wait_ge(s["dpre"], g + 1)
                a.activation(decay[:, g, :], decay[:, g, :], ACT.Exp).then_inc(s["dexp"], 1)
            for g in range(G):
                a.wait_ge(s["cTp"], g + 1)
                a.activation(cT[:, g, :], ps[:, 4 * g + 2:4 * g + 4, :], ACT.Copy).then_inc(s["cT_ready"], 1)
            for g in range(G):
                a.wait_ge(s["o0"], g + 1)
                a.activation(hsq[:, g, :, :].rearrange("p (b th) d -> p b th d", b=2), head_outputs(g)[:, :, :, 0:D0],
                             ACT.Square)
                a.activation(den[:, g, :].rearrange("p (b th) -> p b th", b=2).unsqueeze(3), head_outputs(g)[:, :, :, D0:],
                             ACT.Abs).then_inc(s["hsq_ready"], 1)
            for g in range(G):
                a.wait_ge(s["h_var"], g + 1)
                a.activation(hy[:, g, :], hve[:, g, :], ACT.Ln).then_inc(s["h_ln"], 1)
                a.wait_ge(s["h_ln"], g + 1)
                a.activation(hy[:, g, :], hy[:, g, :], ACT.Exp, scale=-0.5).then_inc(s["h_rstd"], 1)
            a.wait_ge(s["v1_zero"], 1)
            for c in range(4):
                a.wait_ge(s["vproj"], c + 1)
                src = bank((2, 3, 6, 7)[c]).rearrange("p (b c d) -> p b c d", b=4, d=16)
                for hf in range(2):
                    q = slice(hf * S, (hf + 1) * S)
                    last = a.activation(v1[q, 4 * c:4 * c + 4, :, 9 * hf:9 * hf + 8], src[q, :, :, 8 * hf:8 * hf + 8],
                                        ACT.Copy, scale=VS)
                last.then_inc(s["v1_copied"], 1)

            def split_x(l, k, g, b):
                copy_xT(l, g, b)
                a.wait_ge(s["kS_ready"], 16 * 16)
                a.activation(xhi[:, tok(g)], bank(b), ACT.Copy, scale=XS).then_inc(s["xhi_ready"], 1)

            for g in range(G):
                split_x(1, 0, g, 4 * g)
            for g in range(G):
                a.wait_ge(s["logits"], g + 1)
                a.activation(rt[:, g, 0, :, :], bank(logit_bank(0, g))[:, 0:TG * X0].rearrange("p (t x) -> p t x", x=X0),
                             ACT.Exp, scale=-1.0).then_inc(s["lexp"], 1)
            def copy_gates(k, g):
                a.wait_ge(s["combTp"], k * G + g + 1)
                a.activation(combT[:, g, :], bank(gate_bank(k, g))[:, 0:N // 2].bitcast(F16), ACT.Copy).then_inc(s["combT_ready"], 1)

            for g in range(G):
                copy_gates(0, g)

            def silu_step(n, k):
                a.wait_ge(s["mm1"], n + 1)
                a.wait_ge(s["tmul"], reached(n - 1))
                a.activation(act[:, k, :], bank(k), ACT.Silu, scale=1 / (XS * XS)).then_inc(s["silu"], 1)

            def gate_step(n, k):
                a.wait_ge(s["hmul"], reached(n - 1))
                a.activation(cb[:, k, :], bank(4 + k), ACT.Copy, scale=HS / (XS * XS * XS)).then_inc(s["cbx"], 1)

            def high_step(n, k):
                a.wait_ge(s["hmul"], n + 1)
                a.wait_ge(s["mm2"], reached(n - 1))
                a.activation(hhi[:, k, :], h32[:, k, :], ACT.Copy).then_inc(s["hhi_r"], 1)

            def ffn0_step(n, k, last=False):
                if not last:
                    silu_step(n + 1, (k + 1) % 2)
                high_step(n, k)
                if not last:
                    gate_step(n + 1, (k + 1) % 2)

            silu_step(0, 0)
            gate_step(0, 0)
            for n in range(4):
                ffn0_step(n, n % 2)
            with a.Fori(4, 4 * (PAIRS // 2), 4) as n:
                for k in range(4):
                    ffn0_step(n + k, k % 2)
            n0 = 2 * (PAIRS - 1)
            ffn0_step(n0, 0)
            ffn0_step(n0 + 1, 1, last=True)
            for g in range(G):
                a.wait_ge(s["mm2"], reached(2 * PAIRS - 1 + g))
                a.activation(yT[:, g, :], bank(6 + g), ACT.Copy, scale=1 / (XS * HS)).then_inc(s["yT_ready"], 1)

            for g in range(G):
                copy_xT(2, g, 7 - g)

            def query_high(c, jj):
                a.wait_ge(s["qproj"], 2 * c + jj + 1)
                for j in range(2 * jj, 2 * jj + 2):
                    a.activation(qS[:, j, c * Q4:(c + 1) * Q4], bank(qbank(c, jj))[:, (j % 2) * Q4:(j % 2 + 1) * Q4],
                                 ACT.Identity, bias=bqs[:, j:j + 1]).then_inc(s["qhi_ready"], 1)

            for c in range(2):
                for jj in range(2):
                    query_high(c, jj)

            def copy_oT(t):
                a.wait_ge(s["oTp"], t + 1)
                a.wait_ge(s["oproj"], reached(t))
                a.activation(oT[:], bank(7)[:, 0:P], ACT.Copy).then_inc(s["oT_ready"], 1)

            def exp_scores(t):
                a.wait_ge(s["ssub"], t + 1)
                a.wait_ge(s["pTp"], reached(2 * t - 2))
                a.activation(phi[:, t % 2, :], prob[:, t % 2, :], ACT.Exp, bias=log_ps[:], scale=D1 ** -0.5 / (AS * AS))\
                    .then_inc(s["phi_ready"], 1)
                a.wait_ge(s["phi_ready"], t + 1)
                a.activation(prob[:, t % 2, :], prob[:, t % 2, :], ACT.Exp, bias=log_ps[:], scale=D1 ** -0.5 / (AS * AS))\
                    .then_inc(s["sexp"], 1)

            def gate_tanh(g):
                a.wait_ge(s["rdiff"], g + 1)
                a.activation(rt[:, g, 1, :, 0:X1], rt[:, g, 0, :, 0:X1], ACT.Tanh).then_inc(s["lexp"], 1)

            def copy_pT(t):
                for part in range(2):
                    a.wait_ge(s["pTp"], 2 * t + part + 1)
                    a.wait_ge(s["av"], reached(t - 1))
                    a.activation(pT[:, t % 2, part, :].bitcast(F32), bank(4 + part), ACT.Copy).then_inc(s["pT_ready"], 1)

            for i in range(NT + 4):
                if i < 4:
                    query_high(2 + i // 2, i % 2)
                if i >= 4:
                    copy_oT(i - 4)
                if 2 <= i < NT + 2:
                    copy_pT(i - 2)
                if i < NT:
                    exp_scores(i)
                if i == NT:
                    split_x(3, 1, 0, 0)
                if i == NT + 2:
                    gate_tanh(0)
            copy_gates(1, 0)

            def gelu_step(n, q, k, first=False):
                a.wait_ge(s["mm1b"], n + 1)
                a.wait_ge(s["hlo1"], reached(n - 3))
                a.activation(h32[:, k % 4, :], bank(k % 4), ACT.Gelu, scale=1 / (XS * XS)).then_inc(s["gelu"], 1)
                if k % FC == 0 and not (first and k < 16):
                    copy_gate(q, k)

            def copy_gate(q, k, first=False):
                g = place(k, first)[1]
                a.wait_ge(s["ymul"], before(q, first))
                a.activation(cb[:, g, :], bank(6 + g), ACT.Copy, scale=1 / (XS * XS * HS)).then_inc(s["cbx1"], 1)

            def high1_step(n, k):
                a.wait_ge(s["gelu"], n + 1)
                a.wait_ge(s["mm2b"], reached(n - 3))
                a.activation(hhi[:, k % 4, :], h32[:, k % 4, :], ACT.Copy, scale=HS).then_inc(s["hhi1"], 1)

            def expert_pair(base, q0, first=False, last=False):
                for k in range(16):
                    if first and k == 2:
                        split_x(3, 1, 1, 5)
                    if first and k == 4:
                        gate_tanh(1)
                    if first and k == 5:
                        copy_gates(1, 1)
                    if not (last and k == 15):
                        gelu_step(base + (k + 1), q0 + (k + 1) // FC, k + 1, first)
                    high1_step(base + k, k)
                    if first and k % FC == 0:
                        copy_gate(k // FC, k, first)

            gelu_step(0, 0, 0, first=True)
            expert_pair(0, 0, first=True)
            with a.Fori(1, 3) as i:
                expert_pair(i * 16, i * 4)
            expert_pair(48, 12, last=True)

        @block.vector
        def _(v):
            stat = chain(v, s["stat_chain"])
            row = chain(v, s["row_chain"])
            head = chain(v, s["head_chain"])
            route = chain(v, s["route_chain"])

            def ln_stats(l, g):
                for t in range(g * TG, (g + 1) * TG):
                    last = v.bn_stats(stats[:, t, :], xr[:, t, :])
                stat(last)
                for t in range(g * TG, (g + 1) * TG):
                    last = v.bn_aggr(mv[:, t, :], stats[:, t, :])
                stat(last)
                if l:
                    v.wait_ge(s["rstd_ready"], l * G)
                v.tensor_scalar(ve[:, gt(g)], mv[:, gt(g), 1], LN_EPS, None, ALU.add).then_inc(s["var_ready"], 1)

            def ln_apply(l, g):
                v.wait_ge(s["rstd_ready"], l * G + g + 1)
                if l:
                    v.wait_ge(s["xnT_ready"], l * G)
                for t in range(g * TG, (g + 1) * TG):
                    last = v.tensor_scalar(xn[:, t, :], xr[:, t, :], mv[:, t, 0:1], rstd[:, t:t + 1],
                                           ALU.subtract, ALU.mult)
                last.then_inc(s["xn_ready"], 1)

            for g in range(G):
                v.wait_ge(in_x[g], 16)
                ln_stats(0, g)
            v.wait_ge(s["in_pack"], 16)
            v.tensor_tensor(wgc[:], wgv[:, 1, :], wgv[:, 2, :], ALU.add).then_inc(s["wgc_ready"], 1)
            v.tensor_scalar(bks[:], pc("bk"), AS, None, ALU.mult)
            v.tensor_scalar(bqs[:], pc("bq"), AS, None, ALU.mult).then_inc(s["bqs_ready"], 1)
            v.tensor_scalar(owp[:], pc("out_w"), 1.0, None, ALU.add)
            for g in range(G):
                ln_apply(0, g)
            v.wait_ge(s["in_v"], 16)
            stat(v.tensor_reduce(vmean[:], v0[:].rearrange("p b c (h d) -> p (b c h) d", h=2)[:, :, 0:D0], AX_X, ALU.add))
            v.tensor_scalar(vmean[:], vmean[:], 1 / D0, None, ALU.mult).then_inc(s["vmean_ready"], 1)
            fg_bias = pk[32:36, PACK["gb"][0]:PACK["gb"][1]]
            ig_bias = pk[0:4, PACK["gb"][0]:PACK["gb"][1]]
            for g in range(G):
                v.wait_ge(s["gates"], g + 1)
                v.tensor_scalar(zrow[:, g, :], bank(4 * g + 1)[32:36, :], fg_bias, None, ALU.add).then_inc(s["z_ready"], 1)
            v.wait_ge(s["in_rows"], 16)
            v.wait_ge(s["st_zero"], 1)
            for g in range(G):
                v.wait_ge(s["ln_ready"], g + 1)
                row(v.scalar_tensor_tensor(lf[:, g, :], zrow[:, g, :], 0.0, lrow[:, g, :], ALU.min, ALU.subtract))
                row(v.tensor_tensor_scan(csum[:, g, :], reset_mul, lf[:, g, :], 0.0, ALU.mult, ALU.add))
                row(v.scalar_tensor_tensor(urow[:, g, :], bank(4 * g + 1)[0:4, :], ig_bias, lf[:, g, :],
                                                ALU.add, ALU.add))
                v.tensor_tensor(crow[:, g, :], urow[:, g, :], csum[:, g, :], ALU.subtract).then_inc(s["c_ready"], 1)
                v.wait_ge(s["c_ready"], g + 1)
                row(v.tensor_tensor_scan(strow[0:4, g, :], reset_add, crow[:, g, :], 0.0, ALU.add, ALU.max))
                v.tensor_tensor(nmrow[:, g, :], csum[:, g, :], strow[0:4, g, :], ALU.add).then_inc(s["cm_ready"], 1)
            for g in range(G):
                v.wait_ge(s["stT"], g + 1)
                v.tensor_copy(sttok[:, g, :, :], bank(4 * g)[:, 0:TG * S].rearrange("p (t c) -> p t c", c=S))\
                    .then_inc(s["sttok_ready"], 1)
                v.wait_ge(s["sttok_ready"], g + 1)
                head(v.tensor_scalar(sttok[:, g, :, 32:36], sttok[:, g, :, 32:36], NORM_EPS, None, ALU.add))
            for g in range(G):
                v.wait_ge(s["cbc"], g + 1)
                v.wait_ge(s["sttok_ready"], g + 1)
                dv = decay[:, g, :].rearrange("p (t h k) -> p h t k", t=TG, h=H0)
                cv = ps[:, 4 * g + 2:4 * g + 4, :].rearrange("p b (h t k) -> p (b h) t k", t=TG, k=S)
                for h in range(H0):
                    mxv = sttok[:, g, :, h:h + 1].to_broadcast([P, TG, S])
                    last = v.tensor_tensor(dv[:, h, :, :], cv[:, h, :, :], mxv, ALU.subtract)
                last.then_inc(s["dpre"], 1)
            for g in range(G):
                v.wait_ge(s["s0"], g + 1)
                v.wait_ge(s["dexp"], g + 1)
                v.tensor_tensor(cmat[:, g, :], ps[:, 4 * g:4 * g + 2, :].rearrange("p b c -> p (b c)"), decay[:, g, :],
                                ALU.mult).then_inc(s["cmat_ready"], 1)
            for g in range(G):
                v.wait_ge(s["hsq_ready"], g + 1)
                head(v.scalar_tensor_tensor(den[:, g, :].rearrange("p (t h) -> p t h", h=H0),
                                            den[:, g, :].rearrange("p (t h) -> p t h", h=H0), NORM_EPS,
                                            sttok[:, g, :, 32:36], ALU.add, ALU.max))
                head(v.reciprocal(rden[:, g, :], den[:, g, :]))
                v.tensor_tensor(hq[:, g, :], rden[:, g, :], rden[:, g, :], ALU.mult)
                head(v.tensor_reduce(hsum[:, g, :], hsq[:, g, :, :], AX_X, ALU.add))
                head(v.scalar_tensor_tensor(hve[:, g, :], hsum[:, g, :], 1 / D0, hq[:, g, :], ALU.mult, ALU.mult))
                v.tensor_scalar(hve[:, g, :], hve[:, g, :], LN_EPS, None, ALU.add).then_inc(s["h_var"], 1)
            for g in range(G):
                y = hy[:, g, :]
                v.wait_ge(s["h_rstd"], g + 1)
                head(v.tensor_tensor(hq[:, g, :], y, y, ALU.mult))
                head(v.scalar_tensor_tensor(hq[:, g, :], hq[:, g, :], -0.5, hve[:, g, :], ALU.mult, ALU.mult))
                head(v.scalar_tensor_tensor(hrs[:, g, :], hq[:, g, :], 1.5, y, ALU.add, ALU.mult))
                head(v.tensor_tensor(hrs[:, g, :], hrs[:, g, :], rden[:, g, :], ALU.mult))
                head(v.tensor_tensor(hh[:, g, :, :].rearrange("p (b th) d -> p b th d", b=2), head_outputs(g)[:, :, :, 0:D0],
                                     hrs[:, g, :].rearrange("p (b th) -> p b th", b=2).unsqueeze(3)
                                     .to_broadcast([P, 2, 8, D0]), ALU.mult))
                h4 = hh[:, g, :, :].rearrange("p (t h) d -> p t (h d)", h=H0)
                head(v.tensor_tensor(h4, h4, owp[:].unsqueeze(1).to_broadcast([P, TG, E]), ALU.mult))
                head(v.tensor_tensor(xr[:, gt(g), :], xr[:, gt(g), :], h4, ALU.add))
                ln_stats(1, g)

            def low_x(l, k, g, b):
                v.wait_ge(s["xhi_ready"], k * G + g + 1)
                v.wait_ge(s["kS_ready"], 16 * 16)
                v.scalar_tensor_tensor(xlo[:, tok(g)], bank(b), XS, xhi[:, tok(g)], ALU.mult, ALU.subtract)\
                    .then_inc(s["xlo_ready"], 1)

            for g in range(G):
                ln_apply(1, g)
            for g in range(G):
                low_x(1, 0, g, 4 * g)
            v.wait_ge(s["comb_zero"], 1)
            v.wait_ge(s["lexp"], G)
            r = rt[:].rearrange("p g i t x -> p i g t x")
            gbias = pc("gate_b").unsqueeze(1).unsqueeze(1).to_broadcast([P, G, TG, X0])
            route(v.tensor_scalar(r[:, 0], r[:, 0], 1.0, None, ALU.add))
            route(v.reciprocal(r[:, 1], r[:, 0]))
            route(v.tensor_tensor(r[:, 2], r[:, 1], gbias, ALU.add))
            for g in range(G):
                for t in range(TG):
                    last = v.max(top[:, g, t, :], rt[:, g, 2, t, :])
            route(last)
            route(v.memset(top[:, :, :, TOP0:], 3 * LOWEST))
            for g in range(G):
                for t in range(TG):
                    last = v.match_replace(rt[:, g, 3, t, :], top[:, g, t, :], rt[:, g, 2, t, :], LOWEST)
            route(last)
            route(v.tensor_scalar(r[:, 4], r[:, 3], LOWEST / 2, None, ALU.is_lt))
            route(v.tensor_tensor(r[:, 4], r[:, 4], r[:, 1], ALU.mult))
            route(v.tensor_reduce(rsum[:], r[:, 4], AX_X, ALU.add))
            route(v.reciprocal(rrec[:], rsum[:]))
            route(v.tensor_scalar(rrec[:], rrec[:], ROUTE_SCALE * XS, None, ALU.mult))
            route(v.tensor_tensor(r[:, 5], r[:, 4], rrec[:].unsqueeze(3).to_broadcast([P, G, TG, X0]), ALU.mult))
            route(v.tensor_copy(combt[:, :, :, 0:X0], r[:, 5]))
            v.tensor_tensor(combt[:, :, :, 32:32 + X0], r[:, 5], combt[:, :, :, 0:X0], ALU.subtract)\
                .then_inc(s["comb_ready"], G)

            def mul_step(n, k):
                v.wait_ge(s["silu"], n + 1)
                v.tensor_tensor(gu[:, k, :], act[:, k, :], bank(2 + k), ALU.mult).then_inc(s["tmul"], 1)

            def gate_step(n, k):
                v.wait_ge(s["cbx"], n + 1)
                v.wait_ge(s["tmul"], n + 1)
                v.wait_ge(s["hhi_r"], reached(n - 1))
                v.tensor_tensor(h32[:, k, :], gu[:, k, :], cb[:, k, :], ALU.mult).then_inc(s["hmul"], 1)

            def low_step(n, k):
                v.wait_ge(s["hhi_r"], n + 1)
                v.wait_ge(s["mm2"], reached(n - 1))
                v.tensor_tensor(hlo[:, k, :], h32[:, k, :], hhi[:, k, :], ALU.subtract).then_inc(s["hlo_r"], 1)

            def ffn0_step(n, k, last=False):
                if not last:
                    mul_step(n + 1, (k + 1) % 2)
                low_step(n, k)
                if not last:
                    gate_step(n + 1, (k + 1) % 2)

            mul_step(0, 0)
            gate_step(0, 0)
            for n in range(4):
                ffn0_step(n, n % 2)
            with v.Fori(4, 4 * (PAIRS // 2), 4) as n:
                for k in range(4):
                    ffn0_step(n + k, k % 2)
            n0 = 2 * (PAIRS - 1)
            ffn0_step(n0, 0)
            ffn0_step(n0 + 1, 1, last=True)

            def add_y(g, b):
                v.wait_ge(s["yTp"], g + 1)
                stat(v.tensor_tensor(xr[:, gt(g), :], xr[:, gt(g), :], bank(b).rearrange("p (t e) -> p t e", e=E), ALU.add))

            for g in range(G):
                add_y(g, g)
                ln_stats(2, g)
            for g in range(G):
                ln_apply(2, g)
                v.wait_ge(s["xn_ready"], 2 * G + g + 1)
                last = v.tensor_tensor(xr[:, gt(g), :], xr[:, gt(g), :], pc("bo").unsqueeze(1).to_broadcast([P, TG, E]), ALU.add)
                stat(last)

            def scores(t):
                k = t % 2
                v.wait_ge(s["s1"], t + 1)
                sv = ps[:, 2 * k:2 * k + 2, :].rearrange("p b (h k) -> p (b h) k", k=S)
                v.tensor_reduce(rmax[:, k, :], sv, AX_X, ALU.max).then_inc(s["smax"], 1)
                v.wait_ge(s["smax"], t + 1)
                v.wait_ge(s["plo_ready"], reached(t - 1))
                v.tensor_tensor(prob[:, k, :].rearrange("p (h k) -> p h k", k=S), sv,
                                rmax[:, k, :].unsqueeze(2).to_broadcast([P, H1, S]), ALU.subtract).then_inc(s["ssub"], 1)

            o1ch = chain(v, s["o1_chain"])

            def query_low(c, jj):
                v.wait_ge(s["qhi_ready"], 4 * c + 2 * jj + 2)
                for j in range(2 * jj, 2 * jj + 2):
                    q = qS[S:P, j, c * Q4:(c + 1) * Q4]
                    v.scalar_tensor_tensor(q, bank(qbank(c, jj))[S:P, (j % 2) * Q4:(j % 2 + 1) * Q4], bqs[S:P, j:j + 1], q,
                                           ALU.add, ALU.subtract).then_inc(s["qS_ready"], 1)

            for jj in range(2):
                query_low(0, jj)

            def normalise(t):
                v.wait_ge(s["av"], t + 1)
                halves = [(slice(hf * S, (hf + 1) * S), bank(6)[hf * S:(hf + 1) * S, 0:8 * 36]
                           .rearrange("p (c b d e) -> p c b d e", b=2, d=2, e=9)[:, :, hf, :, :]) for hf in range(2)]
                for q, ov in halves:
                    last = v.tensor_scalar(rs1[q, :].rearrange("p (c d) -> p c d", d=2).unsqueeze(3), ov[:, :, :, 8:9],
                                           0.5 * PS * VS, None, ALU.max)
                o1ch(last)
                o1ch(v.reciprocal(rs1b[:], rs1[:]))
                for q, ov in halves:
                    last = v.tensor_tensor(o1[q, :, :].rearrange("p (c d) e -> p c d e", d=2), ov[:, :, :, 0:8],
                                           rs1b[q, :].rearrange("p (c d) -> p c d", d=2).unsqueeze(3)
                                           .to_broadcast([S, 8, 2, D1]), ALU.mult)
                o1ch(last)
                o1ch(v.tensor_scalar(o1n[:], o1[:], 0.0, None, ALU.min))
                v.wait_ge(s["oTp"], reached(t - 1))
                v.scalar_tensor_tensor(o1c[:, t % 2, :], o1[:].rearrange("p h d -> p (h d)"), 0.0,
                                       o1n[:].rearrange("p h d -> p (h d)"), ALU.max, ALU.add).then_inc(s["o1_ready"], 1)

            def add_attention(t):
                v.wait_ge(s["oproj"], t + 1)
                v.tensor_tensor(xr[:, t, :], xr[:, t, :], bank(7)[:, P:2 * P], ALU.add).then_inc(s["x_att"], 1)

            def route1_first(g):
                v.wait_ge(s["logits"], G + g + 1)
                v.wait_ge(s["combTp"], G)
                r = rt[:, g, :, :, 0:X1]
                lv = bank(logit_bank(1, g))[:, 0:TG * X0].rearrange("p (t x) -> p t x", x=X0)[:, :, 0:X1]
                route(v.tensor_copy(r[:, 2], lv))
                for t in range(TG):
                    last = v.max(top[:, g, t, :], r[:, 2, t, :])
                route(last)
                route(v.tensor_tensor(rsum[:, g, :].unsqueeze(2), top[:, g, :, 0:1], top[:, g, :, 1:2], ALU.add))
                v.scalar_tensor_tensor(r[:, 0], rsum[:, g, :].unsqueeze(2).to_broadcast([P, TG, X1]), -0.5, r[:, 2],
                                       ALU.mult, ALU.add).then_inc(s["rdiff"], 1)

            def route1_second(g):
                r = rt[:, g, :, :, 0:X1]
                route(v.memset(top[:, g, :, 2:], 3 * LOWEST))
                for t in range(TG):
                    last = v.match_replace(r[:, 3, t, :], top[:, g, t, :], r[:, 2, t, :], LOWEST)
                route(last)
                route(v.tensor_scalar(r[:, 4], r[:, 3], LOWEST / 2, XS / 2, ALU.is_lt, ALU.mult))
                v.wait_ge(s["lexp"], G + g + 1)
                route(v.scalar_tensor_tensor(r[:, 5], r[:, 1], 1.0, r[:, 4], ALU.add, ALU.mult))
                route(v.tensor_copy(combt[:, g, :, 0:X1], r[:, 5]))
                v.tensor_tensor(combt[:, g, :, 32:32 + X1], r[:, 5], combt[:, g, :, 0:X1], ALU.subtract)\
                    .then_inc(s["comb_ready"], 1)

            for i in range(NT + 4):
                if i < NT:
                    scores(i)
                if i == 0:
                    for jj in range(2):
                        query_low(1, jj)
                if i < 4:
                    query_low(2 + i // 2, i % 2)
                if 3 <= i < NT + 3:
                    normalise(i - 3)
                if i >= 4:
                    add_attention(i - 4)
                if i == NT - 1:
                    v.wait_ge(s["x_att"], TG)
                    ln_stats(3, 0)
                if i == NT:
                    ln_apply(3, 0)
                if i == NT + 1:
                    low_x(3, 1, 0, 0)
                if i == NT + 2:
                    route1_first(0)
                    route1_second(0)
            v.wait_ge(s["x_att"], NT)
            ln_stats(3, 1)
            def low1_step(n, k):
                v.wait_ge(s["hhi1"], n + 1)
                v.wait_ge(s["mm2b"], reached(n - 3))
                v.scalar_tensor_tensor(hlo[:, k % 4, :], h32[:, k % 4, :], HS, hhi[:, k % 4, :], ALU.mult, ALU.subtract)\
                    .then_inc(s["hlo1"], 1)

            def gated(n, q, g, first=False, pair_before=False):
                v.wait_ge(s["mm2b"], n + 1)
                v.wait_ge(s["cbx1"], q + 1)
                v.wait_ge(s["yacc"], before(q, first) if not pair_before else q)
                v.tensor_tensor(ytmp[:, g, :], bank(4 + g), cb[:, g, :], ALU.mult).then_inc(s["ymul"], 1)

            def ffn1_expert_pair(base, q0, first=False):
                for k in range(16):
                    low1_step(base + k, k)
                    if k % FC == 0 and not (first and k == 0):
                        q = k // FC - 1
                        gated(base + (FC * q + 3), q0 + q, place(FC * q + 3, first)[1] if q >= 0 else 1, first, q < 0)
                    if first and k == 0:
                        ln_apply(3, 1)
                    if first and k == 2:
                        low_x(3, 1, 1, 5)
                    if first and k == 3:
                        route1_first(1)
                        route1_second(1)

            ffn1_expert_pair(0, 0, first=True)
            with v.Fori(1, 3) as i:
                ffn1_expert_pair(i * 16, i * 4)
            ffn1_expert_pair(48, 12)
            gated(63, 15, 1)
            for g in range(G):
                v.wait_ge(s["yTp1"], g + 1)
                v.tensor_tensor(xr[:, gt(g), :], xr[:, gt(g), :], bank(g).rearrange("p (t e) -> p t e", e=E), ALU.add)\
                    .then_inc(s["x_out"], 1)

        @block.tensor
        def _(pe):
            mm = pe.matmul

            pe.wait_ge(s["in_pack"], 16)
            pe.wait_ge(s["in_ctx"], 16)

            def transpose_norm(l, g, b):
                pe.wait_ge(s["xn_ready"], l * G + g + 1)
                for t in range(TG):
                    last = pe.transpose(bank(b)[:, t * P:(t + 1) * P], xn[:, g * TG + t, :], ident)
                last.then_inc(s["xnT_ready"], 1)

            def gates(g):
                pe.wait_ge(s["wgc_ready"], 1)
                mm(bank(4 * g + 1)[0:36, :], wgc[:], ctxT[:, tok(g)], start=True, stop=False)
                pe.wait_ge(s["xT_ready"], g + 1)
                mm(bank(4 * g + 1)[0:36, :], wgv[:, 0, :], xT[:, tok(g)], start=False, stop=True).then_inc(s["gates"], 1)

            for g in range(G):
                transpose_norm(0, g, 4 * g)
                gates(g)
            pe.wait_ge(s["in_qkvo"], 16)
            for g in range(G):
                mm(bank(6 + g), wq[:, 1, :], ctxT[:, tok(g)], start=True, stop=True).then_inc(s["kproj"], 1)
            pe.wait_ge(s["kT_ready"], G)
            pe.wait_ge(s["in_rows"], 16)
            pe.wait_ge(s["in_cz"], 16)
            pe.wait_ge(s["in_idh"], 32)
            for g in range(G):
                pe.wait_ge(s["c_ready"], g + 1)
                cv = crow[:, g, :].rearrange("a (t b k) -> a t b k", b=2, k=S)
                for pair in range(2):
                    for hf in range(2):
                        for h in range(2 * pair, 2 * pair + 2):
                            mm(ps[hf * S:(hf + 1) * S, 4 * g + 2 + pair, (h % 2) * TG * S:(h % 2 + 1) * TG * S],
                               head_sel[:, h, :], cv[:, :, hf, :], start=(h % 2 == 0), stop=False, skip_group_check=True)
                    last = mm(bank(4 * g + 2 + pair), idb[:], cz[:].unsqueeze(1).to_broadcast([P, 8, S]),
                              start=False, stop=True, skip_group_check=True)
                last.then_inc(s["cbc"], 1)
            for g in range(G):
                pe.wait_ge(s["en_ready"], g + 1)
                pe.wait_ge(s["xT_ready"], g + 1)
                for t in range(TG):
                    last = pe.transpose(bank(4 * g)[:, t * S:(t + 1) * S], strow[:, g, t * P:(t + 1) * P], ident[0:S, 0:S])
                last.then_inc(s["stT"], 1)
            pe.wait_ge(s["ctxm_ready"], H0)
            for g in range(G):
                pe.wait_ge(s["sttok_ready"], g + 1)
                for t in range(TG):
                    for hf in range(2):
                        b = 2 * (g * TG + t) + hf
                        last = mm(ps[hf * S:(hf + 1) * S, 4 * g + t // 2, (t % 2) * H0 * S:(t % 2 + 1) * H0 * S],
                                  xT[:, b * S:(b + 1) * S], ctxM[:, b, :, :].rearrange("p h k -> p (h k)"),
                                  start=True, stop=True)
                last.then_inc(s["s0"], 1)
            for g in range(G):
                pe.wait_ge(s["cmat_ready"], g + 1)
                for c in range(2 * TG):
                    last = pe.transpose(bank(4 * g + 2 + c // 4)[:, (c % 4) * P:(c % 4 + 1) * P],
                                        cmat[:, g, c * P:(c + 1) * P], ident)
                last.then_inc(s["cTp"], 1)
            pe.wait_ge(s["v0_ready"], 1)
            for g in range(G):
                pe.wait_ge(s["cT_ready"], g + 1)
                for t in range(TG):
                    for pair in range(2):
                        for hf in range(2):
                            b = 2 * (g * TG + t) + hf
                            c = (2 * t + pair) * P + hf * S
                            o = (t % 2) * 132 + pair * 66
                            last = mm(ps[hf * S:(hf + 1) * S, 4 * g + t // 2, o:o + 66], cT[:, g, c:c + S],
                                      v0[:, b, pair, :], start=True, stop=True)
                last.then_inc(s["o0"], 1)

            def v_products(c):
                for b in range(4 * c, 4 * c + 4):
                    for hf in range(2):
                        o = ps[hf * S:(hf + 1) * S, (2, 3, 6, 7)[c], (b % 4) * E:(b % 4 + 1) * E]
                        mm(o, ctxT[:, b * S:(b + 1) * S], wq[:, 2, :], start=True, stop=False)
                        last = mm(o, ones_row[:], pc("bv")[0:1, :], start=False, stop=True)
                last.then_inc(s["vproj"], 1)

            pe.wait_ge(s["ones_ready"], 1)
            for c in range(4):
                v_products(c)
            pe.wait_ge(s["v1_copied"], 4)

            def router(l, k, g, width, name):
                pe.wait_ge(s["xT_ready"], l * G + g + 1)
                for t in range(TG):
                    c = g * N + t * P
                    last = mm(bank(logit_bank(k, g))[:, t * X0:t * X0 + width], xT[:, c:c + P], pc(name), start=True, stop=True)
                last.then_inc(s["logits"], 1)

            def transpose_gates(k, g):
                pe.wait_ge(s["comb_ready"], k * G + g + 1)
                for t in range(TG):
                    last = pe.transpose(bank(gate_bank(k, g))[:, t * S:(t + 1) * S].bitcast(F16), combt[:, g, t, :], idh[:])
                last.then_inc(s["combTp"], 1)

            for g in range(G):
                transpose_norm(1, g, 4 * g)
            for g in range(G):
                router(1, 0, g, X0, "gate_w")

            def up0(n, j, k, p):
                inner0(n, j, k, p)
                broadcast0(j, k)

            def inner0(n, j, k, p):
                g = k
                pe.wait_ge(s["wsp_ready"], j * 2 + 1)
                pe.wait_ge(s["silu"], reached(n - 1))
                pe.wait_ge(s["tmul"], reached(n - 1))
                pe.wait_ge(s["cbx"], reached(n - 1))
                for i in range(2):
                    c = slice(i * P, (i + 1) * P)
                    mm(bank(2 * i + k), wsp[:, p, 0, c], xhi[:, tok(g)], start=True, stop=False)
                    mm(bank(2 * i + k), wsp[:, p, 0, c], xlo[:, tok(g)], start=False, stop=False)
                    mm(bank(2 * i + k), wsp[:, p, 1, c], xhi[:, tok(g)], start=False, stop=True)

            def broadcast0(j, k):
                pick = sel0[:, j, :] if type(j) is int else sel0[:, bass.ds(j, 1), :].rearrange("p a m -> p (a m)")
                mm(bank(4 + k), pick, combT[:, k, :], start=True, stop=True).then_inc(s["mm1"], 1)

            def down0(n, j, k, p, first, last):
                c = slice(2 * P, 3 * P)
                pe.wait_ge(s["wsp_ready"], j * 2 + 2)
                pe.wait_ge(s["hlo_r"], n + 1)
                mm(bank(6 + k), wsp[:, p, 0, c], hhi[:, k, :], start=first, stop=False)
                mm(bank(6 + k), wsp[:, p, 0, c], hlo[:, k, :], start=False, stop=False)
                mm(bank(6 + k), wsp[:, p, 1, c], hhi[:, k, :], start=False, stop=last).then_inc(s["mm2"], 1)

            pe.wait_ge(s["in_sel"], 32)
            pe.wait_ge(s["lexp"], G)
            for g in range(G):
                pe.wait_ge(s["xlo_ready"], g + 1)
                pe.wait_ge(s["xhi_ready"], g + 1)
                inner0(g, 0, g, 0)
            for g in range(G):
                transpose_gates(0, g)
            for g in range(G):
                pe.wait_ge(s["combT_ready"], g + 1)
                broadcast0(0, g)

            def two_pairs(j, first=False):
                for k in range(4):
                    up0(2 * j + (k + 2), j + (k // 2 + 1), k % 2, (k // 2 + 1) % 2)
                    down0(2 * j + k, j + k // 2, k % 2, k // 2, first and k < 2, False)

            two_pairs(0, first=True)
            with pe.Fori(1, PAIRS // 2) as i:
                two_pairs(i * 2)
            n0 = 2 * (PAIRS - 1)
            for g in range(G):
                down0(n0 + g, PAIRS - 1, g, 0, False, True)

            def keep_warm(b, count):
                for _ in range(count):
                    mm(bank(b), idh[:], sel0[:, 0:4, :], start=True, stop=True)

            def transpose_y(g, b, done):
                for t in range(TG):
                    last = pe.transpose(bank(b)[:, t * P:(t + 1) * P], yT[:, g, t * P:(t + 1) * P], ident)
                last.then_inc(done, 1)

            for g in range(G):
                pe.wait_ge(s["yT_ready"], g + 1)
                transpose_y(g, g, s["yTp"])
            keep_warm(3, 24)

            for g in range(G):
                pe.wait_ge(s["yT_ready"], G)
                transpose_norm(2, g, 7 - g)
            pe.wait_ge(s["wqr_ready"], 1)

            def query_products(c, jj):
                pe.wait_ge(s["xT_ready"], 2 * G + c // 2 + 1)
                if c >= 2:
                    if (c, jj) != (2, 0):
                        pe.wait_ge(s["qS_ready"], 4 * c + 2 * jj)
                for j in range(2 * jj, 2 * jj + 2):
                    last = mm(bank(qbank(c, jj))[:, (j % 2) * Q4:(j % 2 + 1) * Q4], wqr[:, j, :], xT[:, c * Q4:(c + 1) * Q4],
                              start=True, stop=True)
                last.then_inc(s["qproj"], 1)

            for jj in range(2):
                query_products(0, jj)
            pe.wait_ge(s["kM_ready"], H1)

            def scores1(t):
                pe.wait_ge(s["qS_ready"], 8 if t == 1 else 4 * (t // 2 + 1))
                pe.wait_ge(s["ssub"], reached(t - 1))
                for j in range(4):
                    for hf in range(2):
                        b = 2 * t + hf
                        last = mm(ps[hf * S:(hf + 1) * S, 2 * (t % 2) + j // 2, (j % 2) * 4 * S:(j % 2 + 1) * 4 * S],
                                  qS[:, j, b * S:(b + 1) * S], kM[:, 4 * j:4 * j + 4, b * S:(b + 1) * S], start=True, stop=True)
                last.then_inc(s["s1"], 1)

            def transpose_weights(t):
                pe.wait_ge(s["qS_ready"], 8)
                for part in range(2):
                    pe.wait_ge((s["phi_ready"], s["plo_ready"])[part], t + 1)
                    pe.wait_ge(s["pT_ready"], reached(2 * t - 1 + part))
                    for c in range(8):
                        last = pe.transpose(bank(4 + part)[:, c * S:(c + 1) * S].bitcast(F16),
                                            (phi, plo)[part][:, t % 2, c * P:(c + 1) * P], idh[:])
                    last.then_inc(s["pTp"], 1)

            def weighted_values(t):
                pe.wait_ge(s["v1lo_ready"], 2)
                pe.wait_ge(s["pT_ready"], 2 * t + 2)
                pe.wait_ge(s["o1_ready"], reached(t))
                for c in range(8):
                    o = bank(6)[:, c * 36:(c + 1) * 36]
                    hi, lo = (pT[:, t % 2, part, c * P:(c + 1) * P] for part in range(2))
                    mm(o, hi, v1hi[:, 2 * t:2 * t + 2, c, :], start=True, stop=False)
                    mm(o, hi, v1lo[:, 2 * t:2 * t + 2, c, :], start=False, stop=False)
                    last = mm(o, lo, v1hi[:, 2 * t:2 * t + 2, c, :], start=False, stop=True)
                last.then_inc(s["av"], 1)

            def transpose_values(t):
                pe.wait_ge(s["o1_ready"], t + 1)
                pe.wait_ge(s["x_att"], reached(t))
                pe.wait_ge(s["qS_ready"], 16)
                pe.transpose(bank(7)[:, 0:P], o1c[:, t % 2, :], ident).then_inc(s["oTp"], 1)

            def output_product(t):
                pe.wait_ge(s["oT_ready"], t + 1)
                mm(bank(7)[:, P:2 * P], oT[:], wq[:, 3, :], start=True, stop=True).then_inc(s["oproj"], 1)

            for i in range(NT + 4):
                if i < NT:
                    scores1(i)
                if i == 0:
                    for jj in range(2):
                        query_products(1, jj)
                if i < 4:
                    query_products(2 + i // 2, i % 2)
                if 3 <= i < NT + 3:
                    weighted_values(i - 3)
                if i >= 4:
                    transpose_values(i - 4)
                if 2 <= i < NT + 2:
                    transpose_weights(i - 2)
                if i >= 4:
                    output_product(i - 4)
                if i == NT:
                    pe.wait_ge(s["ssub"], NT)
                    transpose_norm(3, 0, 0)
                if i == NT + 1:
                    router(3, 1, 0, X1, "router_w")

            transpose_gates(1, 0)
            pe.wait_ge(s["combT_ready"], G + 1)
            pe.wait_ge(s["xlo_ready"], G + 1)
            pe.wait_ge(s["xhi_ready"], G + 1)

            def up1(n, e, q, k, first=False):
                p, g, c = place(k, first)
                pe.wait_ge(s["wsp1_ready"], 2 * (e + p) + 1)
                pe.wait_ge(s["gelu"], reached(n - 3))
                cs = slice(c * P, (c + 1) * P)
                if c == 0:
                    pe.wait_ge(s["cbx1"], before(q, first))
                    pick = sel1[:, e + p, :] if type(e) is int else sel1[:, bass.ds(e + p, 1), :].rearrange("p a m -> p (a m)")
                    mm(bank(6 + g), pick, combT[:, g, :], start=True, stop=True)
                mm(bank(k % 4), wsp[:, p, 0, cs], xhi[:, tok(g)], start=True, stop=False)
                mm(bank(k % 4), wsp[:, p, 0, cs], xlo[:, tok(g)], start=False, stop=False)
                mm(bank(k % 4), wsp[:, p, 1, cs], xhi[:, tok(g)], start=False, stop=True).then_inc(s["mm1b"], 1)

            def down1(n, e, q, k, first=False):
                p, g, c = place(k, first)
                cs = slice(N + c * P, N + (c + 1) * P)
                pe.wait_ge(s["wsp1_ready"], 2 * (e + p) + 2)
                pe.wait_ge(s["hlo1"], n + 1)
                if c == 0:
                    pe.wait_ge(s["ymul"], before(q, first))
                mm(bank(4 + g), wsp[:, p, 0, cs], hhi[:, k % 4, :], start=(c == 0), stop=False)
                mm(bank(4 + g), wsp[:, p, 0, cs], hlo[:, k % 4, :], start=False, stop=False)
                mm(bank(4 + g), wsp[:, p, 1, cs], hhi[:, k % 4, :], start=False, stop=(c == FC - 1)).then_inc(s["mm2b"], 1)

            def expert_pair(e, first=False, last=False):
                for k in range(16):
                    if first and k == 1:
                        pe.wait_ge(s["x_att"], NT)
                        transpose_norm(3, 1, 5)
                    if first and k == 3:
                        router(3, 1, 1, X1, "router_w")
                    if first and k == 5:
                        transpose_gates(1, 1)
                        pe.wait_ge(s["combT_ready"], 2 * G)
                        pe.wait_ge(s["xlo_ready"], 2 * G)
                    ahead = k + 3
                    if not (last and ahead >= 16):
                        up1(8 * e + ahead, e + 2 * (ahead // 16), 2 * e + ahead // 4, ahead, first)
                    down1(8 * e + k, e, 2 * e + k // 4, k, first)

            for k in range(3):
                up1(k, 0, 0, k, first=True)
            expert_pair(0, first=True)
            with pe.Fori(1, X1 // 2 - 1) as i:
                expert_pair(i * 2)
            expert_pair(X1 - 2, last=True)
            pe.wait_ge(s["yacc"], 2 * X1)
            for g in range(G):
                transpose_y(g, g, s["yTp1"])


def kernel(**inputs):
    import numpy as np
    import ml_dtypes
    import concourse.bacc as bacc
    from concourse.bass_utils import run_bass_kernel_spmd

    f = {k: np.asarray(v) for k, v in inputs.items()}
    f32 = np.float32
    x = f["x"].reshape(NB * S, E)
    ctx = f["ctx_1024"]
    pack = np.zeros((P, PACK_W), f32)

    def put(name, value):
        a, b = PACK[name]
        pack[:value.shape[0], a:b] = value.reshape(value.shape[0], b - a)

    wg = np.zeros((P, 3, 36), f32)
    gb = np.zeros((36, 1), f32)
    for c in range(3):
        wg[:, c, 0:H0] = f["L0_xattn_igate_w"][:, c * E:(c + 1) * E].T
        wg[:, c, 32:32 + H0] = f["L0_xattn_fgate_w"][:, c * E:(c + 1) * E].T
    gb[0:H0, 0] = f["L0_xattn_igate_b"]
    gb[32:32 + H0, 0] = f["L0_xattn_fgate_b"]
    put("ident", np.eye(P, dtype=f32))
    put("wg", wg)
    put("gb", gb)
    put("headmask", (np.arange(P)[:, None] % 32 // D1 == np.arange(4)[None, :]).astype(f32))
    put("bq", np.tile(f["L1_xattn_b_q"].reshape(4, E // 4).T, (4, 1)))
    put("bk", f["L1_xattn_b_k"][:, None])
    put("out_w", np.broadcast_to(f["L0_xattn_out_w"], (P, E)))
    put("bv", np.broadcast_to(f["L1_xattn_b_v"], (P, E)))
    put("bo", np.broadcast_to(f["L1_xattn_b_o"], (P, E)))
    put("gate_b", np.broadcast_to(f["L0_ffn_gate_b"], (P, X0)))
    put("gate_w", f["L0_ffn_gate_w"].T)
    put("router_w", f["L1_ffn_router_w"].T)

    rows = np.zeros((4, 2 * N + 4 * S), f32)
    starts = (np.arange(N) % S) == 0
    rows[:, 0:N] = ~starts
    rows[:, N:2 * N] = np.where(starts, LOWEST, 0.0)
    for h in range(H0):
        rows[h, 2 * N + h * S:2 * N + (h + 1) * S] = 1.0

    ctx_v = np.zeros((P, NB, 2, 66), f32)
    for hf in range(2):
        for pair in range(2):
            h = 2 * pair + hf
            ctx_v[hf * S:(hf + 1) * S, :, pair, hf * 33:hf * 33 + D0] = ctx[:, :, h * D0:(h + 1) * D0].transpose(1, 0, 2)
            ctx_v[hf * S:(hf + 1) * S, :, pair, hf * 33 + D0] = 1.0

    w_first = np.zeros((PAIRS, P, 3 * P), f32)
    w13, w2 = f["L0_ffn_w13"], f["L0_ffn_w2"]
    half = w13.shape[1] // 2
    experts = [(w13[e], w2[e]) for e in range(X0)] + [(f["L0_ffn_w13_s"], f["L0_ffn_w2_s"])]
    for e, (up, down) in enumerate(experts):
        j, c = e // 2, (e % 2) * half
        w_first[j, :, c:c + half] = up[0:half].T
        w_first[j, :, P + c:P + c + half] = up[half:].T
        w_first[j, c:c + half, 2 * P:] = down.T
    w_second = np.concatenate([f["L1_ffn_w1"].transpose(0, 2, 1),
                               f["L1_ffn_w2"].transpose(0, 2, 1).reshape(X1, FC, P, E).transpose(0, 2, 1, 3).reshape(X1, P, FC * E)], axis=2)
    qkvo = np.stack([f["L1_xattn_W_q"].T, f["L1_xattn_W_k"].T, f["L1_xattn_W_v"].T, f["L1_xattn_W_o"].T], axis=1)
    causal = np.where(np.arange(S)[None, :] > (np.arange(P) % S)[:, None], LOWEST, 0.0).astype(ml_dtypes.bfloat16)
    sel_first = np.zeros((P, PAIRS, P), np.float16)
    for e in range(X0 + 1):
        for r in (e, 32 + e):
            sel_first[r, e // 2, (e % 2) * half:(e % 2 + 1) * half] = 1.0
    sel_second = np.zeros((P, X1, P), np.float16)
    for e in range(X1):
        sel_second[[e, 32 + e], e, :] = 1.0

    arrays = {
        "x": x, "ctx_t": ctx.reshape(NB * S, E).T, "ctx_v": ctx_v, "pack": pack, "rows": rows, "w_first": w_first,
        "w_second": w_second, "qkvo": qkvo, "causal": causal, "ident_h": np.eye(P, dtype=np.float16),
        "ident_b": np.eye(P, dtype=ml_dtypes.bfloat16),
        "sel_first": sel_first, "sel_second": sel_second,
    }
    arrays = {k: np.ascontiguousarray(v) for k, v in arrays.items()}
    nc = bacc.Bacc("TRN2", target_bir_lowering=False, num_devices=1)
    args = {k: nc.dram_tensor(k, v.shape, mybir.dt.from_np(v.dtype), kind="ExternalInput").ap() for k, v in arrays.items()}
    out = nc.dram_tensor("out", (NB * S, E), F32, kind="ExternalOutput").ap()
    build_program(nc, out=out, **args)
    r = run_bass_kernel_spmd(nc, [arrays], core_ids=[0])
    return r.results[0]["out"].reshape(NB, S, E)
```

```python
import math
from contextlib import ExitStack

import concourse.bass as bass
from concourse import mybir

ALU = mybir.AluOpType
ACT = mybir.ActivationFunctionType
F32 = mybir.dt.float32
F16 = mybir.dt.float16
BF16 = mybir.dt.bfloat16
AX_X = mybir.AxisListType.X

P = 128
E = 128
S = 64
NB = 16
NT = NB * S // P
G = 2
TG = NT // G
N = TG * P
NQ = N // 2
NBG = NB // G
H0, D0 = 4, 32
H1, D1 = 16, 8
X0, TOP0 = 16, 4
PAIRS = X0 // 2 + 1
X1 = 8
FC = 4
XS = 256.0
HS = 16.0
AS = 64.0
VS = 64.0
PS = 1024.0
Q4 = NB * S // 4
LN_EPS = 1e-5
NORM_EPS = 1e-8
ROUTE_SCALE = 2.5
LOWEST = -1e30
PACK = {}
_at = 0
for _name, _w in (("ident", 128), ("wg", 3 * 2 * 32), ("gb", 2), ("headmask", 4), ("bq", 4), ("bk", 1),
                  ("out_w", 128), ("bv", 128), ("bo", 128), ("gate_b", 16), ("gate_w", 16), ("router_w", 8)):
    PACK[_name] = (_at, _at + _w)
    _at += _w
PACK_W = _at


def build_program(nc, x, ctx_t, ctx_v, pack, rows, w_first, w_second, qkvo, causal, ident_h, ident_b, sel_first, sel_second, out):
    with ExitStack() as stack:
        def sb(name, shape, dt=F32):
            return stack.enter_context(nc.sbuf_tensor(name, shape, dt))

        def sem(name):
            return stack.enter_context(nc.semaphore(name))

        ps = stack.enter_context(nc.psum_tensor("ps", [P, 8, 512], F32))

        def bank(n):
            return ps[:, n, :]

        xr = sb("xr", [P, NT, E])
        ctxT = sb("ctxT", [P, NB * S])
        pk = sb("pk", [P, PACK_W])
        rw = sb("rw", [P, 2 * NQ + H0 * P])
        wq = sb("wq", [P, 4, E])
        cz = sb("cz", [P, S], BF16)
        idh = sb("idh", [P, P], F16)
        idb = sb("idb", [P, P], BF16)
        sel0 = sb("sel0", [P, PAIRS, P], F16)
        sel1 = sb("sel1", [P, X1, P], F16)

        def pc(name, rows_=P):
            a, b = PACK[name]
            return pk[0:rows_, a:b]

        ident = pc("ident")
        reset_mul, reset_add = rw[:, 0:NQ], rw[:, NQ:2 * NQ]
        head_sel = rw[:, 2 * NQ:].rearrange("a (h s) -> a h s", h=H0)
        wgv = pc("wg").rearrange("p (c m) -> p c m", c=3)

        def shared(name, width):
            arena = sb(name, [P, width])
            at = [0, 0, 0]

            def take(life, shape, dt=F32):
                cols = 1
                for n in shape[1:]:
                    cols *= n
                cols = cols * (2 if dt == F16 else 4) // 4
                a = arena[0:shape[0], at[life]:at[life] + cols]
                at[life] += cols
                assert at[life] <= width, (name, at)
                if dt == F16:
                    a = a.bitcast(F16)
                if len(shape) > 2:
                    dims = " ".join(f"d{i}" for i in range(len(shape) - 1))
                    a = a.rearrange(f"p ({dims}) -> p {dims}", **{f"d{i}": n for i, n in enumerate(shape[1:])})
                return a
            return take

        kept = shared("keys_or_scores", 8 * NB * S)
        work = shared("attention_or_experts", 11328)

        stats = sb("stats", [P, NT, 6])
        mv = sb("mv", [P, NT, 2])
        ve = sb("ve", [P, NT])
        rstd = sb("rstd", [P, NT])
        minus_half = sb("minus_half", [P, 16])
        xn = sb("xn", [P, NT, E])
        xT = sb("xT", [P, NB * S])
        wgc = sb("wgc", [P, 2 * 32])
        ctxM = kept(0, [P, NB, H0, S])
        v0 = work(0, [P, NB, 2, 66])
        zrow = work(0, [P, NQ])
        lrow = work(0, [P, NQ])
        lf = zrow
        csum = work(0, [P, NQ])
        urow = work(0, [P, NQ])
        crow = urow
        nmrow = csum
        cmax = work(0, [P, NQ])
        enrow = work(0, [P, 2 * NQ])
        sttok = sb("sttok", [P, 2, G, TG, H0])
        decay = kept(0, [P, G, TG * H0 * S])
        cmat = kept(0, [P, G, TG * H0 * S])
        cT = work(0, [P, G, TG * 2 * P])
        den = sb("den", [P, G, TG * H0])
        rden = sb("rden", [P, G, TG * H0])
        vmean = sb("vmean", [P, NB * 2 * 2])
        ones_row = sb("ones_row", [1, S])
        hh = work(0, [P, G, TG * H0, D0])
        hy = sb("hy", [P, G, TG * H0])
        hq = sb("hq", [P, G, TG * H0])
        hsq = work(0, [P, G, TG * H0, D0])
        hsum = sb("hsum", [P, G, TG * H0])
        hve = sb("hve", [P, G, TG * H0])
        hrs = sb("hrs", [P, G, TG * H0])
        owp = sb("owp", [P, E])
        kT = sb("kT", [P, NB * S])
        khi = xhi = sb("xhi", [P, NB * S], F16)
        klo = xlo = sb("xlo", [P, NB * S], F16)
        kS = sb("kS", [P, 4, NB * S], F16)
        kM = sb("kM", [P, H1, NB * S], F16)
        wqr = sb("wqr", [P, 4, P])
        bks = sb("bks", [P, 1])
        v1 = sb("v1", [P, NB, 8, 18])
        bqs = sb("bqs", [P, 4])
        qS = kept(1, [P, 4, NB * S], F16)
        rmax = sb("rmax", [P, 2, H1])
        prob = work(2, [P, 2, H1 * S])
        phi = work(2, [P, 2, H1 * S], F16)
        plo = work(2, [P, 2, H1 * S], F16)
        pT = work(2, [P, 2, 2, H1 * S], F16)
        v1hi = sb("v1hi", [P, NB, 8, 18], F16)
        v1lo = sb("v1lo", [P, NB, 8, 18], F16)
        log_ps = sb("log_ps", [P, 1])
        idle = sb("idle", [P, N], F16)
        rs1 = sb("rs1", [P, H1])
        rs1b = sb("rs1b", [P, H1])
        o1 = sb("o1", [P, H1, D1])
        o1n = sb("o1n", [P, H1, D1])
        o1c = sb("o1c", [P, 2, E])
        oT = sb("oT", [P, P])
        rt = sb("rt", [P, G, 6, TG, X0])
        top = sb("top", [P, G, TG, 8])
        rsum = sb("rsum", [P, G, TG])
        rrec = sb("rrec", [P, G, TG])
        combt = sb("combt", [P, G, TG, P], F16)
        combT = sb("combT", [P, G, N], F16)
        raw = sb("raw", [P, 2, 2 * N])
        raws = kT
        wsp = sb("wsp", [P, 2, 2, 2 * N], F16)
        act = work(1, [P, 2, N])
        cb = work(1, [P, 2, N])
        h32 = work(1, [P, 4, N])
        gu = h32[:, 2:4, :]
        hhi = work(1, [P, 4, N], F16)
        hlo = work(1, [P, 4, N], F16)
        yT = work(1, [P, G, N])
        ytmp = work(1, [P, 2, N])

        names = """in_pack in_ctx in_rows in_v in_cz in_qkvo in_idh in_sel out_done
            ones_set idle_set var_ready rstd_ready xn_ready xnT_ready xT_ready
            wgc_ready ctxm_zero ctxm_ready kproj kT_ready khi_ready klo_ready kS_ready kM_ready wqr_ready vproj v1_zero v1hi_ready v1lo_ready bqs_ready
            rdiff gates z_ready az_ready ez_ready ln_ready c_ready cmax_ready cm_ready en_ready
            cbc stT sttok_ready dpre dexp s0 cmat_ready cTp cT_ready o0 hsq_ready h_var h_ln h_rstd vmean_ready v0_ready ones_ready v1_copied
            fill_chain stat_chain row_chain head_chain route_chain
            logits lexp comb_zero comb_ready combTp combT_ready xhi_ready xlo_ready
            raws_ready wsp_hi wsp_ready
            mm1 silu cbx tmul hmul hhi_r hlo_r mm2 yT_ready yTp
            qproj qhi_ready qS_ready s1 smax ssub phi_ready sexp plo_ready pTp pT_ready av den1 rec1 mul1 min1 o1_ready oTp oT_ready oproj x_att bn3
            raws1_ready wsp1_hi wsp1_ready mm1b gelu cbx1 hhi1 hlo1 mm2b ymul yacc acc_zero
            yTp1 x_out""".split()
        s = {n: sem(n) for n in names}

        def reached(count):
            return max(count, 0) if type(count) is int else count

        def chain(eng, own):
            count = [0]

            def link(ins):
                count[0] += 1
                ins.then_inc(own, 1)
                eng.wait_ge(own, count[0])
            return link

        in_x = [sem(f"in_x{g}") for g in range(G)]
        raw_ready = [sem(f"raw_ready{p}") for p in range(2)]
        raw1_ready = [sem(f"raw1_ready{p}") for p in range(2)]

        block = stack.enter_context(nc.Block())
        x_v = x.rearrange("(t p) e -> p t e", p=P)
        out_v = out.rearrange("(t p) e -> p t e", p=P)

        def qbank(c, jj):
            return (4, 5, 2, 3)[2 * c + jj] if c < 2 else 7

        def head_outputs(g):
            return ps[:, 4 * g:4 * g + 2, 0:2 * 132].rearrange("p b (th c) -> p b th c", c=33)

        def logit_bank(k, g):
            return 7 if k and g else 4 * g + 1

        def gate_bank(k, g):
            return 4 * g + 2 if (k, g) == (1, 0) else 6 + g

        def place(k, first):
            if first and k < 16:
                return k // 4 % 2, k // 8 % 2, k % FC
            return k // 8 % 2, k // 4 % 2, k % FC

        def before(q, first):
            if first and q < 4:
                return q if q % 2 else 0
            return reached(q - 1)

        def tok(g):
            return slice(g * N, (g + 1) * N)

        def gt(g):
            return slice(g * TG, (g + 1) * TG)

        @block.sync
        def _(sp):
            sp.dma_start(xr[:, gt(0), :], x_v[:, gt(0), :]).then_inc(in_x[0], 16)
            sp.dma_start(pk[:], pack).then_inc(s["in_pack"], 16)
            sp.dma_start(ctxT[:], ctx_t).then_inc(s["in_ctx"], 16)
            sp.dma_start(wq[:], qkvo).then_inc(s["in_qkvo"], 16)
            sp.dma_start(v0[:], ctx_v).then_inc(s["in_v"], 16)
            sp.dma_start(sel0[:], sel_first).then_inc(s["in_sel"], 16)
            sp.dma_start(sel1[:], sel_second).then_inc(s["in_sel"], 16)
            for j in range(2):
                sp.dma_start(raw[:, j, 0:3 * P], w_first[j, :, :]).then_inc(raw_ready[j], 16)
            sp.wait_ge(s["khi_ready"], 1)
            sp.wait_ge(s["klo_ready"], 1)
            for quad in range(4):
                for j in range(4):
                    sp.dma_start(kS[quad * 32:(quad + 1) * 32, j, :], (khi, klo)[quad % 2][j * 32:(j + 1) * 32, :])\
                        .then_inc(s["kS_ready"], 16)
            with sp.Fori(1, PAIRS // 2) as i:
                for p in range(2):
                    sp.wait_ge(s["wsp_ready"], i * 4 + 2 * (p - 1))
                    sp.dma_start(raw[:, p, 0:3 * P], w_first[bass.ds(i * 2 + p, 1), :, :]).then_inc(raw_ready[p], 16)
            sp.wait_ge(s["wsp_ready"], 2 * (PAIRS - 2))
            sp.dma_start(raw[:, 0, 0:3 * P], w_first[PAIRS - 1, :, :]).then_inc(raw_ready[0], 16)
            sp.wait_ge(s["wsp_ready"], 2 * PAIRS)
            for e in range(2):
                sp.dma_start(raw[:, e, :], w_second[e, :, :]).then_inc(raw1_ready[e], 16)
            with sp.Fori(1, X1 // 2) as i:
                for p in range(2):
                    sp.wait_ge(s["wsp1_ready"], i * 4 + 2 * (p - 1))
                    sp.dma_start(raw[:, p, :], w_second[bass.ds(i * 2 + p, 1), :, :]).then_inc(raw1_ready[p], 16)
            for g in range(G):
                sp.wait_ge(s["x_out"], g + 1)
                sp.dma_start(out_v[:, gt(g), :], xr[:, gt(g), :]).then_inc(s["out_done"], 16)
            sp.wait_ge(s["out_done"], 16 * G)

        @block.gpsimd
        def _(pool):
            fill = chain(pool, s["fill_chain"])
            def rsqrt(l, g):
                pool.wait_ge(s["var_ready"], l * G + g + 1)
                pool.tensor_tensor(rstd[:, gt(g)], ve[:, gt(g)], minus_half[:, 0:TG], ALU.pow).then_inc(s["rstd_ready"], 1)

            def key_mask(h):
                pool.tensor_scalar(kM[:, h, :], kS[:, h // 4, :], pc("headmask")[:, h % 4:h % 4 + 1], 1.0, ALU.mult, ALU.mult)\
                    .then_inc(s["kM_ready"], 1)

            fill(pool.memset(minus_half[:], -0.5))
            for g in range(G):
                rsqrt(0, g)
            pool.wait_ge(s["rstd_ready"], G)
            pool.memset(log_ps[:], math.log(PS))
            pool.memset(ones_row[:], 1.0).then_inc(s["ones_ready"], 1)
            fill(pool.memset(combt[:], 0.0))
            pool.memset(combt[:, :, :, X0:X0 + 1], XS).then_inc(s["comb_zero"], 1)
            pool.memset(ctxM[:], 0.0).then_inc(s["ctxm_zero"], 1)
            fill(pool.memset(v1[:], 0.0))
            pool.memset(v1[0:S, :, :, 8:9], VS)
            pool.memset(v1[S:P, :, :, 17:18], VS).then_inc(s["v1_zero"], 1)
            pool.wait_ge(s["v1_zero"], 1)

            pool.wait_ge(s["in_ctx"], 16)
            pool.wait_ge(s["ctxm_zero"], 1)
            for h in range(H0):
                q = slice(h * D0, (h + 1) * D0)
                pool.tensor_scalar(ctxM[q, :, h, :], ctxT[q, :].rearrange("p (b s) -> p b s", s=S), D0 ** -0.5, 1.0,
                                   ALU.mult, ALU.mult).then_inc(s["ctxm_ready"], 1)
                pool.wait_ge(s["ctxm_ready"], h + 1)
            pool.wait_ge(s["kT_ready"], G)
            pool.tensor_scalar(khi[:], kT[:], 1.0, 1.0, ALU.mult, ALU.mult).then_inc(s["khi_ready"], 1)
            pool.wait_ge(s["khi_ready"], 1)
            pool.tensor_tensor(klo[:], kT[:], khi[:], ALU.subtract).then_inc(s["klo_ready"], 1)
            pool.wait_ge(s["in_qkvo"], 16)
            pool.tensor_scalar(wqr[:].rearrange("p j (r f) -> p j r f", f=32),
                               wq[:, 0, :].rearrange("p (j f) -> p j f", f=32).unsqueeze(2).to_broadcast([P, 4, 4, 32]),
                               AS, 1.0, ALU.mult, ALU.mult).then_inc(s["wqr_ready"], 1)
            pool.wait_ge(s["vmean_ready"], 1)
            v0g = v0[:].rearrange("p b c (h d) -> p (b c h) d", h=2)[:, :, 0:D0]
            pool.tensor_tensor(v0g, v0g, vmean[:].unsqueeze(2).to_broadcast([P, NB * 4, D0]), ALU.subtract).then_inc(s["v0_ready"], 1)
            pool.wait_ge(s["kS_ready"], 16 * 16)
            for h in range(7):
                key_mask(h)
            rsqrt(1, 0)
            for h in range(7, 10):
                key_mask(h)
            rsqrt(1, 1)

            def split_pair(j, p, arrivals):
                for q in range(2):
                    c = slice(0, 2 * P) if q == 0 else slice(2 * P, 3 * P)
                    n = 2 * j + q
                    pool.wait_ge(raw_ready[p], arrivals)
                    pool.wait_ge(s["wsp_ready"], n)
                    pool.tensor_scalar(raws[:, c], raw[:, p, c], XS, 1.0, ALU.mult, ALU.mult).then_inc(s["raws_ready"], 1)
                    pool.wait_ge((s["mm1"], s["mm2"])[q], reached(2 * j - 2))
                    pool.tensor_scalar(wsp[:, p, 0, c], raw[:, p, c], XS, 1.0, ALU.mult, ALU.mult).then_inc(s["wsp_hi"], 1)
                    pool.wait_ge(s["raws_ready"], n + 1)
                    pool.wait_ge(s["wsp_hi"], n + 1)
                    pool.tensor_tensor(wsp[:, p, 1, c], raws[:, c], wsp[:, p, 0, c], ALU.subtract).then_inc(s["wsp_ready"], 1)

            split_pair(0, 0, 16)
            split_pair(1, 1, 16)
            pool.wait_ge(s["v1hi_ready"], 1)
            pool.tensor_tensor(v1lo[:], v1[:], v1hi[:], ALU.subtract).then_inc(s["v1lo_ready"], 1)
            for j in range(2, PAIRS):
                split_pair(j, j % 2, 16 * (j // 2 + 1))
                if j in (3, 4, 5, 6, 7):
                    key_mask(7 + j)
            key_mask(H1 - 1)
            for g in range(G):
                rsqrt(2, g)

            def split_expert(e, p, arrivals):
                pool.wait_ge(raw1_ready[p], arrivals)
                for q in range(2):
                    c = slice(q * N, (q + 1) * N)
                    n = 2 * e + q
                    pool.wait_ge(s["wsp1_ready"], n)
                    pool.tensor_scalar(raws[:, c], raw[:, p, c], XS, 1.0, ALU.mult, ALU.mult).then_inc(s["raws1_ready"], 1)
                    pool.wait_ge((s["mm1b"], s["mm2b"])[q], 12 if e == 2 else reached(8 * e - 8))
                    pool.tensor_scalar(wsp[:, p, 0, c], raw[:, p, c], XS, 1.0, ALU.mult, ALU.mult).then_inc(s["wsp1_hi"], 1)
                    pool.wait_ge(s["raws1_ready"], n + 1)
                    pool.wait_ge(s["wsp1_hi"], n + 1)
                    pool.tensor_tensor(wsp[:, p, 1, c], raws[:, c], wsp[:, p, 0, c], ALU.subtract).then_inc(s["wsp1_ready"], 1)

            pool.wait_ge(s["mm2"], 2 * PAIRS)
            split_expert(0, 0, 16)
            split_expert(1, 1, 16)
            for t in range(NT):
                pool.wait_ge(s["sexp"], t + 1)
                pool.wait_ge(s["pTp"], reached(2 * t - 2))
                pool.tensor_tensor(plo[:, t % 2, :], prob[:, t % 2, :], phi[:, t % 2, :], ALU.subtract).then_inc(s["plo_ready"], 1)
                if t == NT - 2:
                    rsqrt(3, 0)
            rsqrt(3, 1)

            def accumulate(n, g):
                pool.wait_ge(s["ymul"], n + 1)
                pool.wait_ge(s["yacc"], n)
                pool.tensor_tensor(yT[:, g, :], yT[:, g, :], ytmp[:, g, :], ALU.add).then_inc(s["yacc"], 1)

            pool.wait_ge(s["yTp"], G)
            pool.memset(yT[:], 0.0).then_inc(s["acc_zero"], 1)
            pool.wait_ge(s["acc_zero"], 1)
            accumulate(0, 0)
            for e in range(2, X1):
                split_expert(e, e % 2, 16 * (e // 2 + 1))
                for n in (2 * e - 3, 2 * e - 2):
                    accumulate(n, n // 2 % 2 if n < 4 else n % 2)
            for n in range(2 * X1 - 3, 2 * X1):
                accumulate(n, n % 2)

        @block.scalar
        def _(a):
            a.dma_start(xr[:, gt(1), :], x_v[:, gt(1), :]).then_inc(in_x[1], 16)
            a.dma_start(rw[:], rows).then_inc(s["in_rows"], 16)
            a.dma_start(cz[:], causal).then_inc(s["in_cz"], 16)
            a.dma_start(idh[:], ident_h).then_inc(s["in_idh"], 16)
            a.dma_start(idb[:], ident_b).then_inc(s["in_idh"], 16)
            a.preload_act_table_set("natural_log_exp_and_others")

            def copy_xT(l, g, b):
                a.wait_ge(s["xnT_ready"], l * G + g + 1)
                a.activation(xT[:, tok(g)], bank(b), ACT.Copy).then_inc(s["xT_ready"], 1)

            for g in range(G):
                copy_xT(0, g, 4 * g)
            a.wait_ge(s["z_ready"], 1)
            a.activation(lrow, zrow, ACT.Abs).then_inc(s["az_ready"], 1)
            a.wait_ge(s["az_ready"], 1)
            a.activation(lrow, lrow, ACT.Exp, scale=-1.0).then_inc(s["ez_ready"], 1)
            a.wait_ge(s["ez_ready"], 1)
            a.activation(lrow, lrow, ACT.Ln, bias=1.0).then_inc(s["ln_ready"], 1)
            for g in range(G):
                a.wait_ge(s["kproj"], g + 1)
                a.wait_ge(s["bqs_ready"], 1)
                a.activation(kT[:, tok(g)], bank(6 + g), ACT.Identity, bias=bks[:], scale=AS).then_inc(s["kT_ready"], 1)
            a.wait_ge(s["cm_ready"], 1)
            a.activation(enrow.rearrange("p (t f c) -> p t f c", t=TG, f=2),
                         nmrow.rearrange("p (t c) -> p t c", t=TG).unsqueeze(2).to_broadcast([P, TG, 2, S]), ACT.Exp, scale=-1.0).then_inc(s["en_ready"], 1)
            for g in range(G):
                a.wait_ge(s["dpre"], g + 1)
                a.activation(decay[:, g, :], decay[:, g, :], ACT.Exp).then_inc(s["dexp"], 1)
            for g in range(G):
                a.wait_ge(s["cTp"], g + 1)
                a.activation(cT[:, g, :], ps[:, 4 * g + 2:4 * g + 4, :], ACT.Copy).then_inc(s["cT_ready"], 1)
            for g in range(G):
                a.wait_ge(s["o0"], g + 1)
                a.activation(hsq[:, g, :, :].rearrange("p (b th) d -> p b th d", b=2), head_outputs(g)[:, :, :, 0:D0],
                             ACT.Square)
                a.activation(den[:, g, :].rearrange("p (b th) -> p b th", b=2).unsqueeze(3), head_outputs(g)[:, :, :, D0:],
                             ACT.Abs).then_inc(s["hsq_ready"], 1)
            for g in range(G):
                a.wait_ge(s["h_var"], g + 1)
                a.activation(hy[:, g, :], hve[:, g, :], ACT.Ln).then_inc(s["h_ln"], 1)
                a.wait_ge(s["h_ln"], g + 1)
                a.activation(hy[:, g, :], hy[:, g, :], ACT.Exp, scale=-0.5).then_inc(s["h_rstd"], 1)
            a.wait_ge(s["v1_zero"], 1)
            for c in range(4):
                a.wait_ge(s["vproj"], c + 1)
                src = bank((2, 3, 6, 7)[c]).rearrange("p (b c d) -> p b c d", b=4, d=16)
                for hf in range(2):
                    q = slice(hf * S, (hf + 1) * S)
                    last = a.activation(v1[q, 4 * c:4 * c + 4, :, 9 * hf:9 * hf + 8], src[q, :, :, 8 * hf:8 * hf + 8],
                                        ACT.Copy, scale=VS)
                last.then_inc(s["v1_copied"], 1)
            a.wait_ge(s["v1_copied"], 4)
            a.activation(v1hi[:], v1[:], ACT.Copy).then_inc(s["v1hi_ready"], 1)

            def split_x(l, k, g, b):
                copy_xT(l, g, b)
                a.wait_ge(s["kS_ready"], 16 * 16)
                a.activation(xhi[:, tok(g)], bank(b), ACT.Copy, scale=XS).then_inc(s["xhi_ready"], 1)

            for g in range(G):
                split_x(1, 0, g, 4 * g)
            for g in range(G):
                a.wait_ge(s["logits"], g + 1)
                a.activation(rt[:, g, 0, :, :], bank(logit_bank(0, g))[:, 0:TG * X0].rearrange("p (t x) -> p t x", x=X0),
                             ACT.Exp, scale=-1.0).then_inc(s["lexp"], 1)
            def copy_gates(k, g):
                a.wait_ge(s["combTp"], k * G + g + 1)
                a.activation(combT[:, g, :], bank(gate_bank(k, g))[:, 0:N // 2].bitcast(F16), ACT.Copy).then_inc(s["combT_ready"], 1)

            a.preload_act_table_set("silu_and_others")
            for g in range(G):
                copy_gates(0, g)

            def silu_step(n, k):
                a.wait_ge(s["mm1"], n + 1)
                a.wait_ge(s["tmul"], reached(n - 1))
                a.activation(act[:, k, :], bank(k), ACT.Silu, scale=1 / (XS * XS)).then_inc(s["silu"], 1)

            def gate_step(n, k):
                a.wait_ge(s["hmul"], reached(n - 1))
                a.activation(cb[:, k, :], bank(4 + k), ACT.Copy, scale=HS / (XS * XS * XS)).then_inc(s["cbx"], 1)

            def high_step(n, k):
                a.wait_ge(s["hmul"], n + 1)
                a.wait_ge(s["mm2"], reached(n - 1))
                a.activation(hhi[:, k, :], h32[:, k, :], ACT.Copy).then_inc(s["hhi_r"], 1)

            def ffn0_step(n, k, last=False):
                if not last:
                    silu_step(n + 1, (k + 1) % 2)
                high_step(n, k)
                if not last:
                    gate_step(n + 1, (k + 1) % 2)

            silu_step(0, 0)
            gate_step(0, 0)
            for n in range(4):
                ffn0_step(n, n % 2)
            with a.Fori(4, 4 * (PAIRS // 2), 4) as n:
                for k in range(4):
                    ffn0_step(n + k, k % 2)
            n0 = 2 * (PAIRS - 1)
            ffn0_step(n0, 0)
            ffn0_step(n0 + 1, 1, last=True)
            for g in range(G):
                a.wait_ge(s["mm2"], reached(2 * PAIRS - 1 + g))
                a.activation(yT[:, g, :], bank(6 + g), ACT.Copy, scale=1 / (XS * HS)).then_inc(s["yT_ready"], 1)

            a.preload_act_table_set("exp_and_others")
            copy_xT(2, 0, 7)

            def query_high(c, jj):
                a.wait_ge(s["qproj"], 2 * c + jj + 1)
                for j in range(2 * jj, 2 * jj + 2):
                    a.activation(qS[:, j, c * Q4:(c + 1) * Q4], bank(qbank(c, jj))[:, (j % 2) * Q4:(j % 2 + 1) * Q4],
                                 ACT.Identity, bias=bqs[:, j:j + 1]).then_inc(s["qhi_ready"], 1)

            for jj in range(2):
                query_high(0, jj)
            copy_xT(2, 1, 6)
            for jj in range(2):
                query_high(1, jj)

            def copy_oT(t):
                a.wait_ge(s["oTp"], t + 1)
                a.wait_ge(s["oproj"], reached(t))
                a.activation(oT[:], bank(7)[:, 0:P], ACT.Copy).then_inc(s["oT_ready"], 1)

            def exp_scores(t):
                a.wait_ge(s["ssub"], t + 1)
                a.wait_ge(s["pTp"], reached(2 * t - 2))
                a.activation(phi[:, t % 2, :], prob[:, t % 2, :], ACT.Exp, bias=log_ps[:], scale=D1 ** -0.5 / (AS * AS))\
                    .then_inc(s["phi_ready"], 1)
                a.wait_ge(s["phi_ready"], t + 1)
                a.activation(prob[:, t % 2, :], prob[:, t % 2, :], ACT.Exp, bias=log_ps[:], scale=D1 ** -0.5 / (AS * AS))\
                    .then_inc(s["sexp"], 1)

            def gate_tanh(g):
                a.wait_ge(s["rdiff"], g + 1)
                a.activation(rt[:, g, 1, :, 0:X1], rt[:, g, 0, :, 0:X1], ACT.Tanh).then_inc(s["lexp"], 1)

            def copy_pT(t):
                for part in range(2):
                    a.wait_ge(s["pTp"], 2 * t + part + 1)
                    a.wait_ge(s["av"], reached(t - 1))
                    a.activation(pT[:, t % 2, part, :].bitcast(F32), bank(4 + part), ACT.Copy).then_inc(s["pT_ready"], 1)

            for i in range(NT + 4):
                if i < 4:
                    query_high(2 + i // 2, i % 2)
                if i >= 4:
                    copy_oT(i - 4)
                if 2 <= i < NT + 2:
                    copy_pT(i - 2)
                if i < NT:
                    exp_scores(i)
                if i == NT:
                    split_x(3, 1, 0, 0)
                if i == NT + 1:
                    a.preload_act_table_set("gelu_and_others")
                    gate_tanh(0)
                if i == NT + 2:
                    copy_gates(1, 0)

            def gelu_step(n, q, k, first=False):
                a.wait_ge(s["mm1b"], n + 1)
                a.wait_ge(s["hlo1"], reached(n - 3))
                a.activation(h32[:, k % 4, :], bank(k % 4), ACT.Gelu, scale=1 / (XS * XS)).then_inc(s["gelu"], 1)
                if k % FC == 0 and not (first and k < 16):
                    copy_gate(q, k)

            def copy_gate(q, k, first=False):
                g = place(k, first)[1]
                a.wait_ge(s["ymul"], before(q, first))
                a.activation(cb[:, g, :], bank(6 + g), ACT.Copy, scale=1 / (XS * XS * HS)).then_inc(s["cbx1"], 1)

            def high1_step(n, k):
                a.wait_ge(s["gelu"], n + 1)
                a.wait_ge(s["mm2b"], reached(n - 3))
                a.activation(hhi[:, k % 4, :], h32[:, k % 4, :], ACT.Copy, scale=HS).then_inc(s["hhi1"], 1)

            def expert_pair(base, q0, first=False, last=False):
                for k in range(16):
                    if first and k == 1:
                        split_x(3, 1, 1, 5)
                    if first and k == 4:
                        gate_tanh(1)
                    if first and k == 5:
                        copy_gates(1, 1)
                    if not (last and k == 15):
                        gelu_step(base + (k + 1), q0 + (k + 1) // FC, k + 1, first)
                    high1_step(base + k, k)
                    if first and k % FC == 0:
                        copy_gate(k // FC, k, first)

            gelu_step(0, 0, 0, first=True)
            expert_pair(0, 0, first=True)
            with a.Fori(1, 3) as i:
                expert_pair(i * 16, i * 4)
            expert_pair(48, 12, last=True)

        @block.vector
        def _(v):
            stat = chain(v, s["stat_chain"])
            row = chain(v, s["row_chain"])
            head = chain(v, s["head_chain"])
            route = chain(v, s["route_chain"])

            def ln_stats(l, g):
                for t in range(g * TG, (g + 1) * TG):
                    last = v.bn_stats(stats[:, t, :], xr[:, t, :])
                stat(last)
                ln_variance(l, g)

            def ln_variance(l, g):
                for t in range(g * TG, (g + 1) * TG):
                    last = v.bn_aggr(mv[:, t, :], stats[:, t, :])
                stat(last)
                if l:
                    v.wait_ge(s["rstd_ready"], l * G)
                v.tensor_scalar(ve[:, gt(g)], mv[:, gt(g), 1], LN_EPS, None, ALU.add).then_inc(s["var_ready"], 1)

            def ln_apply(l, g):
                v.wait_ge(s["rstd_ready"], l * G + g + 1)
                if l:
                    v.wait_ge(s["xnT_ready"], l * G)
                for t in range(g * TG, (g + 1) * TG):
                    last = v.tensor_scalar(xn[:, t, :], xr[:, t, :], mv[:, t, 0:1], rstd[:, t:t + 1],
                                           ALU.subtract, ALU.mult)
                last.then_inc(s["xn_ready"], 1)

            v.memset(idle[:], 0.0).then_inc(s["idle_set"], 1)
            for g in range(G):
                v.wait_ge(in_x[g], 16)
                ln_stats(0, g)
            v.wait_ge(s["in_pack"], 16)
            v.tensor_tensor(wgc[:], wgv[:, 1, :], wgv[:, 2, :], ALU.add).then_inc(s["wgc_ready"], 1)
            v.tensor_scalar(bks[:], pc("bk"), AS, None, ALU.mult)
            v.tensor_scalar(bqs[:], pc("bq"), AS, None, ALU.mult).then_inc(s["bqs_ready"], 1)
            v.tensor_scalar(owp[:], pc("out_w"), 1.0, None, ALU.add)
            for g in range(G):
                ln_apply(0, g)
            v.wait_ge(s["in_v"], 16)
            stat(v.tensor_reduce(vmean[:], v0[:].rearrange("p b c (h d) -> p (b c h) d", h=2)[:, :, 0:D0], AX_X, ALU.add))
            v.tensor_scalar(vmean[:], vmean[:], 1 / D0, None, ALU.mult).then_inc(s["vmean_ready"], 1)
            ig_bias, fg_bias = (pk[:, PACK["gb"][0] + i:PACK["gb"][0] + i + 1] for i in range(2))
            v.wait_ge(s["gates"], G)
            v.tensor_scalar(zrow, bank(5)[:, 0:NQ], fg_bias, None, ALU.add).then_inc(s["z_ready"], 1)
            v.wait_ge(s["in_rows"], 16)
            v.wait_ge(s["ln_ready"], 1)
            row(v.scalar_tensor_tensor(lf, zrow, 0.0, lrow, ALU.min, ALU.subtract))
            row(v.tensor_tensor_scan(csum, reset_mul, lf, 0.0, ALU.mult, ALU.add))
            row(v.scalar_tensor_tensor(urow, bank(1)[:, 0:NQ], ig_bias, lf, ALU.add, ALU.add))
            v.tensor_tensor(crow, urow, csum, ALU.subtract).then_inc(s["c_ready"], 1)
            v.wait_ge(s["c_ready"], 1)
            v.tensor_tensor_scan(cmax, reset_add, crow, 0.0, ALU.add, ALU.max).then_inc(s["cmax_ready"], 1)
            v.wait_ge(s["cmax_ready"], 1)
            v.tensor_tensor(nmrow, csum, cmax, ALU.add).then_inc(s["cm_ready"], 1)
            def copy_rows(i):
                v.wait_ge(s["stT"], i + 1)
                for hf in range(2):
                    q = slice(hf * S, (hf + 1) * S)
                    src = bank(4 * i)[q, :].rearrange("p (t g f r) -> p g t f r", g=G, f=2, r=32)[:, :, :, hf, 0:H0]
                    last = v.tensor_copy(sttok[q, i, :, :, :], src) if i == 0 else \
                        v.tensor_scalar(sttok[q, i, :, :, :], src, NORM_EPS, None, ALU.add)
                last.then_inc(s["sttok_ready"], 1)
            for g in range(G):
                copy_rows(g)
                v.wait_ge(s["sttok_ready"], g + 1)
                v.wait_ge(s["cbc"], g + 1)
                dv = decay[:, g, :].rearrange("p (t h k) -> p h t k", t=TG, h=H0)
                cv = ps[:, 4 * g + 2:4 * g + 4, :].rearrange("p b (h t k) -> p (b h) t k", t=TG, k=S)
                for h in range(H0):
                    mxv = sttok[:, 0, g, :, h:h + 1].to_broadcast([P, TG, S])
                    last = v.tensor_tensor(dv[:, h, :, :], cv[:, h, :, :], mxv, ALU.subtract)
                last.then_inc(s["dpre"], 1)
            for g in range(G):
                v.wait_ge(s["s0"], g + 1)
                v.wait_ge(s["dexp"], g + 1)
                v.tensor_tensor(cmat[:, g, :], ps[:, 4 * g:4 * g + 2, :].rearrange("p b c -> p (b c)"), decay[:, g, :],
                                ALU.mult).then_inc(s["cmat_ready"], 1)
            for g in range(G):
                v.wait_ge(s["hsq_ready"], g + 1)
                head(v.scalar_tensor_tensor(den[:, g, :].rearrange("p (t h) -> p t h", h=H0),
                                            den[:, g, :].rearrange("p (t h) -> p t h", h=H0), NORM_EPS,
                                            sttok[:, 1, g, :, :], ALU.add, ALU.max))
                head(v.reciprocal(rden[:, g, :], den[:, g, :]))
                v.tensor_tensor(hq[:, g, :], rden[:, g, :], rden[:, g, :], ALU.mult)
                head(v.tensor_reduce(hsum[:, g, :], hsq[:, g, :, :], AX_X, ALU.add))
                head(v.scalar_tensor_tensor(hve[:, g, :], hsum[:, g, :], 1 / D0, hq[:, g, :], ALU.mult, ALU.mult))
                v.tensor_scalar(hve[:, g, :], hve[:, g, :], LN_EPS, None, ALU.add).then_inc(s["h_var"], 1)
            for g in range(G):
                y = hy[:, g, :]
                v.wait_ge(s["h_rstd"], g + 1)
                head(v.tensor_tensor(hq[:, g, :], y, y, ALU.mult))
                head(v.scalar_tensor_tensor(hq[:, g, :], hq[:, g, :], -0.5, hve[:, g, :], ALU.mult, ALU.mult))
                head(v.scalar_tensor_tensor(hrs[:, g, :], hq[:, g, :], 1.5, y, ALU.add, ALU.mult))
                head(v.tensor_tensor(hrs[:, g, :], hrs[:, g, :], rden[:, g, :], ALU.mult))
                head(v.tensor_tensor(hh[:, g, :, :].rearrange("p (b th) d -> p b th d", b=2), head_outputs(g)[:, :, :, 0:D0],
                                     hrs[:, g, :].rearrange("p (b th) -> p b th", b=2).unsqueeze(3)
                                     .to_broadcast([P, 2, 8, D0]), ALU.mult))
                h4 = hh[:, g, :, :].rearrange("p (t h) d -> p t (h d)", h=H0)
                head(v.tensor_tensor(h4, h4, owp[:].unsqueeze(1).to_broadcast([P, TG, E]), ALU.mult))
                head(v.tensor_tensor(xr[:, gt(g), :], xr[:, gt(g), :], h4, ALU.add))
                if g:
                    ln_apply(1, 0)
                ln_stats(1, g)

            def low_x(l, k, g, b):
                v.wait_ge(s["xhi_ready"], k * G + g + 1)
                v.wait_ge(s["kS_ready"], 16 * 16)
                v.scalar_tensor_tensor(xlo[:, tok(g)], bank(b), XS, xhi[:, tok(g)], ALU.mult, ALU.subtract)\
                    .then_inc(s["xlo_ready"], 1)

            ln_apply(1, 1)
            for g in range(G):
                low_x(1, 0, g, 4 * g)
            v.wait_ge(s["comb_zero"], 1)
            v.wait_ge(s["lexp"], G)
            r = rt[:].rearrange("p g i t x -> p i g t x")
            gbias = pc("gate_b").unsqueeze(1).unsqueeze(1).to_broadcast([P, G, TG, X0])
            route(v.tensor_scalar(r[:, 0], r[:, 0], 1.0, None, ALU.add))
            route(v.reciprocal(r[:, 1], r[:, 0]))
            route(v.tensor_tensor(r[:, 2], r[:, 1], gbias, ALU.add))
            for g in range(G):
                for t in range(TG):
                    last = v.max(top[:, g, t, :], rt[:, g, 2, t, :])
            route(last)
            route(v.memset(top[:, :, :, TOP0:], 3 * LOWEST))
            for g in range(G):
                for t in range(TG):
                    last = v.match_replace(rt[:, g, 3, t, :], top[:, g, t, :], rt[:, g, 2, t, :], LOWEST)
            route(last)
            route(v.tensor_scalar(r[:, 4], r[:, 3], LOWEST / 2, None, ALU.is_lt))
            route(v.tensor_tensor(r[:, 4], r[:, 4], r[:, 1], ALU.mult))
            route(v.tensor_reduce(rsum[:], r[:, 4], AX_X, ALU.add))
            route(v.reciprocal(rrec[:], rsum[:]))
            route(v.tensor_scalar(rrec[:], rrec[:], ROUTE_SCALE * XS, None, ALU.mult))
            route(v.tensor_tensor(r[:, 5], r[:, 4], rrec[:].unsqueeze(3).to_broadcast([P, G, TG, X0]), ALU.mult))
            route(v.tensor_copy(combt[:, :, :, 0:X0], r[:, 5]))
            v.tensor_tensor(combt[:, :, :, 32:32 + X0], r[:, 5], combt[:, :, :, 0:X0], ALU.subtract)\
                .then_inc(s["comb_ready"], G)

            def mul_step(n, k):
                v.wait_ge(s["silu"], n + 1)
                v.tensor_tensor(gu[:, k, :], act[:, k, :], bank(2 + k), ALU.mult).then_inc(s["tmul"], 1)

            def gate_step(n, k):
                v.wait_ge(s["cbx"], n + 1)
                v.wait_ge(s["tmul"], n + 1)
                v.wait_ge(s["hhi_r"], reached(n - 1))
                v.tensor_tensor(h32[:, k, :], gu[:, k, :], cb[:, k, :], ALU.mult).then_inc(s["hmul"], 1)

            def low_step(n, k):
                v.wait_ge(s["hhi_r"], n + 1)
                v.wait_ge(s["mm2"], reached(n - 1))
                v.tensor_tensor(hlo[:, k, :], h32[:, k, :], hhi[:, k, :], ALU.subtract).then_inc(s["hlo_r"], 1)

            def ffn0_step(n, k, last=False):
                if not last:
                    mul_step(n + 1, (k + 1) % 2)
                low_step(n, k)
                if not last:
                    gate_step(n + 1, (k + 1) % 2)

            mul_step(0, 0)
            gate_step(0, 0)
            for n in range(4):
                ffn0_step(n, n % 2)
            with v.Fori(4, 4 * (PAIRS // 2), 4) as n:
                for k in range(4):
                    ffn0_step(n + k, k % 2)
            n0 = 2 * (PAIRS - 1)
            ffn0_step(n0, 0)
            ffn0_step(n0 + 1, 1, last=True)

            def add_y(g, b):
                v.wait_ge(s["yTp"], g + 1)
                stat(v.tensor_tensor(xr[:, gt(g), :], xr[:, gt(g), :], bank(b).rearrange("p (t e) -> p t e", e=E), ALU.add))

            add_y(0, 0)
            ln_stats(2, 0)
            add_y(1, 1)
            ln_apply(2, 0)
            ln_stats(2, 1)

            def add_output_bias(g):
                v.wait_ge(s["xn_ready"], 2 * G + g + 1)
                stat(v.tensor_tensor(xr[:, gt(g), :], xr[:, gt(g), :], pc("bo").unsqueeze(1).to_broadcast([P, TG, E]), ALU.add))

            def scores_of(t):
                return ps[:, 2 * (t % 2):2 * (t % 2) + 2, :].rearrange("p b (h k) -> p (b h) k", k=S)

            def largest(t):
                v.wait_ge(s["s1"], t + 1)
                v.tensor_reduce(rmax[:, t % 2, :], scores_of(t), AX_X, ALU.max).then_inc(s["smax"], 1)

            def subtract_largest(t):
                v.wait_ge(s["smax"], t + 1)
                v.wait_ge(s["plo_ready"], reached(t - 1))
                v.tensor_tensor(prob[:, t % 2, :].rearrange("p (h k) -> p h k", k=S), scores_of(t),
                                rmax[:, t % 2, :].unsqueeze(2).to_broadcast([P, H1, S]), ALU.subtract).then_inc(s["ssub"], 1)


            def query_low(c, jj):
                v.wait_ge(s["qhi_ready"], 4 * c + 2 * jj + 2)
                for j in range(2 * jj, 2 * jj + 2):
                    q = qS[S:P, j, c * Q4:(c + 1) * Q4]
                    v.scalar_tensor_tensor(q, bank(qbank(c, jj))[S:P, (j % 2) * Q4:(j % 2 + 1) * Q4], bqs[S:P, j:j + 1], q,
                                           ALU.add, ALU.subtract).then_inc(s["qS_ready"], 1)

            ln_apply(2, 1)
            for jj in range(2):
                query_low(0, jj)

            halves = [(slice(hf * S, (hf + 1) * S), bank(6)[hf * S:(hf + 1) * S, 0:8 * 36]
                       .rearrange("p (c b d e) -> p c b d e", b=2, d=2, e=9)[:, :, hf, :, :]) for hf in range(2)]

            def sums_of_weights(t):
                v.wait_ge(s["av"], t + 1)
                for q, ov in halves:
                    last = v.tensor_scalar(rs1[q, :].rearrange("p (c d) -> p c d", d=2).unsqueeze(3), ov[:, :, :, 8:9],
                                           0.5 * PS * VS, None, ALU.max)
                last.then_inc(s["den1"], 1)

            def invert_sums(t):
                v.wait_ge(s["den1"], t + 1)
                v.reciprocal(rs1b[:], rs1[:]).then_inc(s["rec1"], 1)

            def divide(t):
                v.wait_ge(s["rec1"], t + 1)
                for q, ov in halves:
                    last = v.tensor_tensor(o1[q, :, :].rearrange("p (c d) e -> p c d e", d=2), ov[:, :, :, 0:8],
                                           rs1b[q, :].rearrange("p (c d) -> p c d", d=2).unsqueeze(3)
                                           .to_broadcast([S, 8, 2, D1]), ALU.mult)
                last.then_inc(s["mul1"], 1)

            def negative_part(t):
                v.wait_ge(s["mul1"], t + 1)
                v.tensor_scalar(o1n[:], o1[:], 0.0, None, ALU.min).then_inc(s["min1"], 1)

            def numbers_only(t):
                v.wait_ge(s["min1"], t + 1)
                v.wait_ge(s["oTp"], reached(t - 1))
                v.scalar_tensor_tensor(o1c[:, t % 2, :], o1[:].rearrange("p h d -> p (h d)"), 0.0,
                                       o1n[:].rearrange("p h d -> p (h d)"), ALU.max, ALU.add).then_inc(s["o1_ready"], 1)

            def add_attention(t):
                v.wait_ge(s["oproj"], t + 1)
                v.tensor_tensor(xr[:, t, :], xr[:, t, :], bank(7)[:, P:2 * P], ALU.add).then_inc(s["x_att"], 1)

            def route1_first(g):
                v.wait_ge(s["logits"], G + g + 1)
                v.wait_ge(s["combTp"], G)
                r = rt[:, g, :, :, 0:X1]
                lv = bank(logit_bank(1, g))[:, 0:TG * X0].rearrange("p (t x) -> p t x", x=X0)[:, :, 0:X1]
                route(v.tensor_copy(r[:, 2], lv))
                for t in range(TG):
                    last = v.max(top[:, g, t, :], r[:, 2, t, :])
                route(last)
                route(v.tensor_tensor(rsum[:, g, :].unsqueeze(2), top[:, g, :, 0:1], top[:, g, :, 1:2], ALU.add))
                v.scalar_tensor_tensor(r[:, 0], rsum[:, g, :].unsqueeze(2).to_broadcast([P, TG, X1]), -0.5, r[:, 2],
                                       ALU.mult, ALU.add).then_inc(s["rdiff"], 1)

            def route1_second(g):
                r = rt[:, g, :, :, 0:X1]
                route(v.memset(top[:, g, :, 2:], 3 * LOWEST))
                for t in range(TG):
                    last = v.match_replace(r[:, 3, t, :], top[:, g, t, :], r[:, 2, t, :], LOWEST)
                route(last)
                route(v.tensor_scalar(r[:, 4], r[:, 3], LOWEST / 2, XS / 2, ALU.is_lt, ALU.mult))
                v.wait_ge(s["lexp"], G + g + 1)
                route(v.scalar_tensor_tensor(r[:, 5], r[:, 1], 1.0, r[:, 4], ALU.add, ALU.mult))
                route(v.tensor_copy(combt[:, g, :, 0:X1], r[:, 5]))
                v.tensor_tensor(combt[:, g, :, 32:32 + X1], r[:, 5], combt[:, g, :, 0:X1], ALU.subtract)\
                    .then_inc(s["comb_ready"], 1)

            for i in range(NT + 4):
                if i < NT:
                    largest(i)
                if 3 <= i < NT + 3:
                    sums_of_weights(i - 3)
                if i < NT:
                    subtract_largest(i)
                if i == 0:
                    for jj in range(2):
                        query_low(1, jj)
                if i in (1, 2):
                    add_output_bias(i - 1)
                if 3 <= i < NT + 3:
                    invert_sums(i - 3)
                if i >= 4:
                    add_attention(i - 4)
                if 3 <= i < NT + 3:
                    divide(i - 3)
                if i >= 4:
                    v.wait_ge(s["x_att"], i - 3)
                    v.bn_stats(stats[:, i - 4, :], xr[:, i - 4, :]).then_inc(s["bn3"], 1)
                if 3 <= i < NT + 3:
                    negative_part(i - 3)
                if i < 4:
                    query_low(2 + i // 2, i % 2)
                if i == NT - 1:
                    v.wait_ge(s["bn3"], TG)
                    ln_variance(3, 0)
                    ln_apply(3, 0)
                if 3 <= i < NT + 3:
                    numbers_only(i - 3)
                if i == NT:
                    low_x(3, 1, 0, 0)
                if i == NT + 1:
                    route1_first(0)
                    route1_second(0)
            v.wait_ge(s["bn3"], NT)
            ln_variance(3, 1)
            ln_apply(3, 1)

            def low1_step(n, k):
                v.wait_ge(s["hhi1"], n + 1)
                v.wait_ge(s["mm2b"], reached(n - 3))
                v.scalar_tensor_tensor(hlo[:, k % 4, :], h32[:, k % 4, :], HS, hhi[:, k % 4, :], ALU.mult, ALU.subtract)\
                    .then_inc(s["hlo1"], 1)

            def gated(n, q, g, first=False, pair_before=False):
                v.wait_ge(s["mm2b"], n + 1)
                v.wait_ge(s["cbx1"], q + 1)
                v.wait_ge(s["yacc"], before(q, first) if not pair_before else q)
                v.tensor_tensor(ytmp[:, g, :], bank(4 + g), cb[:, g, :], ALU.mult).then_inc(s["ymul"], 1)

            def ffn1_expert_pair(base, q0, first=False):
                for k in range(16):
                    low1_step(base + k, k)
                    if k % FC == 0 and not (first and k == 0):
                        q = k // FC - 1
                        gated(base + (FC * q + 3), q0 + q, place(FC * q + 3, first)[1] if q >= 0 else 1, first, q < 0)
                    if first and k == 1:
                        low_x(3, 1, 1, 5)
                    if first and k == 3:
                        route1_first(1)
                        route1_second(1)

            ffn1_expert_pair(0, 0, first=True)
            with v.Fori(1, 3) as i:
                ffn1_expert_pair(i * 16, i * 4)
            ffn1_expert_pair(48, 12)
            gated(63, 15, 1)
            for g in range(G):
                v.wait_ge(s["yTp1"], g + 1)
                v.tensor_tensor(xr[:, gt(g), :], xr[:, gt(g), :], bank(g).rearrange("p (t e) -> p t e", e=E), ALU.add)\
                    .then_inc(s["x_out"], 1)

        @block.tensor
        def _(pe):
            mm = pe.matmul

            def keep_warm(b, count):
                for _ in range(count):
                    mm(bank(b), idle[:, 0:P], idle[:], start=True, stop=True)

            pe.wait_ge(s["idle_set"], 1)
            keep_warm(7, 26)

            pe.wait_ge(s["in_pack"], 16)
            pe.wait_ge(s["in_ctx"], 16)

            def transpose_norm(l, g, b):
                pe.wait_ge(s["xn_ready"], l * G + g + 1)
                for t in range(TG):
                    last = pe.transpose(bank(b)[:, t * P:(t + 1) * P], xn[:, g * TG + t, :], ident)
                last.then_inc(s["xnT_ready"], 1)

            def gates(g):
                pe.wait_ge(s["wgc_ready"], 1)
                rows = [slice(64 * g + 32 * hf, 64 * g + 32 * (hf + 1)) for hf in range(2)]
                ctx_g, x_g = (m[:, tok(g)].rearrange("p (t f k) -> p f t k", f=2, k=S) for m in (ctxT, xT))
                for i in range(2):
                    for hf in range(2):
                        mm(bank(4 * i + 1)[rows[hf], 0:NQ], wgc[:, 32 * i:32 * (i + 1)], ctx_g[:, hf], start=True, stop=False)
                pe.wait_ge(s["xT_ready"], g + 1)
                for i in range(2):
                    for hf in range(2):
                        last = mm(bank(4 * i + 1)[rows[hf], 0:NQ], wgv[:, 0, 32 * i:32 * (i + 1)], x_g[:, hf],
                                  start=False, stop=True)
                last.then_inc(s["gates"], 1)

            for g in range(G):
                transpose_norm(0, g, 4 * g)
                gates(g)
            pe.wait_ge(s["in_qkvo"], 16)
            for g in range(G):
                mm(bank(6 + g), wq[:, 1, :], ctxT[:, tok(g)], start=True, stop=True).then_inc(s["kproj"], 1)
            pe.wait_ge(s["kT_ready"], G)
            keep_warm(3, 4)
            pe.wait_ge(s["in_rows"], 16)
            pe.wait_ge(s["in_cz"], 16)
            pe.wait_ge(s["in_idh"], 32)
            def transpose_rows(i):
                pe.wait_ge((s["cmax_ready"], s["en_ready"])[i], 1)
                pe.wait_ge(s["xT_ready"], i + 1)
                for t in range(TG):
                    if i == 0:
                        for hf in range(2):
                            last = mm(bank(0)[hf * S:(hf + 1) * S, t * P:(t + 1) * P], cmax[:, t * S:(t + 1) * S], ident,
                                      start=True, stop=True)
                    else:
                        last = pe.transpose(bank(4)[:, t * P:(t + 1) * P], enrow[:, t * P:(t + 1) * P], ident)
                last.then_inc(s["stT"], 1)

            for g in range(G):
                pe.wait_ge(s["c_ready"], 1)
                q = slice(64 * g, 64 * (g + 1))
                for pair in range(2):
                    for h in range(2 * pair, 2 * pair + 2):
                        mm(bank(4 * g + 2 + pair)[:, (h % 2) * NQ:(h % 2 + 1) * NQ], head_sel[q, h, :], crow[q, :],
                           start=(h % 2 == 0), stop=False, skip_group_check=True)
                    last = mm(bank(4 * g + 2 + pair), idb[:], cz[:].unsqueeze(1).to_broadcast([P, 8, S]),
                              start=False, stop=True, skip_group_check=True)
                last.then_inc(s["cbc"], 1)
                transpose_rows(g)
            pe.wait_ge(s["ctxm_ready"], H0)
            for g in range(G):
                pe.wait_ge(s["sttok_ready"], 2)
                for t in range(TG):
                    for hf in range(2):
                        b = 2 * (g * TG + t) + hf
                        last = mm(ps[hf * S:(hf + 1) * S, 4 * g + t // 2, (t % 2) * H0 * S:(t % 2 + 1) * H0 * S],
                                  xT[:, b * S:(b + 1) * S], ctxM[:, b, :, :].rearrange("p h k -> p (h k)"),
                                  start=True, stop=True)
                last.then_inc(s["s0"], 1)
            for g in range(G):
                pe.wait_ge(s["cmat_ready"], g + 1)
                for c in range(2 * TG):
                    last = pe.transpose(bank(4 * g + 2 + c // 4)[:, (c % 4) * P:(c % 4 + 1) * P],
                                        cmat[:, g, c * P:(c + 1) * P], ident)
                last.then_inc(s["cTp"], 1)
            pe.wait_ge(s["v0_ready"], 1)
            for g in range(G):
                pe.wait_ge(s["cT_ready"], g + 1)
                for t in range(TG):
                    for pair in range(2):
                        for hf in range(2):
                            b = 2 * (g * TG + t) + hf
                            c = (2 * t + pair) * P + hf * S
                            o = (t % 2) * 132 + pair * 66
                            last = mm(ps[hf * S:(hf + 1) * S, 4 * g + t // 2, o:o + 66], cT[:, g, c:c + S],
                                      v0[:, b, pair, :], start=True, stop=True)
                last.then_inc(s["o0"], 1)

            def v_products(c):
                for b in range(4 * c, 4 * c + 4):
                    for hf in range(2):
                        o = ps[hf * S:(hf + 1) * S, (2, 3, 6, 7)[c], (b % 4) * E:(b % 4 + 1) * E]
                        mm(o, ctxT[:, b * S:(b + 1) * S], wq[:, 2, :], start=True, stop=False)
                        last = mm(o, ones_row[:], pc("bv")[0:1, :], start=False, stop=True)
                last.then_inc(s["vproj"], 1)

            pe.wait_ge(s["ones_ready"], 1)
            for c in range(4):
                v_products(c)
            pe.wait_ge(s["v1_copied"], 4)
            keep_warm(3, 4)

            def router(l, k, g, width, name):
                pe.wait_ge(s["xT_ready"], l * G + g + 1)
                for t in range(TG):
                    c = g * N + t * P
                    last = mm(bank(logit_bank(k, g))[:, t * X0:t * X0 + width], xT[:, c:c + P], pc(name), start=True, stop=True)
                last.then_inc(s["logits"], 1)

            def transpose_gates(k, g):
                pe.wait_ge(s["comb_ready"], k * G + g + 1)
                for t in range(TG):
                    last = pe.transpose(bank(gate_bank(k, g))[:, t * S:(t + 1) * S].bitcast(F16), combt[:, g, t, :], idh[:])
                last.then_inc(s["combTp"], 1)

            transpose_norm(1, 0, 0)
            keep_warm(3, 6)
            transpose_norm(1, 1, 4)
            for g in range(G):
                router(1, 0, g, X0, "gate_w")

            def up0(n, j, k, p):
                inner0(n, j, k, p)
                broadcast0(j, k)

            def inner0(n, j, k, p):
                g = k
                pe.wait_ge(s["wsp_ready"], j * 2 + 1)
                pe.wait_ge(s["silu"], reached(n - 1))
                pe.wait_ge(s["tmul"], reached(n - 1))
                pe.wait_ge(s["cbx"], reached(n - 1))
                for i in range(2):
                    c = slice(i * P, (i + 1) * P)
                    mm(bank(2 * i + k), wsp[:, p, 0, c], xhi[:, tok(g)], start=True, stop=False)
                    mm(bank(2 * i + k), wsp[:, p, 0, c], xlo[:, tok(g)], start=False, stop=False)
                    mm(bank(2 * i + k), wsp[:, p, 1, c], xhi[:, tok(g)], start=False, stop=True)

            def broadcast0(j, k):
                pick = sel0[:, j, :] if type(j) is int else sel0[:, bass.ds(j, 1), :].rearrange("p a m -> p (a m)")
                mm(bank(4 + k), pick, combT[:, k, :], start=True, stop=True).then_inc(s["mm1"], 1)

            def down0(n, j, k, p, first, last):
                c = slice(2 * P, 3 * P)
                pe.wait_ge(s["wsp_ready"], j * 2 + 2)
                pe.wait_ge(s["hlo_r"], n + 1)
                mm(bank(6 + k), wsp[:, p, 0, c], hhi[:, k, :], start=first, stop=False)
                mm(bank(6 + k), wsp[:, p, 0, c], hlo[:, k, :], start=False, stop=False)
                mm(bank(6 + k), wsp[:, p, 1, c], hhi[:, k, :], start=False, stop=last).then_inc(s["mm2"], 1)

            pe.wait_ge(s["in_sel"], 32)
            pe.wait_ge(s["lexp"], G)
            for g in range(G):
                pe.wait_ge(s["xlo_ready"], g + 1)
                pe.wait_ge(s["xhi_ready"], g + 1)
                inner0(g, 0, g, 0)
            for g in range(G):
                transpose_gates(0, g)
            for g in range(G):
                pe.wait_ge(s["combT_ready"], g + 1)
                broadcast0(0, g)

            def two_pairs(j, first=False):
                for k in range(4):
                    up0(2 * j + (k + 2), j + (k // 2 + 1), k % 2, (k // 2 + 1) % 2)
                    down0(2 * j + k, j + k // 2, k % 2, k // 2, first and k < 2, False)

            two_pairs(0, first=True)
            with pe.Fori(1, PAIRS // 2) as i:
                two_pairs(i * 2)
            n0 = 2 * (PAIRS - 1)
            for g in range(G):
                down0(n0 + g, PAIRS - 1, g, 0, False, True)

            def transpose_y(g, b, done):
                for t in range(TG):
                    last = pe.transpose(bank(b)[:, t * P:(t + 1) * P], yT[:, g, t * P:(t + 1) * P], ident)
                last.then_inc(done, 1)

            for g in range(G):
                pe.wait_ge(s["yT_ready"], g + 1)
                transpose_y(g, g, s["yTp"])
            keep_warm(3, 16)

            pe.wait_ge(s["yT_ready"], G)
            transpose_norm(2, 0, 7)
            pe.wait_ge(s["wqr_ready"], 1)

            def query_products(c, jj):
                pe.wait_ge(s["xT_ready"], 2 * G + c // 2 + 1)
                if c >= 2:
                    if (c, jj) != (2, 0):
                        pe.wait_ge(s["qS_ready"], 4 * c + 2 * jj)
                for j in range(2 * jj, 2 * jj + 2):
                    last = mm(bank(qbank(c, jj))[:, (j % 2) * Q4:(j % 2 + 1) * Q4], wqr[:, j, :], xT[:, c * Q4:(c + 1) * Q4],
                              start=True, stop=True)
                last.then_inc(s["qproj"], 1)

            for jj in range(2):
                query_products(0, jj)
            transpose_norm(2, 1, 6)
            pe.wait_ge(s["kM_ready"], H1)

            def scores1(t):
                pe.wait_ge(s["qS_ready"], 8 if t == 1 else 4 * (t // 2 + 1))
                pe.wait_ge(s["ssub"], reached(t - 1))
                for j in range(4):
                    for hf in range(2):
                        b = 2 * t + hf
                        last = mm(ps[hf * S:(hf + 1) * S, 2 * (t % 2) + j // 2, (j % 2) * 4 * S:(j % 2 + 1) * 4 * S],
                                  qS[:, j, b * S:(b + 1) * S], kM[:, 4 * j:4 * j + 4, b * S:(b + 1) * S], start=True, stop=True)
                last.then_inc(s["s1"], 1)

            def transpose_weights(t):
                pe.wait_ge(s["qS_ready"], 8)
                for part in range(2):
                    pe.wait_ge((s["phi_ready"], s["plo_ready"])[part], t + 1)
                    pe.wait_ge(s["pT_ready"], reached(2 * t - 1 + part))
                    for c in range(8):
                        last = pe.transpose(bank(4 + part)[:, c * S:(c + 1) * S].bitcast(F16),
                                            (phi, plo)[part][:, t % 2, c * P:(c + 1) * P], idh[:])
                    last.then_inc(s["pTp"], 1)

            def weighted_values(t):
                pe.wait_ge(s["v1lo_ready"], 1)
                pe.wait_ge(s["pT_ready"], 2 * t + 2)
                pe.wait_ge(s["o1_ready"], reached(t))
                for c in range(8):
                    o = bank(6)[:, c * 36:(c + 1) * 36]
                    hi, lo = (pT[:, t % 2, part, c * P:(c + 1) * P] for part in range(2))
                    mm(o, hi, v1hi[:, 2 * t:2 * t + 2, c, :], start=True, stop=False)
                    mm(o, hi, v1lo[:, 2 * t:2 * t + 2, c, :], start=False, stop=False)
                    last = mm(o, lo, v1hi[:, 2 * t:2 * t + 2, c, :], start=False, stop=True)
                last.then_inc(s["av"], 1)

            def transpose_values(t):
                pe.wait_ge(s["o1_ready"], t + 1)
                pe.wait_ge(s["x_att"], reached(t))
                pe.wait_ge(s["qS_ready"], 16)
                pe.transpose(bank(7)[:, 0:P], o1c[:, t % 2, :], ident).then_inc(s["oTp"], 1)

            def output_product(t):
                pe.wait_ge(s["oT_ready"], t + 1)
                mm(bank(7)[:, P:2 * P], oT[:], wq[:, 3, :], start=True, stop=True).then_inc(s["oproj"], 1)

            def up1(n, e, q, k, first=False):
                p, g, c = place(k, first)
                pe.wait_ge(s["wsp1_ready"], 2 * (e + p) + 1)
                pe.wait_ge(s["gelu"], reached(n - 3))
                cs = slice(c * P, (c + 1) * P)
                if c == 0:
                    pe.wait_ge(s["cbx1"], before(q, first))
                    pick = sel1[:, e + p, :] if type(e) is int else sel1[:, bass.ds(e + p, 1), :].rearrange("p a m -> p (a m)")
                    mm(bank(6 + g), pick, combT[:, g, :], start=True, stop=True)
                mm(bank(k % 4), wsp[:, p, 0, cs], xhi[:, tok(g)], start=True, stop=False)
                mm(bank(k % 4), wsp[:, p, 0, cs], xlo[:, tok(g)], start=False, stop=False)
                mm(bank(k % 4), wsp[:, p, 1, cs], xhi[:, tok(g)], start=False, stop=True).then_inc(s["mm1b"], 1)

            def down1(n, e, q, k, first=False):
                p, g, c = place(k, first)
                cs = slice(N + c * P, N + (c + 1) * P)
                pe.wait_ge(s["wsp1_ready"], 2 * (e + p) + 2)
                pe.wait_ge(s["hlo1"], n + 1)
                if c == 0:
                    pe.wait_ge(s["ymul"], before(q, first))
                mm(bank(4 + g), wsp[:, p, 0, cs], hhi[:, k % 4, :], start=(c == 0), stop=False)
                mm(bank(4 + g), wsp[:, p, 0, cs], hlo[:, k % 4, :], start=False, stop=False)
                mm(bank(4 + g), wsp[:, p, 1, cs], hhi[:, k % 4, :], start=False, stop=(c == FC - 1)).then_inc(s["mm2b"], 1)

            for i in range(NT + 4):
                if i < NT:
                    scores1(i)
                if i == 0:
                    for jj in range(2):
                        query_products(1, jj)
                if i < 4:
                    query_products(2 + i // 2, i % 2)
                if 3 <= i < NT + 3:
                    weighted_values(i - 3)
                if i >= 4:
                    transpose_values(i - 4)
                if 2 <= i < NT + 2:
                    transpose_weights(i - 2)
                if i == NT + 3:
                    pe.wait_ge(s["combT_ready"], G + 1)
                    pe.wait_ge(s["xlo_ready"], G + 1)
                    pe.wait_ge(s["xhi_ready"], G + 1)
                    up1(0, 0, 0, 0, first=True)
                if i >= 4:
                    output_product(i - 4)
                if i == NT:
                    pe.wait_ge(s["ssub"], NT)
                    transpose_norm(3, 0, 0)
                    router(3, 1, 0, X1, "router_w")
                if i == NT + 1:
                    keep_warm(3, 16)
                    transpose_gates(1, 0)
                if i == NT + 2:
                    keep_warm(3, 8)

            def expert_pair(e, first=False, last=False):
                for k in range(16):
                    if first and k == 0:
                        pe.wait_ge(s["x_att"], NT)
                        transpose_norm(3, 1, 5)
                    if first and k == 1:
                        router(3, 1, 1, X1, "router_w")
                    if first and k == 5:
                        transpose_gates(1, 1)
                        pe.wait_ge(s["combT_ready"], 2 * G)
                        pe.wait_ge(s["xlo_ready"], 2 * G)
                    ahead = k + 3
                    if not (last and ahead >= 16):
                        up1(8 * e + ahead, e + 2 * (ahead // 16), 2 * e + ahead // 4, ahead, first)
                    down1(8 * e + k, e, 2 * e + k // 4, k, first)

            up1(1, 0, 0, 1, first=True)
            up1(2, 0, 0, 2, first=True)
            expert_pair(0, first=True)
            with pe.Fori(1, X1 // 2 - 1) as i:
                expert_pair(i * 2)
            expert_pair(X1 - 2, last=True)
            pe.wait_ge(s["yacc"], 2 * X1)
            for g in range(G):
                transpose_y(g, g, s["yTp1"])


def kernel(**inputs):
    import numpy as np
    import ml_dtypes
    import concourse.bacc as bacc
    from concourse.bass_utils import run_bass_kernel_spmd

    f = {k: np.asarray(v) for k, v in inputs.items()}
    f32 = np.float32
    x = f["x"].reshape(NB * S, E)
    ctx = f["ctx_1024"]
    pack = np.zeros((P, PACK_W), f32)

    def put(name, value):
        a, b = PACK[name]
        pack[:value.shape[0], a:b] = value.reshape(value.shape[0], b - a)

    wg = np.zeros((P, 3, 64), f32)
    gb = np.zeros((P, 2), f32)
    for c in range(3):
        wg[:, c, 0:H0] = f["L0_xattn_igate_w"][:, c * E:(c + 1) * E].T
        wg[:, c, 32:32 + H0] = f["L0_xattn_fgate_w"][:, c * E:(c + 1) * E].T
    for q in range(0, P, 32):
        gb[q:q + H0, 0] = f["L0_xattn_igate_b"]
        gb[q:q + H0, 1] = f["L0_xattn_fgate_b"]
    put("ident", np.eye(P, dtype=f32))
    put("wg", wg)
    put("gb", gb)
    put("headmask", (np.arange(P)[:, None] % 32 // D1 == np.arange(4)[None, :]).astype(f32))
    put("bq", np.tile(f["L1_xattn_b_q"].reshape(4, E // 4).T, (4, 1)))
    put("bk", f["L1_xattn_b_k"][:, None])
    put("out_w", np.broadcast_to(f["L0_xattn_out_w"], (P, E)))
    put("bv", np.broadcast_to(f["L1_xattn_b_v"], (P, E)))
    put("bo", np.broadcast_to(f["L1_xattn_b_o"], (P, E)))
    put("gate_b", np.broadcast_to(f["L0_ffn_gate_b"], (P, X0)))
    put("gate_w", f["L0_ffn_gate_w"].T)
    put("router_w", f["L1_ffn_router_w"].T)

    rows = np.zeros((P, 2 * NQ + H0 * P), f32)
    starts = (np.arange(NQ) % S) == 0
    rows[:, 0:NQ] = ~starts
    rows[:, NQ:2 * NQ] = np.where(starts, LOWEST, 0.0)
    for g in range(G):
        for hf in range(2):
            for h in range(H0):
                c = 2 * NQ + h * P + hf * S
                rows[64 * g + 32 * hf + h, c:c + S] = 1.0

    ctx_v = np.zeros((P, NB, 2, 66), f32)
    for hf in range(2):
        for pair in range(2):
            h = 2 * pair + hf
            ctx_v[hf * S:(hf + 1) * S, :, pair, hf * 33:hf * 33 + D0] = ctx[:, :, h * D0:(h + 1) * D0].transpose(1, 0, 2)
            ctx_v[hf * S:(hf + 1) * S, :, pair, hf * 33 + D0] = 1.0

    w_first = np.zeros((PAIRS, P, 3 * P), f32)
    w13, w2 = f["L0_ffn_w13"], f["L0_ffn_w2"]
    half = w13.shape[1] // 2
    experts = [(w13[e], w2[e]) for e in range(X0)] + [(f["L0_ffn_w13_s"], f["L0_ffn_w2_s"])]
    for e, (up, down) in enumerate(experts):
        j, c = e // 2, (e % 2) * half
        w_first[j, :, c:c + half] = up[0:half].T
        w_first[j, :, P + c:P + c + half] = up[half:].T
        w_first[j, c:c + half, 2 * P:] = down.T
    w_second = np.concatenate([f["L1_ffn_w1"].transpose(0, 2, 1),
                               f["L1_ffn_w2"].transpose(0, 2, 1).reshape(X1, FC, P, E).transpose(0, 2, 1, 3).reshape(X1, P, FC * E)], axis=2)
    qkvo = np.stack([f["L1_xattn_W_q"].T, f["L1_xattn_W_k"].T, f["L1_xattn_W_v"].T, f["L1_xattn_W_o"].T], axis=1)
    causal = np.where(np.arange(S)[None, :] > (np.arange(P) % S)[:, None], LOWEST, 0.0).astype(ml_dtypes.bfloat16)
    sel_first = np.zeros((P, PAIRS, P), np.float16)
    for e in range(X0 + 1):
        for r in (e, 32 + e):
            sel_first[r, e // 2, (e % 2) * half:(e % 2 + 1) * half] = 1.0
    sel_second = np.zeros((P, X1, P), np.float16)
    for e in range(X1):
        sel_second[[e, 32 + e], e, :] = 1.0

    arrays = {
        "x": x, "ctx_t": ctx.reshape(NB * S, E).T, "ctx_v": ctx_v, "pack": pack, "rows": rows, "w_first": w_first,
        "w_second": w_second, "qkvo": qkvo, "causal": causal, "ident_h": np.eye(P, dtype=np.float16),
        "ident_b": np.eye(P, dtype=ml_dtypes.bfloat16),
        "sel_first": sel_first, "sel_second": sel_second,
    }
    arrays = {k: np.ascontiguousarray(v) for k, v in arrays.items()}
    nc = bacc.Bacc("TRN2", target_bir_lowering=False, num_devices=1)
    args = {k: nc.dram_tensor(k, v.shape, mybir.dt.from_np(v.dtype), kind="ExternalInput").ap() for k, v in arrays.items()}
    out = nc.dram_tensor("out", (NB * S, E), F32, kind="ExternalOutput").ap()
    build_program(nc, out=out, **args)
    r = run_bass_kernel_spmd(nc, [arrays], core_ids=[0])
    return r.results[0]["out"].reshape(NB, S, E)
```
